# Optimizing a Trainium2 kernel written in Bass

```python
import numpy as np
import jax
import jax.numpy as jnp

def _softmax(x, axis=-1):
    return jax.nn.softmax(x, axis=axis)

def _gelu(x):
    return jax.nn.gelu(x, approximate=True)

def _silu(x):
    return jax.nn.silu(x)

def _sigmoid(x):
    return jax.nn.sigmoid(x)

def _layernorm(x, axis=-1, eps=1e-05):
    m = jnp.mean(x, axis=axis, keepdims=True)
    v = jnp.var(x, axis=axis, keepdims=True)
    return (x - m) / jnp.sqrt(v + eps)

def _scatter_add(tgt, idx, src, axis=0):
    return tgt.at[idx].add(src)

def _segment_sum(src, seg, n):
    return jax.ops.segment_sum(src, seg, n)
kernel_name = 'mk_gps_d2_gnn_r32_ae08c1'

def setup_inputs(seed: int=0):
    np.random.seed(seed)
    _w = jnp.asarray

    def _rec_inputs():
        import jax
        import jax.numpy as jnp
        _gk = jax.random.key(seed)
        x = -0.0006008 + 1.001 * jax.random.normal(jax.random.fold_in(_gk, 1), (3125, 256), jnp.float32)
        src = jax.random.randint(jax.random.fold_in(_gk, 2), (50000,), 0, 3125, jnp.int32)
        dst = jnp.minimum((3125 * jax.random.uniform(jax.random.fold_in(_gk, 3), (50000,)) ** 2.0).astype(jnp.int32), 99999)
        _o = jnp.argsort(dst, stable=True)
        src = src[_o]
        dst = dst[_o]
        return (x, src, dst)
    x, src, dst = _rec_inputs()

    def _L0_gnn_setup():
        import jax, jax.numpy as jnp
        import numpy as np
        N_NODES = 10000
        N_EDGES = 10000
        D = 256
        key = jax.random.key(seed)
        k1, k2, k3, k4, k5 = jax.random.split(key, 5)
        x = jax.random.normal(k1, (N_NODES, D), dtype=jnp.float32)
        src = jax.random.randint(k2, (N_EDGES,), 0, N_NODES, dtype=jnp.int32)
        dst = jax.random.randint(k3, (N_EDGES,), 0, N_NODES, dtype=jnp.int32)
        s = 1.0 / np.sqrt(D)
        theta_w = jax.random.uniform(k4, (D, D), jnp.float32, -s, s)
        theta_b = jnp.zeros((D,), jnp.float32)
        phi_w = jax.random.uniform(k5, (D, D), jnp.float32, -s, s)
        phi_b = jnp.zeros((D,), jnp.float32)
        return {'x': x, 'src': src, 'dst': dst, 'theta_w': theta_w, 'theta_b': theta_b, 'phi_w': phi_w, 'phi_b': phi_b}
    _L0_gnn_all = _L0_gnn_setup()
    _L0_gnn_in = {k: v for k, v in _L0_gnn_all.items() if k in ('theta_w', 'theta_b', 'phi_w', 'phi_b')}
    del _L0_gnn_all

    def _L0_mix_setup():
        import jax, jax.numpy as jnp
        import numpy as np
        DIM = 256
        HEADS = 4
        HEAD_DIM = DIM // HEADS
        MLP_HIDDEN = DIM * 3
        B, N = (8, 128)
        EPS = 1e-05

        def _layernorm(x, g, b):
            mu = jnp.mean(x, axis=-1, keepdims=True)
            var = jnp.mean(jnp.square(x - mu), axis=-1, keepdims=True)
            return (x - mu) * jax.lax.rsqrt(var + EPS) * g + b
        key = jax.random.key(seed)
        ks = jax.random.split(key, 8)
        s = 0.02
        return {'x': jax.random.normal(ks[0], (B, N, DIM), dtype=jnp.float32), 'w_qkv': jax.random.normal(ks[1], (DIM, 3 * DIM), dtype=jnp.float32) * s, 'b_qkv': jnp.zeros((3 * DIM,), dtype=jnp.float32), 'norm_g': jnp.ones((DIM,), dtype=jnp.float32), 'norm_b': jnp.zeros((DIM,), dtype=jnp.float32), 'w_fc1': jax.random.normal(ks[2], (DIM, MLP_HIDDEN), dtype=jnp.float32) * s, 'b_fc1': jnp.zeros((MLP_HIDDEN,), dtype=jnp.float32), 'w_fc2': jax.random.normal(ks[3], (MLP_HIDDEN, DIM), dtype=jnp.float32) * s, 'b_fc2': jnp.zeros((DIM,), dtype=jnp.float32)}
    _L0_mix_all = _L0_mix_setup()
    _L0_mix_in = {k: v for k, v in _L0_mix_all.items() if k in ('w_qkv', 'b_qkv', 'norm_g', 'norm_b', 'w_fc1', 'b_fc1', 'w_fc2', 'b_fc2')}
    del _L0_mix_all

    def _L0_ffn_setup():
        import jax, jax.numpy as jnp
        import numpy as np
        BN_EPS = 0.001

        def _bn(h, g, b, m, v):
            return g * (h - m) * jax.lax.rsqrt(v + BN_EPS) + b
        key = jax.random.key(seed)
        ks = jax.random.split(key, 8)
        B, F, Df = (256, 64, 256)
        E, H, D = (8, 256, 256)
        s1 = 1.0 / np.sqrt(Df)
        s2 = 1.0 / np.sqrt(H)
        return {'x': jax.random.normal(ks[0], (B, F, Df), jnp.float32), 'Wr': jax.random.normal(ks[1], (Df, E), jnp.float32) * s1, 'br': jnp.zeros((E,), jnp.float32), 'W1': jax.random.normal(ks[2], (E, Df, H), jnp.float32) * s1, 'b1': jnp.zeros((E, H), jnp.float32), 'g1': jnp.ones((E, H), jnp.float32), 'be1': jnp.zeros((E, H), jnp.float32), 'm1': jnp.zeros((E, H), jnp.float32), 'v1': jnp.ones((E, H), jnp.float32), 'W2': jax.random.normal(ks[3], (E, H, H), jnp.float32) * s2, 'b2': jnp.zeros((E, H), jnp.float32), 'g2': jnp.ones((E, H), jnp.float32), 'be2': jnp.zeros((E, H), jnp.float32), 'm2': jnp.zeros((E, H), jnp.float32), 'v2': jnp.ones((E, H), jnp.float32), 'Wo': jax.random.normal(ks[4], (E, H, D), jnp.float32) * s2, 'bo': jnp.zeros((E, D), jnp.float32)}
    _L0_ffn_all = _L0_ffn_setup()
    _L0_ffn_in = {k: v for k, v in _L0_ffn_all.items() if k in ('Wr', 'br', 'W1', 'b1', 'g1', 'be1', 'm1', 'v1', 'W2', 'b2', 'g2', 'be2', 'm2', 'v2', 'Wo', 'bo')}
    del _L0_ffn_all

    def _L1_gnn_setup():
        import jax, jax.numpy as jnp
        import numpy as np
        N_NODES = 50000
        N_EDGES = 25000
        D_IN = 256
        D_HID = 256
        D_OUT = 256

        def _sage_conv(x, src, dst, Wl, bl, Wr, num_nodes):
            msg = x[src]
            agg = jax.ops.segment_sum(msg, dst, num_segments=num_nodes)
            deg = jax.ops.segment_sum(jnp.ones((src.shape[0],), x.dtype), dst, num_segments=num_nodes)
            mean = agg / jnp.maximum(deg, 1.0)[:, None]
            return jnp.einsum('nd,od->no', mean, Wl) + bl + jnp.einsum('nd,od->no', x, Wr)
        key = jax.random.key(seed)
        ks = jax.random.split(key, 12)
        x = jax.random.normal(ks[0], (N_NODES, D_IN), dtype=jnp.float32)
        edge_index = jax.random.randint(ks[1], (2, N_EDGES), 0, N_NODES, dtype=jnp.int32)

        def lin(k, dout, din):
            return jax.random.normal(k, (dout, din), dtype=jnp.float32) * (1.0 / np.sqrt(din))
        return {'x': x, 'edge_index': edge_index, 'W1l': lin(ks[2], D_HID, D_IN), 'b1l': jnp.zeros((D_HID,), jnp.float32), 'W1r': lin(ks[3], D_HID, D_IN), 'W2l': lin(ks[4], D_HID, D_HID), 'b2l': jnp.zeros((D_HID,), jnp.float32), 'W2r': lin(ks[5], D_HID, D_HID), 'W3l': lin(ks[6], D_OUT, D_HID), 'b3l': jnp.zeros((D_OUT,), jnp.float32), 'W3r': lin(ks[7], D_OUT, D_HID)}
    _L1_gnn_all = _L1_gnn_setup()
    _L1_gnn_in = {k: v for k, v in _L1_gnn_all.items() if k in ('W1l', 'b1l', 'W1r', 'W2l', 'b2l', 'W2r', 'W3l', 'b3l', 'W3r')}
    del _L1_gnn_all

    def _L1_mix_setup():
        import jax, jax.numpy as jnp
        import numpy as np
        DIM = 256
        HEADS = 4
        DIM_HEAD = 32
        NUM_MEM = 4
        HIDDEN = HEADS * DIM_HEAD
        SCALE = DIM_HEAD ** (-0.5)

        def rmsnorm(x, g):
            n = jnp.linalg.norm(x, axis=-1, keepdims=True)
            return x / jnp.maximum(n, 1e-12) * g * x.shape[-1] ** 0.5
        key = jax.random.key(seed)
        ks = jax.random.split(key, 8)
        B, N = (4, 512)
        return {'x': jax.random.normal(ks[0], (B, N, DIM), jnp.float32), 't': jax.random.normal(ks[1], (B,), jnp.float32), 'w_qkv': jax.random.normal(ks[2], (DIM, 3 * HIDDEN), jnp.float32) * 0.02, 'mem_kv': jax.random.normal(ks[3], (2, HEADS, DIM_HEAD, NUM_MEM), jnp.float32), 'w_out': jax.random.normal(ks[4], (HIDDEN, DIM), jnp.float32) * 0.02, 'b_out': jnp.zeros((DIM,), jnp.float32), 'g_out': jnp.ones((DIM,), jnp.float32), 'g_pre': jnp.ones((DIM,), jnp.float32)}
    _L1_mix_all = _L1_mix_setup()
    _L1_mix_in = {k: v for k, v in _L1_mix_all.items() if k in ('t', 'w_qkv', 'mem_kv', 'w_out', 'b_out', 'g_out', 'g_pre')}
    del _L1_mix_all

    def _L1_ffn_setup():
        import jax, jax.numpy as jnp
        import numpy as np
        B, S, D = (8, 128, 256)
        H = 4 * D
        CAPACITY = 0.5
        key = jax.random.key(seed)
        ks = jax.random.split(key, 6)
        x = jax.random.normal(ks[0], (B, S, D), dtype=jnp.float32)
        attention_mask = jnp.zeros((B, 1, 1, S), dtype=jnp.float32)
        wr = jax.random.normal(ks[1], (D, 1), dtype=jnp.float32) * 0.02
        br = jnp.zeros((1,), dtype=jnp.float32)
        w1 = jax.random.normal(ks[2], (D, H), dtype=jnp.float32) * 0.02
        b1 = jnp.zeros((H,), dtype=jnp.float32)
        w2 = jax.random.normal(ks[3], (H, D), dtype=jnp.float32) * 0.02
        b2 = jnp.zeros((D,), dtype=jnp.float32)
        return {'x': x, 'attention_mask': attention_mask, 'wr': wr, 'br': br, 'w1': w1, 'b1': b1, 'w2': w2, 'b2': b2}
    _L1_ffn_all = _L1_ffn_setup()
    _L1_ffn_in = {k: v for k, v in _L1_ffn_all.items() if k in ('attention_mask', 'wr', 'br', 'w1', 'b1', 'w2', 'b2')}
    del _L1_ffn_all
    return {'x': x, 'src': src, 'dst': dst, 'L0_gnn_theta_w': _L0_gnn_in['theta_w'], 'L0_gnn_theta_b': _L0_gnn_in['theta_b'], 'L0_gnn_phi_w': _L0_gnn_in['phi_w'], 'L0_gnn_phi_b': _L0_gnn_in['phi_b'], 'L0_mix_w_qkv': _L0_mix_in['w_qkv'], 'L0_mix_b_qkv': _L0_mix_in['b_qkv'], 'L0_mix_norm_g': _L0_mix_in['norm_g'], 'L0_mix_norm_b': _L0_mix_in['norm_b'], 'L0_mix_w_fc1': _L0_mix_in['w_fc1'], 'L0_mix_b_fc1': _L0_mix_in['b_fc1'], 'L0_mix_w_fc2': _L0_mix_in['w_fc2'], 'L0_mix_b_fc2': _L0_mix_in['b_fc2'], 'L0_ffn_Wr': _L0_ffn_in['Wr'], 'L0_ffn_br': _L0_ffn_in['br'], 'L0_ffn_W1': _L0_ffn_in['W1'], 'L0_ffn_b1': _L0_ffn_in['b1'], 'L0_ffn_g1': _L0_ffn_in['g1'], 'L0_ffn_be1': _L0_ffn_in['be1'], 'L0_ffn_m1': _L0_ffn_in['m1'], 'L0_ffn_v1': _L0_ffn_in['v1'], 'L0_ffn_W2': _L0_ffn_in['W2'], 'L0_ffn_b2': _L0_ffn_in['b2'], 'L0_ffn_g2': _L0_ffn_in['g2'], 'L0_ffn_be2': _L0_ffn_in['be2'], 'L0_ffn_m2': _L0_ffn_in['m2'], 'L0_ffn_v2': _L0_ffn_in['v2'], 'L0_ffn_Wo': _L0_ffn_in['Wo'], 'L0_ffn_bo': _L0_ffn_in['bo'], 'L1_gnn_W1l': _L1_gnn_in['W1l'], 'L1_gnn_b1l': _L1_gnn_in['b1l'], 'L1_gnn_W1r': _L1_gnn_in['W1r'], 'L1_gnn_W2l': _L1_gnn_in['W2l'], 'L1_gnn_b2l': _L1_gnn_in['b2l'], 'L1_gnn_W2r': _L1_gnn_in['W2r'], 'L1_gnn_W3l': _L1_gnn_in['W3l'], 'L1_gnn_b3l': _L1_gnn_in['b3l'], 'L1_gnn_W3r': _L1_gnn_in['W3r'], 'L1_mix_t': _L1_mix_in['t'], 'L1_mix_w_qkv': _L1_mix_in['w_qkv'], 'L1_mix_mem_kv': _L1_mix_in['mem_kv'], 'L1_mix_w_out': _L1_mix_in['w_out'], 'L1_mix_b_out': _L1_mix_in['b_out'], 'L1_mix_g_out': _L1_mix_in['g_out'], 'L1_mix_g_pre': _L1_mix_in['g_pre'], 'L1_ffn_attention_mask': _L1_ffn_in['attention_mask'], 'L1_ffn_wr': _L1_ffn_in['wr'], 'L1_ffn_br': _L1_ffn_in['br'], 'L1_ffn_w1': _L1_ffn_in['w1'], 'L1_ffn_b1': _L1_ffn_in['b1'], 'L1_ffn_w2': _L1_ffn_in['w2'], 'L1_ffn_b2': _L1_ffn_in['b2']}

def reference(x, src, dst, L0_gnn_theta_w, L0_gnn_theta_b, L0_gnn_phi_w, L0_gnn_phi_b, L0_mix_w_qkv, L0_mix_b_qkv, L0_mix_norm_g, L0_mix_norm_b, L0_mix_w_fc1, L0_mix_b_fc1, L0_mix_w_fc2, L0_mix_b_fc2, L0_ffn_Wr, L0_ffn_br, L0_ffn_W1, L0_ffn_b1, L0_ffn_g1, L0_ffn_be1, L0_ffn_m1, L0_ffn_v1, L0_ffn_W2, L0_ffn_b2, L0_ffn_g2, L0_ffn_be2, L0_ffn_m2, L0_ffn_v2, L0_ffn_Wo, L0_ffn_bo, L1_gnn_W1l, L1_gnn_b1l, L1_gnn_W1r, L1_gnn_W2l, L1_gnn_b2l, L1_gnn_W2r, L1_gnn_W3l, L1_gnn_b3l, L1_gnn_W3r, L1_mix_t, L1_mix_w_qkv, L1_mix_mem_kv, L1_mix_w_out, L1_mix_b_out, L1_mix_g_out, L1_mix_g_pre, L1_ffn_attention_mask, L1_ffn_wr, L1_ffn_br, L1_ffn_w1, L1_ffn_b1, L1_ffn_w2, L1_ffn_b2):
    import jax
    import jax.numpy as jnp

    def _L0_gnn_ref(x, src, dst, theta_w, theta_b, phi_w, phi_b):
        import jax, jax.numpy as jnp
        import numpy as np
        N_NODES = 10000
        N_EDGES = 10000
        D = 256
        x_src = x[src]
        x_dst = x[dst]
        theta_x = (x_dst - x_src) @ theta_w.T + theta_b
        phi_x = x_src @ phi_w.T + phi_b
        e = jax.nn.relu(theta_x + phi_x)
        out = jax.ops.segment_max(e, dst, num_segments=x.shape[0])
        return jnp.where(jnp.isfinite(out), out, 0.0)

    def _L0_mix_ref(x, w_qkv, b_qkv, norm_g, norm_b, w_fc1, b_fc1, w_fc2, b_fc2):
        import jax, jax.numpy as jnp
        import numpy as np
        DIM = 256
        HEADS = 4
        HEAD_DIM = DIM // HEADS
        MLP_HIDDEN = DIM * 3
        B, N = (8, 128)
        EPS = 1e-05

        def _layernorm(x, g, b):
            mu = jnp.mean(x, axis=-1, keepdims=True)
            var = jnp.mean(jnp.square(x - mu), axis=-1, keepdims=True)
            return (x - mu) * jax.lax.rsqrt(var + EPS) * g + b
        Bx, Nx, C = x.shape
        scale = HEAD_DIM ** (-0.5)
        qkv = (x @ w_qkv + b_qkv).reshape(Bx, Nx, 3, HEADS, HEAD_DIM)
        qkv = jnp.transpose(qkv, (2, 0, 3, 1, 4))
        q, k, v = (qkv[0], qkv[1], qkv[2])
        k = k * scale
        attn = jnp.einsum('bhnd,bhne->bhde', k, v)
        attn = jax.nn.softmax(attn, axis=-1)
        xf = jnp.einsum('bhde,bhne->bhnd', attn, q)
        xf = jnp.transpose(xf, (0, 2, 1, 3)).reshape(Bx, Nx, C)
        x = x + xf
        h = _layernorm(x, norm_g, norm_b)
        h = jax.nn.gelu(h @ w_fc1 + b_fc1, approximate=False) @ w_fc2 + b_fc2
        return x + h

    def _L0_ffn_ref(x, Wr, br, W1, b1, g1, be1, m1, v1, W2, b2, g2, be2, m2, v2, Wo, bo):
        import jax, jax.numpy as jnp
        import numpy as np
        BN_EPS = 0.001

        def _bn(h, g, b, m, v):
            return g * (h - m) * jax.lax.rsqrt(v + BN_EPS) + b
        feat = jnp.mean(x, axis=0)
        w = jax.nn.softmax(feat @ Wr + br, axis=-1)
        h = jnp.einsum('bfd,edh->bfeh', x, W1) + b1
        h = jax.nn.relu(_bn(h, g1, be1, m1, v1))
        h = jnp.einsum('bfeh,ehk->bfek', h, W2) + b2
        h = jax.nn.relu(_bn(h, g2, be2, m2, v2))
        y = jnp.einsum('bfeh,ehd->bfed', h, Wo) + bo
        return jnp.einsum('bfed,fe->bfd', y, w)

    def _L1_gnn_ref(x, edge_index, W1l, b1l, W1r, W2l, b2l, W2r, W3l, b3l, W3r):
        import jax, jax.numpy as jnp
        import numpy as np
        N_NODES = 50000
        N_EDGES = 25000
        D_IN = 256
        D_HID = 256
        D_OUT = 256

        def _sage_conv(x, src, dst, Wl, bl, Wr, num_nodes):
            msg = x[src]
            agg = jax.ops.segment_sum(msg, dst, num_segments=num_nodes)
            deg = jax.ops.segment_sum(jnp.ones((src.shape[0],), x.dtype), dst, num_segments=num_nodes)
            mean = agg / jnp.maximum(deg, 1.0)[:, None]
            return jnp.einsum('nd,od->no', mean, Wl) + bl + jnp.einsum('nd,od->no', x, Wr)
        src, dst = (edge_index[0], edge_index[1])
        n = x.shape[0]
        h = _sage_conv(x, src, dst, W1l, b1l, W1r, n)
        h = jax.nn.relu(h)
        h = _sage_conv(h, src, dst, W2l, b2l, W2r, n)
        h = jax.nn.relu(h)
        h = _sage_conv(h, src, dst, W3l, b3l, W3r, n)
        return h

    def _L1_mix_ref(x, t, w_qkv, mem_kv, w_out, b_out, g_out, g_pre):
        import jax, jax.numpy as jnp
        import numpy as np
        DIM = 256
        HEADS = 4
        DIM_HEAD = 32
        NUM_MEM = 4
        HIDDEN = HEADS * DIM_HEAD
        SCALE = DIM_HEAD ** (-0.5)

        def rmsnorm(x, g):
            n = jnp.linalg.norm(x, axis=-1, keepdims=True)
            return x / jnp.maximum(n, 1e-12) * g * x.shape[-1] ** 0.5
        b, n, c = x.shape
        xn = rmsnorm(x, g_pre)
        qkv = xn @ w_qkv
        q, k, v = jnp.split(qkv, 3, axis=-1)

        def to_heads(z):
            return z.reshape(b, n, HEADS, DIM_HEAD).transpose(0, 2, 3, 1)
        q, k, v = map(to_heads, (q, k, v))
        mk = jnp.broadcast_to(mem_kv[0], (b, HEADS, DIM_HEAD, NUM_MEM))
        mv = jnp.broadcast_to(mem_kv[1], (b, HEADS, DIM_HEAD, NUM_MEM))
        k = jnp.concatenate([mk, k], axis=-1)
        v = jnp.concatenate([mv, v], axis=-1)
        q = jax.nn.softmax(q, axis=-2) * SCALE
        k = jax.nn.softmax(k, axis=-1)
        context = jnp.einsum('bhdn,bhen->bhde', k, v)
        out = jnp.einsum('bhde,bhdn->bhen', context, q)
        out = out.transpose(0, 3, 1, 2).reshape(b, n, HIDDEN)
        out = rmsnorm(out @ w_out + b_out, g_out)
        return out + x

    def _L1_ffn_ref(x, attention_mask, wr, br, w1, b1, w2, b2):
        import jax, jax.numpy as jnp
        import numpy as np
        B, S, D = (8, 128, 256)
        H = 4 * D
        CAPACITY = 0.5
        b, s, d = x.shape
        weights = (jnp.einsum('bsd,do->bso', x, wr) + br)[..., 0]
        k = max(1, int(CAPACITY * s))
        kk = k - 1 if k > 1 else 1
        _, idx = jax.lax.top_k(weights, k)
        sel_idx = idx[:, :kk]
        sel = jnp.take_along_axis(x, sel_idx[:, :, None], axis=1)
        h = jax.nn.gelu(jnp.einsum('bkd,dh->bkh', sel, w1) + b1)
        y = jnp.einsum('bkh,hd->bkd', h, w2) + b2
        w_sel = jnp.take_along_axis(weights, sel_idx, axis=1)
        y = y * w_sel[..., None]
        batch_idx = jnp.arange(b)[:, None]
        processed = jnp.zeros_like(x).at[batch_idx, sel_idx].set(y)
        return processed + x
    edge_index = jnp.stack([src, dst])
    xn = _layernorm(x, axis=-1)
    x = x + _L0_gnn_ref(xn, src, dst, L0_gnn_theta_w, L0_gnn_theta_b, L0_gnn_phi_w, L0_gnn_phi_b) + _L0_mix_ref(xn[None], L0_mix_w_qkv, L0_mix_b_qkv, L0_mix_norm_g, L0_mix_norm_b, L0_mix_w_fc1, L0_mix_b_fc1, L0_mix_w_fc2, L0_mix_b_fc2)[0]
    x = x + _L0_ffn_ref(_layernorm(x, axis=-1)[None], L0_ffn_Wr, L0_ffn_br, L0_ffn_W1, L0_ffn_b1, L0_ffn_g1, L0_ffn_be1, L0_ffn_m1, L0_ffn_v1, L0_ffn_W2, L0_ffn_b2, L0_ffn_g2, L0_ffn_be2, L0_ffn_m2, L0_ffn_v2, L0_ffn_Wo, L0_ffn_bo)[0]
    xn = _layernorm(x, axis=-1)
    x = x + _L1_gnn_ref(xn, edge_index, L1_gnn_W1l, L1_gnn_b1l, L1_gnn_W1r, L1_gnn_W2l, L1_gnn_b2l, L1_gnn_W2r, L1_gnn_W3l, L1_gnn_b3l, L1_gnn_W3r) + _L1_mix_ref(xn[None], L1_mix_t, L1_mix_w_qkv, L1_mix_mem_kv, L1_mix_w_out, L1_mix_b_out, L1_mix_g_out, L1_mix_g_pre)[0]
    x = x + _L1_ffn_ref(_layernorm(x, axis=-1)[None], L1_ffn_attention_mask, L1_ffn_wr, L1_ffn_br, L1_ffn_w1, L1_ffn_b1, L1_ffn_w2, L1_ffn_b2)[0]
    return x

_drawn_inputs = setup_inputs


def setup_inputs(seed=0):
    import zlib

    import numpy as np

    out = dict(_drawn_inputs(seed))
    spreads = {'L0_gnn_theta_b': (0.0, 0.1),
     'L0_gnn_phi_b': (0.0, 0.1),
     'L0_mix_b_qkv': (0.0, 0.1),
     'L0_mix_norm_g': (1.0, 0.6),
     'L0_mix_norm_b': (0.0, 0.8),
     'L0_mix_b_fc1': (0.0, 0.638),
     'L0_mix_b_fc2': (0.0, 0.1),
     'L0_ffn_br': (0.0, 0.544),
     'L0_ffn_b1': (0.0, 0.741),
     'L0_ffn_g1': (1.0, 0.6),
     'L0_ffn_be1': (0.0, 0.755),
     'L0_ffn_m1': (0.0, 0.729),
     'L0_ffn_v1': (1.0, 0.6),
     'L0_ffn_b2': (0.0, 0.531),
     'L0_ffn_g2': (1.0, 0.6),
     'L0_ffn_be2': (0.0, 0.555),
     'L0_ffn_m2': (0.0, 0.542),
     'L0_ffn_v2': (1.0, 0.6),
     'L0_ffn_bo': (0.0, 0.381),
     'L1_gnn_b1l': (0.0, 0.336),
     'L1_gnn_b2l': (0.0, 0.323),
     'L1_gnn_b3l': (0.0, 0.294),
     'L1_mix_b_out': (0.0, 0.1),
     'L1_mix_g_out': (1.0, 0.2),
     'L1_mix_g_pre': (1.0, 0.6),
     'L1_ffn_b1': (0.0, 0.8),
     'L1_ffn_b2': (0.0, 0.8)}
    factors = {'L1_mix_w_qkv': 8.0,
     'L1_mix_mem_kv': 8.0,
     'L1_mix_w_out': 8.0,
     'L1_ffn_wr': 8.0,
     'L1_ffn_w1': 8.0,
     'L1_ffn_w2': 8.0}
    for name, (base, spread) in spreads.items():
        noise = np.random.default_rng([zlib.crc32(name.encode()), seed]).standard_normal(out[name].shape)
        drawn = base * np.exp(spread * noise) if base else spread * noise
        out[name] = jnp.asarray(drawn.astype(out[name].dtype))
    for name, factor in factors.items():
        out[name] = (out[name] * factor).astype(out[name].dtype)
    return out
```

```python
from contextlib import ExitStack

import concourse.bass as bass
from concourse import mybir

F32 = mybir.dt.float32
F16 = mybir.dt.float16
BF16 = mybir.dt.bfloat16
I32 = mybir.dt.int32
ALU = mybir.AluOpType
ACT = mybir.ActivationFunctionType
AX = mybir.AxisListType

N = 3125
E = 50000
D = 256
P = 128
KH = D // P
B = 125
NB = N // B
T = 448
NT = -(-N // T)
NP = NT * T
EC = E // B
WC = 4
WE = WC * B
NW = EC // WC
HEADS0, HD0 = 4, 64
HEADS1, HD1, MEM = 4, 32, 4
HID0 = 3 * D
NEXP = 8
HID1 = 4 * D
TOPK = int(0.5 * N) - 1
BIG = 3.3895313892515355e38
ROUND = 12582912.0


class Steps:

    def __init__(self, eng, sem):
        self.eng, self.sem, self.base, self.n = eng, sem, 0, 0

    def __call__(self, ins):
        self.n += 1
        ins.then_inc(self.sem, 1)
        self.eng.wait_ge(self.sem, self.base + self.n)

    def turn(self, t, per_turn):
        self.base, self.n = t * per_turn, 0


class Scope(ExitStack):

    def __init__(self, nc, stage):
        super().__init__()
        self.nc, self.stage, self.sems = nc, stage, []

    def sb(self, name, shape, dt=F32):
        return self.enter_context(self.nc.sbuf_tensor(f"{self.stage}_{name}", shape, dt))

    def sem(self, name):
        self.sems.append(self.nc.alloc_semaphore(f"{self.stage}_{name}"))
        return self.sems[-1]

    def __exit__(self, *error):
        if self.sems and not error[0]:
            self.nc.clear_and_free_semaphores(self.sems)
            self.nc.all_engine_barrier()
        return super().__exit__(*error)


def constants(nc, c):
    with Scope(nc, "constants") as s:
        row_i = s.sb("row_i", [P, P], I32)
        col_i = s.sb("col_i", [P, 1], I32)
        col_f = s.sb("col_f", [P, 1])
        made = s.sem("iota_made")
        own = s.sem("const_steps")
        with nc.Block() as block:
            @block.gpsimd
            def _(pool):
                nc.gpsimd.iota(row_i[:], [[1, P]], base=0, channel_multiplier=0).then_inc(made, 1)
                nc.gpsimd.iota(col_i[:], [[0, 1]], base=0, channel_multiplier=1).then_inc(made, 1)
                nc.gpsimd.iota(c.spare[:], [[B, WC]], base=N * NP, channel_multiplier=1).then_inc(made, 1)

            @block.vector
            def _(dve):
                step = Steps(dve, own)
                v = nc.vector
                v.memset(c.ones[:], 1.0)
                v.memset(c.mean_w[:], 1.0 / D)
                dve.wait_ge(made, 3)
                v.tensor_copy(c.spare_f[:], c.spare[:])
                step(v.tensor_copy(c.row[:], row_i[:]))
                step(v.tensor_copy(col_f[:], col_i[:]))
                v.tensor_scalar(c.ident[:], c.row[:], col_f[:, 0:1], None, ALU.is_equal)
                v.tensor_scalar(c.upto[:], c.row[:], col_f[:, 0:1], None, ALU.is_ge)
                v.memset(c.before[:], 1.0)
                step(v.tensor_scalar(c.eps5[:], col_f[:, 0:1], 0.0, 1e-5, ALU.mult, ALU.add))
                step(v.tensor_scalar(c.before[:, (WC - 1) * B:WE], c.row[0:B, 0:B], col_f[0:B, 0:1], None, ALU.is_lt))
                step(v.tensor_copy(c.row_b[:], c.row[0:B, 0:B]))


def edges(nc, c, src, dst, dram):
    A = EC // 100
    with Scope(nc, "edges") as s:
        src_r = s.sb("src_r", [100, A, B], I32)
        dst_r = s.sb("dst_r", [100, A, B], I32)
        prev_r = s.sb("prev_r", [100, A, B], I32)
        f_r = s.sb("f_r", [100, 3, A, B])
        same = s.sb("same", [100, A, B])
        reset = s.sb("reset", [100, A, B], BF16)
        dst_c = s.sb("dst_c", [B, EC])
        hi = s.sb("hi", [B, EC])
        hi_r = s.sb("hi_r", [B, EC])
        lo = s.sb("lo", [B, EC])
        oh_hi = s.sb("oh_hi", [B, EC, NB], BF16)
        oh_lo = s.sb("oh_lo", [B, 2, 16, B], BF16)
        deg = s.sb("deg", [B, NB])
        tot = s.sb("tot", [B, NB])
        off = s.sb("off", [B, NB])
        last = s.sb("last", [B, NB])
        rdeg = s.sb("rdeg", [B, NB])
        rdeg_t = s.sb("rdeg_t", [NB, B])
        zero = s.sb("zero", [B, NP], F16)
        ps = c.ps
        loaded = s.sem("edges_loaded")
        prev0 = s.sem("prev_cleared")
        own = s.sem("edge_steps")
        rows_ready = s.sem("rows_ready")
        turned = s.sem("rows_turned")
        hot_ready = s.sem("onehot_ready")
        hot_used = s.sem("onehot_used")
        deg_ready = s.sem("deg_ready")
        cum = s.sem("cum_done")
        rd = s.sem("rdeg_ready")
        rdt = s.sem("rdeg_turned")
        rdo = s.sem("rdeg_row_ready")
        stored = s.sem("edges_stored")
        z_ready = s.sem("zero_ready")
        zeroed = s.sem("adj_zeroed")
        HOT = 16
        NH = EC // HOT
        view = lambda a: a.rearrange("(a c p) -> c a p", c=100, p=B)
        with nc.Block() as block:
            @block.sync
            def _(sp):
                with nc.allow_non_contiguous_dma(reason="rows of 500 bytes"):
                    sp.dma_start(src_r[:], view(src)).then_inc(loaded, 16)
                    sp.dma_start(dst_r[:], view(dst)).then_inc(loaded, 16)
                    sp.wait_ge(prev0, 1)
                    sp.dma_start(prev_r[0:1, 0, 1:B], dst[0:B - 1].rearrange("(o p) -> o p", o=1)).then_inc(loaded, 16)
                    sp.dma_start(prev_r[1:100, 0, :], dst[B - 1:B - 1 + 99 * B].rearrange("(c p) -> c p", p=B)).then_inc(loaded, 16)
                    sp.dma_start(prev_r[:, 1:A, :], dst[100 * B - 1:E - 1].rearrange("(a c p) -> c a p", c=100, p=B)).then_inc(loaded, 16)
                    sp.wait_ge(z_ready, 1)
                    for j in range(NB):
                        sp.dma_start(dram.adj[B * j:B * (j + 1), :], zero[:]).then_inc(zeroed, 16)
                    sp.dma_start(dram.adj[N:N + 1, :], zero[0:1, :]).then_inc(zeroed, 16)
                    sp.wait_ge(rows_ready, 2)
                    sp.dma_start(view(dram.keys), f_r[:, 2]).then_inc(stored, 16)
                    sp.dma_start(view(dram.reset), reset[:]).then_inc(stored, 16)
                    sp.wait_ge(rdo, 1)
                    sp.dma_start(dram.rdeg.rearrange("(a p) -> a p", p=B), rdeg_t[:]).then_inc(stored, 16)
                    sp.wait_ge(stored, 48)
                    sp.wait_ge(zeroed, 16 * (NB + 1))

            @block.vector
            def _(dve):
                step = Steps(dve, own)
                v = nc.vector
                v.memset(prev_r[:], -1).then_inc(prev0, 1)
                v.memset(zero[:], 0.0).then_inc(z_ready, 1)
                dve.wait_ge(loaded, 80)
                v.tensor_copy(f_r[:, 0], src_r[:])
                step(v.tensor_copy(f_r[:, 1], dst_r[:]))
                step(v.scalar_tensor_tensor(f_r[:, 2], f_r[:, 0], float(NP), f_r[:, 1], ALU.mult, ALU.add))
                dve.sem_inc(rows_ready, 1)
                step(v.tensor_tensor(same[:], dst_r[:], prev_r[:], ALU.is_equal))
                step(v.tensor_scalar(same[:], same[:], 2.0, 1.0, ALU.mult, ALU.subtract))
                v.tensor_scalar(reset[:], same[:], BIG, None, ALU.mult).then_inc(rows_ready, 1)
                dve.wait_ge(turned, 1)
                v.tensor_copy(c.src_idx[:], ps[0][0:B, 0:EC])
                step(v.tensor_copy(dst_c[:], ps[1][0:B, 0:EC]))
                step(v.tensor_copy(c.key_c[:], ps[2][0:B, 0:EC]))
                step(v.tensor_scalar(hi[:], dst_c[:], (B - 1) / 2.0, 1.0 / B, ALU.subtract, ALU.mult))
                step(v.tensor_scalar(hi_r[:], hi[:], ROUND, None, ALU.add))
                step(v.tensor_scalar(hi[:], hi_r[:], ROUND, None, ALU.subtract))
                step(v.scalar_tensor_tensor(lo[:], hi[:], -float(B), dst_c[:], ALU.mult, ALU.add))
                step(v.tensor_tensor(oh_hi[:], hi[:].unsqueeze(2).to_broadcast([B, EC, NB]),
                                     c.row[0:B, 0:NB].unsqueeze(1).to_broadcast([B, EC, NB]), ALU.is_equal))
                for g in range(NH):
                    if g >= 2:
                        dve.wait_ge(hot_used, g - 1)
                    v.tensor_tensor(oh_lo[:, g % 2], lo[:, g * HOT:(g + 1) * HOT].unsqueeze(2).to_broadcast([B, HOT, B]),
                                    c.row_b[:].unsqueeze(1).to_broadcast([B, HOT, B]), ALU.is_equal).then_inc(hot_ready, 1)
                dve.wait_ge(hot_used, NH)
                step(v.tensor_copy(deg[:], ps[3][0:B, 0:NB]))
                v.tensor_scalar(c.has[:], deg[:], 0.0, None, ALU.is_gt)
                v.tensor_scalar(rdeg[:], deg[:], 1.0, None, ALU.max).then_inc(deg_ready, 1)
                dve.wait_ge(deg_ready, 1)
                step(v.tensor_scalar(c.lack[:], c.has[:], 1.0, BIG, ALU.subtract, ALU.mult))
                v.reciprocal(rdeg[:], rdeg[:]).then_inc(rd, 1)
                dve.wait_ge(cum, 1)
                step(v.tensor_copy(tot[:], ps[5][0:B, 0:NB]))
                step(v.tensor_tensor_scan(off[:], tot[:], tot[:], 0.0, ALU.add, ALU.max))
                step(v.tensor_tensor(off[:], off[:], tot[:], ALU.subtract))
                step(v.tensor_tensor(last[:], off[:], ps[4][0:B, 0:NB], ALU.add))
                step(v.tensor_scalar(last[:], last[:], 1.0, 0.0, ALU.subtract, ALU.max))
                step(v.tensor_copy(c.last_idx[:], last[:]))
                dve.wait_ge(rdt, 1)
                v.tensor_copy(rdeg_t[:], ps[6][0:NB, 0:B]).then_inc(rdo, 1)

            @block.tensor
            def _(pe):
                pe.wait_ge(rows_ready, 1)
                for k in range(3):
                    for a in range(A):
                        mm = nc.tensor.transpose(ps[k][0:B, 100 * a:100 * (a + 1)], f_r[:, k, a, :], c.ident[0:100, 0:100])
                mm.then_inc(turned, 1)
                for g in range(NH):
                    pe.wait_ge(hot_ready, g + 1)
                    for k in range(HOT):
                        e = g * HOT + k
                        mm = nc.tensor.matmul(ps[3][0:B, 0:NB], oh_lo[:, g % 2, k, :], oh_hi[:, e, :],
                                              start=(e == 0), stop=(e == EC - 1))
                    mm.then_inc(hot_used, 1)
                pe.wait_ge(deg_ready, 1)
                nc.tensor.matmul(ps[4][0:B, 0:NB], c.upto[0:B, 0:B], deg[:], start=True, stop=True)
                nc.tensor.matmul(ps[5][0:B, 0:NB], c.ones[0:B, 0:B], deg[:], start=True, stop=True).then_inc(cum, 1)
                pe.wait_ge(rd, 1)
                nc.tensor.transpose(ps[6][0:NB, 0:B], rdeg[:], c.ident[0:B, 0:B]).then_inc(rdt, 1)


def cols(t, width=T):
    return bass.ds(t * width, width)


def half(h):
    return slice(h * P, (h + 1) * P)


def nodes(nc, c, x, dram, w):
    with Scope(nc, "nodes") as s:
        xt = s.sb("xt", [B, NB, D])
        xn = s.sb("xn", [B, NB, D + 1])
        stats = s.sb("stats", [B, NB, 6])
        mv = s.sb("mv", [B, NB, 2])
        sd = s.sb("sd", [B, NB])
        rs = s.sb("rs", [B, NB])
        wb = s.sb("wb", [P, KH, D])
        bo = s.sb("bo", [B, 4, D])
        gram = s.sb("gram", [P, KH, D + 1])
        uu = s.sb("uu", [P, KH, D])
        csum = s.sb("csum", [1, D])
        rr = s.sb("rr", [1, D])
        cnt = s.sb("cnt", [1, 1])
        gs = s.sb("gs", [P, KH, P])
        mx = s.sb("mx", [P, KH])
        sm = s.sb("sm", [P, KH])
        att = s.sb("att", [P, KH, P])
        ps = c.ps
        loaded = s.sem("x_loaded")
        own = s.sem("node_steps")
        var_ready, sd_ready = s.sem("var_ready"), s.sem("sd_ready")
        xn_ready = s.sem("xn_ready")
        turned, taken_v, taken_a = s.sem("turned"), s.sem("taken_v"), s.sem("taken_a")
        gram_done, gram_out = s.sem("gram_done"), s.sem("gram_out")
        b_done, b_out = s.sem("b_done"), s.sem("b_out")
        b_stored = [s.sem(f"b_stored{k}") for k in range(4)]
        wb_ready = s.sem("wb_ready")
        att_pe, att_v, att_a = s.sem("att_pe"), s.sem("att_v"), s.sem("att_a")
        G4 = -(-NB // 4)
        groups = [(g, min(4, NB - 4 * g)) for g in range(G4)]
        with nc.Block() as block:
            @block.sync
            def _(sp):
                sp.dma_start(xt[:], x.rearrange("(j p) f -> p j f", p=B)).then_inc(loaded, 16)
                for j in range(NB):
                    sp.wait_ge(b_out, j + 1)
                    sp.dma_start(dram.rows[B * j:B * (j + 1), :], bo[:, j % 4, :]).then_inc(b_stored[j % 4], 16)
                for k in range(4):
                    sp.wait_ge(b_stored[k], 16 * len(range(k, NB, 4)))

            @block.scalar
            def _(act):
                act.wait_ge(var_ready, 1)
                nc.scalar.activation(sd[:], mv[:, :, 1], ACT.Sqrt, bias=c.eps5[0:B, 0:1]).then_inc(sd_ready, 1)
                for g, n in groups:
                    for h in range(KH):
                        k = 4 * g + 2 + h
                        act.wait_ge(turned, k + 1)
                        nc.scalar.copy(c.yn[:, h, 4 * B * g:4 * B * g + n * B], ps[k % 4][:, 0:n * B]).then_inc(taken_a, 1)
                act.wait_ge(att_v, 2)
                nc.scalar.activation(att[:], gs[:], ACT.Exp).then_inc(att_a, 1)

            @block.vector
            def _(dve):
                step = Steps(dve, own)
                v = nc.vector
                v.memset(c.xT[:, :, N:NP], 0.0)
                v.memset(c.yn[:, :, N:NP], 0.0)
                v.memset(cnt[:], float(N))
                step(v.memset(xn[:, :, D:D + 1], 1.0))
                dve.wait_ge(w.loaded, w.total)
                v.tensor_tensor(wb[:], w.phi[:], w.theta[:], ALU.subtract).then_inc(wb_ready, 1)
                dve.wait_ge(loaded, 16)
                for j in range(NB):
                    ins = v.bn_stats(stats[:, j, :], xt[:, j, :])
                step(ins)
                for j in range(NB):
                    ins = v.bn_aggr(mv[:, j, :], stats[:, j, :])
                ins.then_inc(var_ready, 1)
                dve.wait_ge(sd_ready, 1)
                dve.wait_ge(var_ready, 1)
                step(v.reciprocal(rs[:], sd[:]))
                for j in range(NB):
                    v.tensor_scalar(xn[:, j, 0:D], xt[:, j, :], mv[:, j, 0:1], rs[:, j:j + 1],
                                    ALU.subtract, ALU.mult).then_inc(xn_ready, 1)
                for g, n in groups:
                    for h in range(KH):
                        k = 4 * g + h
                        dve.wait_ge(turned, k + 1)
                        v.tensor_copy(c.xT[:, h, 4 * B * g:4 * B * g + n * B], ps[k % 4][:, 0:n * B]).then_inc(taken_v, 1)
                for j in range(NB):
                    dve.wait_ge(b_done, j + 1)
                    if j >= 4:
                        dve.wait_ge(b_stored[j % 4], 16 * (j // 4))
                    v.tensor_copy(bo[:, j % 4, :], ps[j % 4][0:B, 0:D]).then_inc(b_out, 1)
                dve.wait_ge(gram_done, 1)
                v.tensor_copy(gram[:, 0, :], ps[4][:, 0:D + 1])
                v.tensor_copy(gram[:, 1, :], ps[5][:, 0:D + 1])
                v.tensor_copy(csum[:], ps[6][0:1, 0:D]).then_inc(gram_out, 1)
                dve.wait_ge(att_pe, 1)
                v.tensor_copy(uu[:, 0, :], ps[0][:, 0:D])
                v.tensor_copy(uu[:, 1, :], ps[1][:, 0:D])
                v.tensor_copy(rr[:], ps[2][0:1, 0:D]).then_inc(att_v, 1)
                dve.wait_ge(att_pe, 2)
                scale = HD0 ** -0.5
                v.tensor_scalar(gs[:, 0, :], ps[3][:, 0:P], scale, None, ALU.mult)
                step(v.tensor_scalar(gs[:, 1, :], ps[4][:, P:2 * P], scale, None, ALU.mult))
                for h in range(KH):
                    for q in range(2):
                        r = slice(q * HD0, (q + 1) * HD0)
                        ins = v.tensor_reduce(mx[r, h:h + 1], gs[r, h, r], AX.X, ALU.max)
                step(ins)
                step(v.tensor_copy(sm[:], mx[:]))
                for h in range(KH):
                    ins = v.tensor_scalar(gs[:, h, :], gs[:, h, :], mx[:, h:h + 1], 0.0, ALU.subtract, ALU.min)
                ins.then_inc(att_v, 1)
                dve.wait_ge(att_a, 1)
                for h in range(KH):
                    v.memset(att[0:HD0, h, HD0:P], 0.0)
                    step(v.memset(att[HD0:P, h, 0:HD0], 0.0))
                step(v.tensor_reduce(sm[:], att[:], AX.X, ALU.add))
                step(v.reciprocal(sm[:], sm[:]))
                for h in range(KH):
                    ins = v.tensor_scalar(att[:, h, :], att[:, h, :], sm[:, h:h + 1], None, ALU.mult)
                ins.then_inc(att_v, 1)
                dve.wait_ge(att_pe, 3)
                v.tensor_copy(c.attT[:, 0, :], ps[0][:, 0:P])
                v.tensor_copy(c.attT[:, 1, :], ps[1][:, 0:P])

            @block.tensor
            def _(pe):
                mm = nc.tensor.matmul
                pe.wait_ge(loaded, 16)
                for g, n in groups:
                    pe.wait_ge(xn_ready, 4 * g + n)
                    for k, (a, h) in enumerate(((xt, 0), (xt, 1), (xn, 0), (xn, 1))):
                        if g >= 1:
                            if k < 2:
                                pe.wait_ge(taken_v, 2 * (g - 1) + k + 1)
                            else:
                                pe.wait_ge(taken_a, 2 * (g - 1) + k - 1)
                        for i in range(n):
                            ins = nc.tensor.transpose(ps[k][:, B * i:B * (i + 1)], a[:, 4 * g + i, half(h)], c.ident[0:B, 0:B])
                        ins.then_inc(turned, 1)
                pe.wait_ge(taken_v, 2 * G4)
                pe.wait_ge(taken_a, 2 * G4)
                pe.wait_ge(wb_ready, 1)
                for j in range(NB):
                    if j >= 4:
                        pe.wait_ge(b_out, j - 3)
                    for k in range(KH):
                        ins = mm(ps[j % 4][0:B, 0:D], c.yn[:, k, B * j:B * (j + 1)], wb[:, k, :], start=(k == 0), stop=(k == KH - 1))
                    ins.then_inc(b_done, 1)
                for j in range(NB):
                    for h in range(KH):
                        mm(ps[4 + h][:, 0:D + 1], xn[:, j, half(h)], xn[:, j, :], start=(j == 0), stop=(j == NB - 1))
                    ins = mm(ps[6][0:1, 0:D], c.ones[0:B, 0:1], xn[:, j, 0:D], start=(j == 0), stop=(j == NB - 1))
                ins.then_inc(gram_done, 1)
                pe.wait_ge(gram_out, 1)
                pe.wait_ge(b_out, NB)
                for h in range(KH):
                    for k in range(KH):
                        mm(ps[h][:, 0:D], gram[:, k, half(h)], w.qkv[:, k, 2 * D:3 * D], start=(k == 0), stop=False)
                    mm(ps[h][:, 0:D], csum[0:1, half(h)], w.bqkv_row[0:1, 2 * D:3 * D], start=False, stop=True)
                for k in range(KH):
                    mm(ps[2][0:1, 0:D], gram[:, k, D:D + 1], w.qkv[:, k, 2 * D:3 * D], start=(k == 0), stop=False)
                mm(ps[2][0:1, 0:D], cnt[0:1, 0:1], w.bqkv_row[0:1, 2 * D:3 * D], start=False, stop=True).then_inc(att_pe, 1)
                pe.wait_ge(att_v, 1)
                for h in range(KH):
                    for k in range(KH):
                        mm(ps[3 + h][:, 0:D], w.qkv[:, k, D + h * P:D + (h + 1) * P], uu[:, k, :], start=(k == 0), stop=False)
                    ins = mm(ps[3 + h][:, 0:D], w.bqkv_row[0:1, D + h * P:D + (h + 1) * P], rr[0:1, :], start=False, stop=True)
                ins.then_inc(att_pe, 1)
                pe.wait_ge(att_v, 3)
                for h in range(KH):
                    ins = nc.tensor.transpose(ps[h][:, 0:P], att[:, h, :], c.ident[:])
                ins.then_inc(att_pe, 1)


def segment_max(nc, c, dram):
    with Scope(nc, "segment_max") as s:
        got = [s.sb(f"got{i}", [B, D]) for i in range(2 * WC)]
        rst = s.sb("rst", [P, 2, WE], BF16)
        scan = s.sb("scan", [P, 2, KH, WE])
        back = s.sb("back", [B, 2, WC, D])
        ps = c.ps
        gathered = [s.sem(f"gathered{i}") for i in range(2 * WC)]
        rst_in = [s.sem(f"rst_in{b}") for b in range(2)]
        stored = [s.sem(f"run_stored{b}") for b in range(2)]
        turned, scanned, turned_back, copied = s.sem("g_turned"), s.sem("scanned"), s.sem("turned_back"), s.sem("back_copied")
        runs = dram.runs.rearrange("(w c p) f -> w p c f", c=WC, p=B)
        with nc.Block() as block:
            @block.gpsimd
            def _(pool):
                for w in range(NW):
                    for j in range(WC):
                        if w >= 2:
                            pool.wait_ge(turned, WC * (w - 2) + j + 1)
                        i, k = WC * (w % 2) + j, WC * w + j
                        nc.gpsimd.indirect_dma_start(got[i][:, :], None, dram.rows[:, :],
                                                     bass.IndirectOffsetOnAxis(ap=c.src_idx[:, k:k + 1], axis=0)).then_inc(gathered[i], 16)

            @block.sync
            def _(sp):
                def load(w, b):
                    sp.wait_ge(scanned, 2 * w + 2)
                    sp.dma_start(rst[:, b, :], dram.reset[bass.ds(w * WE, WE)].partition_broadcast(P)).then_inc(rst_in[b], 16)

                def store(w, b):
                    sp.wait_ge(copied, 2 * w + 6)
                    sp.dma_start(runs[bass.ds(w, 1)].rearrange("o p c f -> (o p) c f"), back[:, b]).then_inc(stored[b], 16)

                for b in range(2):
                    sp.sem_inc(stored[b], 16)
                    load(b, b)
                with sp.Fori(0, NW // 2 - 1) as i:
                    for b in range(2):
                        store(2 * i + b, b)
                        load(2 * i + 2 + b, b)
                for b in range(2):
                    store(NW - 2 + b, b)
                for b in range(2):
                    sp.wait_ge(stored[b], 16 * (NW // 2 + 1))

            @block.tensor
            def _(pe):
                def forward(w, b):
                    pe.wait_ge(scanned, 2 * w + 2)
                    for j in range(WC):
                        pe.wait_ge(gathered[WC * b + j], 8 * (w - b) + 16)
                        for h in range(KH):
                            ins = nc.tensor.transpose(ps[2 * b + h][:, B * j:B * (j + 1)], got[WC * b + j][:, half(h)], c.ident[0:B, 0:B])
                        ins.then_inc(turned, 1)

                def backward(w, b):
                    pe.wait_ge(scanned, 2 * w + 6)
                    pe.wait_ge(copied, 2 * w + 2)
                    for j in range(WC):
                        for h in range(KH):
                            at = D * (j % 2) + P * h
                            ins = nc.tensor.transpose(ps[4 + 2 * b + j // 2][0:B, at:at + P], scan[:, b, h, B * j:B * (j + 1)], c.ident[:])
                        if j % 2:
                            ins.then_inc(turned_back, 1)

                pe.sem_inc(turned_back, 4)
                forward(0, 0)
                with pe.Fori(0, NW // 2 - 1) as i:
                    forward(2 * i + 1, 1)
                    backward(2 * i, 0)
                    forward(2 * i + 2, 0)
                    backward(2 * i + 1, 1)
                forward(NW - 1, 1)
                backward(NW - 2, 0)
                backward(NW - 1, 1)

            @block.vector
            def _(dve):
                nc.vector.memset(scan[:, 1, :, :], -BIG).then_inc(scanned, 4)
                with dve.Fori(0, NW // 2) as i:
                    for b in range(2):
                        w = 2 * i + b
                        dve.wait_ge(rst_in[b], 8 * (w - b) + 16)
                        dve.wait_ge(turned, WC * w + WC)
                        dve.wait_ge(turned_back, 2 * w + 2)
                        for h in range(KH):
                            dve.wait_ge(scanned, 2 * w + 3 + h)
                            nc.vector.tensor_tensor_scan(scan[:, b, h, :], rst[:, b, :], ps[2 * b + h][:, 0:WE],
                                                         scan[:, 1 - b, h, WE - 1:WE], ALU.min, ALU.max).then_inc(scanned, 1)

            @block.scalar
            def _(act):
                act.sem_inc(copied, 4)
                with act.Fori(0, NW // 2) as i:
                    for b in range(2):
                        w = 2 * i + b
                        act.wait_ge(stored[b], 8 * (w - b) + 16)
                        for q in range(2):
                            act.wait_ge(turned_back, 2 * w + 5 + q)
                            nc.scalar.copy(back[:, b, 2 * q:2 * q + 2, :], ps[4 + 2 * b + q][0:B, 0:2 * D]).then_inc(copied, 1)


def join_max(nc, c, dram):
    with Scope(nc, "join_max") as s:
        m = s.sb("m", [B, NB, D])
        mm_ = s.sb("mm_", [B, NB, D])
        t1 = s.sb("t1", [P, 2, 4 * B])
        got = [s.sem(f"m_got{i}") for i in range(NB)]
        masked, turned, summed, own = s.sem("m_masked"), s.sem("m_turned"), s.sem("m_summed"), s.sem("join_steps")
        G4 = -(-NB // 4)
        with nc.Block() as block:
            @block.gpsimd
            def _(pool):
                for j in range(NB):
                    nc.gpsimd.indirect_dma_start(m[:, j, :], None, dram.runs[:, :],
                                                 bass.IndirectOffsetOnAxis(ap=c.last_idx[:, j:j + 1], axis=0)).then_inc(got[j], 16)

            @block.vector
            def _(dve):
                v = nc.vector
                step = Steps(dve, own)
                for j in range(NB):
                    dve.wait_ge(got[j], 16)
                    v.tensor_scalar(mm_[:, j, :], m[:, j, :], c.has[:, j:j + 1], c.lack[:, j:j + 1], ALU.mult, ALU.add).then_inc(masked, 1)
                for g in range(G4):
                    n = min(4, NB - 4 * g) * B
                    at = slice(4 * B * g, 4 * B * g + n)
                    for h in range(KH):
                        k = 2 * g + h
                        dve.wait_ge(turned, k + 1)
                        v.tensor_tensor(t1[:, h, 0:n], c.ps[k % 8][:, 0:n], c.a[:, h, at], ALU.add).then_inc(summed, 1)
                        dve.wait_ge(summed, k + 1)
                        step(v.scalar_tensor_tensor(c.xT[:, h, at], t1[:, h, 0:n], 0.0, c.xT[:, h, at], ALU.max, ALU.add))

            @block.tensor
            def _(pe):
                for g in range(G4):
                    n = min(4, NB - 4 * g)
                    pe.wait_ge(masked, 4 * g + n)
                    for h in range(KH):
                        k = 2 * g + h
                        if k >= 8:
                            pe.wait_ge(summed, k - 7)
                        for i in range(n):
                            ins = nc.tensor.transpose(c.ps[k % 8][:, B * i:B * (i + 1)], mm_[:, 4 * g + i, half(h)], c.ident[0:B, 0:B])
                        ins.then_inc(turned, 1)


def product(nc, out, lhs, rhs, chain=True):
    for k, (a, b) in enumerate(zip(lhs, rhs)):
        ins = nc.tensor.matmul(out, a, b, start=(k == 0), stop=(k == len(lhs) - 1))
    return ins


def mix0(nc, c, w):
    with Scope(nc, "mix0") as s:
        q = s.sb("q", [P, KH, T])
        sx = s.sb("sx", [P, KH, T])
        cen = s.sb("cen", [P, KH, T])
        sq = s.sb("sq", [P, KH, T])
        sd = s.sb("sd", [P, T])
        hn = s.sb("hn", [P, KH, T])
        hid = s.sb("hid", [P, HID0 // P, T])
        ab = s.sb("ab", [P, KH])
        ps = c.ps
        M1 = HID0 // P
        pe_done, act_done, own = s.sem("mix_pe"), s.sem("mix_act"), s.sem("mix_steps")
        PE_N, ACT_N, DVE_N = 6 + M1, 3 + M1, 15
        with nc.Block() as block:
            @block.tensor
            def _(pe):
                with pe.Fori(0, NT) as t:
                    pe_at = lambda n: t * PE_N + n
                    tile = [c.yn[:, k, cols(t)] for k in range(KH)]
                    pe.wait_ge(own, t * DVE_N + 1)
                    for h in range(KH):
                        product(nc, ps[h][:, 0:T], [w.qkv[:, k, half(h)] for k in range(KH)], tile)
                    for h in range(KH):
                        ins = product(nc, ps[2 + h][:, 0:T], [w.theta[:, k, half(h)] for k in range(KH)], tile)
                    ins.then_inc(pe_done, 1)
                    pe.wait_ge(act_done, t * ACT_N + 1)
                    for h in range(KH):
                        ins = product(nc, ps[4 + h][:, 0:T], [c.attT[:, h, :]], [q[:, h, :]])
                    ins.then_inc(pe_done, 1)
                    pe.wait_ge(own, t * DVE_N + 5)
                    product(nc, ps[6][:, 0:T], [c.mean_w[:]] * KH, [sx[:, k, :] for k in range(KH)]).then_inc(pe_done, 1)
                    pe.wait_ge(act_done, t * ACT_N + 2)
                    product(nc, ps[7][:, 0:T], [c.mean_w[:]] * KH, [sq[:, k, :] for k in range(KH)]).then_inc(pe_done, 1)
                    pe.wait_ge(own, t * DVE_N + 12)
                    for m in range(M1):
                        product(nc, ps[m][:, 0:T], [w.fc1[:, k, m * P:(m + 1) * P] for k in range(KH)],
                                [hn[:, k, :] for k in range(KH)]).then_inc(pe_done, 1)
                    pe.wait_ge(act_done, t * ACT_N + 3 + M1)
                    for h in range(KH):
                        product(nc, ps[6 + h][:, 0:T], [w.fc2[:, m, half(h)] for m in range(M1)],
                                [hid[:, m, :] for m in range(M1)]).then_inc(pe_done, 1)

            @block.scalar
            def _(act):
                a = nc.scalar.activation
                with act.Fori(0, NT) as t:
                    act.wait_ge(pe_done, t * PE_N + 1)
                    a(q[:, 0, :], ps[0][:, 0:T], ACT.Identity, bias=w.bq[:, 0:1])
                    a(q[:, 1, :], ps[1][:, 0:T], ACT.Identity, bias=w.bq[:, 1:2]).then_inc(act_done, 1)
                    act.wait_ge(own, t * DVE_N + 7)
                    a(sq[:], cen[:], ACT.Square).then_inc(act_done, 1)
                    act.wait_ge(pe_done, t * PE_N + 4)
                    a(sd[:], ps[7][:, 0:T], ACT.Sqrt, bias=c.eps5[:, 0:1]).then_inc(act_done, 1)
                    for m in range(M1):
                        act.wait_ge(pe_done, t * PE_N + 5 + m)
                        a(hid[:, m, :], ps[m][:, 0:T], ACT.Gelu, bias=w.b1[:, m:m + 1]).then_inc(act_done, 1)

            @block.vector
            def _(dve):
                v = nc.vector
                step = Steps(dve, own)
                step(v.tensor_tensor(ab[:], w.tb[:], w.pb[:], ALU.add))
                with dve.Fori(0, NT) as t:
                    step.turn(t, DVE_N)
                    step.n = 1
                    at = cols(t)
                    dve.wait_ge(pe_done, t * PE_N + 1)
                    for h in range(KH):
                        step(v.tensor_scalar(c.a[:, h, at], ps[2 + h][:, 0:T], ab[:, h:h + 1], None, ALU.add))
                    dve.wait_ge(pe_done, t * PE_N + 2)
                    for h in range(KH):
                        step(v.tensor_tensor(sx[:, h, :], ps[4 + h][:, 0:T], c.yn[:, h, at], ALU.add))
                    dve.wait_ge(pe_done, t * PE_N + 3)
                    for h in range(KH):
                        step(v.tensor_tensor(cen[:, h, :], sx[:, h, :], ps[6][:, 0:T], ALU.subtract))
                    dve.wait_ge(act_done, t * ACT_N + 3)
                    step(v.reciprocal(sd[:], sd[:]))
                    for h in range(KH):
                        step(v.tensor_tensor(cen[:, h, :], cen[:, h, :], sd[:], ALU.mult))
                    for h in range(KH):
                        step(v.tensor_scalar(hn[:, h, :], cen[:, h, :], w.ng[:, h:h + 1], w.nb[:, h:h + 1], ALU.mult, ALU.add))
                    dve.wait_ge(pe_done, t * PE_N + 6 + M1)
                    for h in range(KH):
                        step(v.scalar_tensor_tensor(cen[:, h, :], ps[6 + h][:, 0:T], w.b2[:, h:h + 1], sx[:, h, :], ALU.add, ALU.add))
                    for h in range(KH):
                        step(v.tensor_tensor(c.xT[:, h, at], c.xT[:, h, at], cen[:, h, :], ALU.add))


def norm(nc, c, out, n):
    with Scope(nc, f"norm{n}") as s:
        sq = s.sb("sq", [P, 2, KH, T])
        sd = s.sb("sd", [P, 2, T])
        ps = c.ps
        mean_done, var_done = s.sem("mean_done"), s.sem("var_done")
        cen_ready, sq_ready, sd_ready, sd_used = s.sem("cen_ready"), s.sem("sq_ready"), s.sem("sd_ready"), s.sem("sd_used")
        own = s.sem("norm_steps")
        at = lambda t: slice(t * T, (t + 1) * T)
        with nc.Block() as block:
            @block.tensor
            def _(pe):
                def mean(t):
                    if t >= 4:
                        pe.wait_ge(cen_ready, t - 3)
                    product(nc, ps[t % 4][:, 0:T], [c.mean_w[:]] * KH, [c.xT[:, k, at(t)] for k in range(KH)]).then_inc(mean_done, 1)

                def var(t):
                    if t >= 4:
                        pe.wait_ge(sd_ready, t - 3)
                    pe.wait_ge(sq_ready, t + 1)
                    product(nc, ps[4 + t % 4][:, 0:T], [c.mean_w[:]] * KH, [sq[:, t % 2, k, :] for k in range(KH)]).then_inc(var_done, 1)

                for t in range(NT + 2):
                    if t < NT:
                        mean(t)
                    if t >= 2:
                        var(t - 2)

            @block.scalar
            def _(act):
                for t in range(NT + 1):
                    if t < NT:
                        act.wait_ge(cen_ready, t + 1)
                        if t >= 2:
                            act.wait_ge(var_done, t - 1)
                        nc.scalar.activation(sq[:, t % 2], out[:, :, at(t)], ACT.Square).then_inc(sq_ready, 1)
                    if t >= 1:
                        act.wait_ge(var_done, t)
                        if t >= 3:
                            act.wait_ge(sd_used, t - 2)
                        nc.scalar.activation(sd[:, (t - 1) % 2], ps[4 + (t - 1) % 4][:, 0:T], ACT.Sqrt, bias=c.eps5[:, 0:1]).then_inc(sd_ready, 1)

            @block.vector
            def _(dve):
                v = nc.vector
                step = Steps(dve, own)
                for t in range(NT + 1):
                    if t < NT:
                        dve.wait_ge(mean_done, t + 1)
                        v.tensor_tensor(out[:, 0, at(t)], c.xT[:, 0, at(t)], ps[t % 4][:, 0:T], ALU.subtract)
                        v.tensor_tensor(out[:, 1, at(t)], c.xT[:, 1, at(t)], ps[t % 4][:, 0:T], ALU.subtract).then_inc(cen_ready, 1)
                    if t >= 1:
                        dve.wait_ge(sd_ready, t)
                        step(v.reciprocal(sd[:, (t - 1) % 2], sd[:, (t - 1) % 2]))
                        dve.wait_ge(sq_ready, t)
                        v.tensor_tensor(out[:, 0, at(t - 1)], out[:, 0, at(t - 1)], sd[:, (t - 1) % 2], ALU.mult)
                        v.tensor_tensor(out[:, 1, at(t - 1)], out[:, 1, at(t - 1)], sd[:, (t - 1) % 2], ALU.mult).then_inc(sd_used, 1)


def gate(nc, c, w, dram):
    with Scope(nc, "gate") as s:
        lg = s.sb("lg", [B, NB, NEXP])
        mx = s.sb("mx", [B, NB])
        wT = s.sb("wT", [NEXP, NP])
        ps = c.ps
        G4 = -(-NB // 4)
        logits, ready, ex, own = s.sem("logits"), s.sem("lg_ready"), s.sem("lg_exp"), s.sem("gate_steps")
        turned, copied, stored = s.sem("wg_turned"), s.sem("wg_copied"), s.sem("wg_stored")
        with nc.Block() as block:
            @block.tensor
            def _(pe):
                for j in range(NB):
                    at = slice(B * j, B * (j + 1))
                    out = ps[0][0:B, NEXP * j:NEXP * (j + 1)]
                    for k in range(KH):
                        nc.tensor.matmul(out, c.yn[:, k, at], w.Wr[:, k, :], start=(k == 0), stop=False)
                    ins = nc.tensor.matmul(out, c.ones[0:1, 0:B], w.br[:, :], start=False, stop=True)
                ins.then_inc(logits, 1)
                pe.wait_ge(ready, 2)
                for g in range(G4):
                    n = min(4, NB - 4 * g)
                    for i in range(n):
                        ins = nc.tensor.transpose(ps[1 + g][0:NEXP, B * i:B * (i + 1)], lg[:, 4 * g + i, :], c.ident[0:B, 0:B])
                    ins.then_inc(turned, 1)

            @block.vector
            def _(dve):
                v = nc.vector
                step = Steps(dve, own)
                v.memset(wT[:, N:NP], 0.0)
                dve.wait_ge(logits, 1)
                step(v.tensor_copy(lg[:], ps[0][0:B, 0:NB * NEXP].rearrange("p (j e) -> p j e", e=NEXP)))
                wide = mx[:].unsqueeze(2).to_broadcast([B, NB, NEXP])
                step(v.tensor_reduce(mx[:], lg[:], AX.X, ALU.max))
                v.tensor_tensor(lg[:], lg[:], wide, ALU.subtract).then_inc(ready, 1)
                dve.wait_ge(ex, 1)
                step(v.tensor_reduce(mx[:], lg[:], AX.X, ALU.add))
                step(v.reciprocal(mx[:], mx[:]))
                v.tensor_tensor(lg[:], lg[:], wide, ALU.mult).then_inc(ready, 1)
                for g in range(G4):
                    n = min(4, NB - 4 * g) * B
                    dve.wait_ge(turned, g + 1)
                    v.tensor_copy(wT[:, 4 * B * g:4 * B * g + n], ps[1 + g][0:NEXP, 0:n]).then_inc(copied, 1)

            @block.scalar
            def _(act):
                act.wait_ge(ready, 1)
                nc.scalar.activation(lg[:], lg[:], ACT.Exp).then_inc(ex, 1)

            @block.sync
            def _(sp):
                sp.wait_ge(copied, G4)
                sp.dma_start(dram.gate[:, :], wT[:]).then_inc(stored, 16)
                sp.wait_ge(stored, 16)


def fold(nc, c, w):
    with Scope(nc, "fold") as s:
        sd, own = s.sem("bn_sd"), s.sem("bn_steps")
        with nc.Block() as block:
            @block.scalar
            def _(act):
                act.wait_ge(w.loaded, w.total)
                act.wait_ge(own, 1)
                for i in range(2):
                    nc.scalar.activation(w.bn[:, i, 4], w.bn[:, i, 4], ACT.Sqrt, bias=c.eps3[:, 0:1]).then_inc(sd, 1)

            @block.vector
            def _(dve):
                v = nc.vector
                step = Steps(dve, own)
                step(v.memset(c.eps3[:], 1e-3))
                dve.wait_ge(sd, 2)
                for i in range(2):
                    b, g, be, m, sv = (w.bn[:, i, k] for k in range(5))
                    step(v.reciprocal(sv, sv))
                    step(v.tensor_tensor(w.scale[:, i], g, sv, ALU.mult))
                    step(v.tensor_tensor(b, b, m, ALU.subtract))
                    step(v.tensor_tensor(b, b, w.scale[:, i], ALU.mult))
                    step(v.tensor_tensor(w.shift[:, i], b, be, ALU.add))


def experts(nc, c, w, dram):
    with Scope(nc, "experts") as s:
        gb = [s.sb(f"gb{e}", [P, T]) for e in range(NEXP)]
        gT = s.sb("gT", [NEXP, NP])
        h1 = s.sb("h1", [P, 2, KH, T])
        h2 = s.sb("h2", [P, 2, KH, T])
        hw = s.sb("hw", [P, 2, KH, T])
        ps = c.ps
        gb_in = [s.sem(f"gb_in{e}") for e in range(NEXP)]
        gt_in = s.sem("gt_in")
        l1, l2, lo = s.sem("e_l1"), s.sem("e_l2"), s.sem("e_out")
        a1, a2, dw, dx = s.sem("e_relu1"), s.sem("e_relu2"), s.sem("e_weighted"), s.sem("e_added")
        K = NEXP
        with nc.Block() as block:
            @block.sync
            def _(sp):
                sp.dma_start(gT[:], dram.gate[:, :]).then_inc(gt_in, 16)
                for e in range(K):
                    sp.dma_start(gb[e][:], dram.gate[e, 0:T].partition_broadcast(P)).then_inc(gb_in[e], 16)
                with sp.Fori(1, NT) as t:
                    for e in range(K):
                        sp.wait_ge(dw, K * (t - 1) + e + 1)
                        sp.dma_start(gb[e][:], dram.gate[e, cols(t)].partition_broadcast(P)).then_inc(gb_in[e], 16)

            @block.tensor
            def _(pe):
                pe.wait_ge(w.loaded, w.total)
                pe.wait_ge(gt_in, 16)
                pe.wait_ge(dx, 1)
                with pe.Fori(0, NT) as t:
                    tile = [c.yn[:, k, cols(t)] for k in range(KH)]

                    def first(e):
                        pe.wait_ge(a1, K * t + e + 1)
                        for h in range(KH):
                            ins = product(nc, ps[2 * (e % 2) + h][:, 0:T], [w.W1[:, e, k, half(h)] for k in range(KH)], tile)
                        ins.then_inc(l1, 1)

                    def second(e):
                        pe.wait_ge(a1, K * t + e + 3)
                        pe.wait_ge(a2, K * t + e + 2)
                        for h in range(KH):
                            ins = product(nc, ps[4 + h][:, 0:T], [w.W2[:, e, k, half(h)] for k in range(KH)], [h1[:, e % 2, k, :] for k in range(KH)])
                        ins.then_inc(l2, 1)

                    def last(e):
                        if e == 0:
                            pe.wait_ge(dx, KH * t + 1)
                            for h in range(KH):
                                nc.tensor.matmul(ps[6 + h][:, 0:T], w.bo[:, half(h)], gT[:, cols(t)], start=True, stop=False)
                        pe.wait_ge(dw, K * t + e + 1)
                        for h in range(KH):
                            for k in range(KH):
                                ins = nc.tensor.matmul(ps[6 + h][:, 0:T], w.Wo[:, e, k, half(h)], hw[:, e % 2, k, :],
                                                       start=False, stop=(e == K - 1 and k == KH - 1))
                        ins.then_inc(lo, 1)

                    for e in range(K + 3):
                        if e < K:
                            first(e)
                        if 1 <= e <= K:
                            second(e - 1)
                        if e >= 3:
                            last(e - 3)

            @block.scalar
            def _(act):
                a = nc.scalar.activation
                act.sem_inc(a1, 2)
                act.sem_inc(a2, 2)
                with act.Fori(0, NT) as t:
                    for e in range(K + 1):
                        if e < K:
                            act.wait_ge(l1, K * t + e + 1)
                            if e >= 2:
                                act.wait_ge(l2, K * t + e - 1)
                            for h in range(KH):
                                ins = a(h1[:, e % 2, h, :], ps[2 * (e % 2) + h][:, 0:T], ACT.Relu,
                                        bias=w.shift[:, 0, h, e:e + 1], scale=w.scale[:, 0, h, e:e + 1])
                            ins.then_inc(a1, 1)
                        if e >= 1:
                            f = e - 1
                            act.wait_ge(l2, K * t + f + 1)
                            if f >= 2:
                                act.wait_ge(dw, K * t + f - 1)
                            for h in range(KH):
                                ins = a(h2[:, f % 2, h, :], ps[4 + h][:, 0:T], ACT.Relu,
                                        bias=w.shift[:, 1, h, f:f + 1], scale=w.scale[:, 1, h, f:f + 1])
                            ins.then_inc(a2, 1)

            @block.vector
            def _(dve):
                v = nc.vector
                dve.sem_inc(dx, 1)
                with dve.Fori(0, NT) as t:
                    for e in range(K):
                        dve.wait_ge(gb_in[e], 16 * (t + 1))
                        dve.wait_ge(a2, K * t + e + 3)
                        if e >= 2:
                            dve.wait_ge(lo, K * t + e - 1)
                        v.tensor_tensor(hw[:, e % 2], h2[:, e % 2], gb[e][:].unsqueeze(1).to_broadcast([P, KH, T]), ALU.mult).then_inc(dw, 1)
                    dve.wait_ge(lo, K * t + K)
                    for h in range(KH):
                        v.tensor_tensor(c.xT[:, h, cols(t)], c.xT[:, h, cols(t)], ps[6 + h][:, 0:T], ALU.add).then_inc(dx, 1)


def adjacency(nc, c, dram):
    with Scope(nc, "adjacency") as s:
        krow = s.sb("krow", [B, 2, WE])
        junk = s.sb("junk", [B, 2, 2, WE], BF16)
        cnt = s.sb("cnt_", [B, EC])
        bef = s.sb("bef", [B, EC])
        idx = s.sb("idx", [B, EC], I32)
        t = s.sb("cell", [B, EC])
        val = s.sb("val", [B, EC], F16)
        k_in = [s.sem(f"krow_in{b}") for b in range(2)]
        counted, own, ready, added = s.sem("counted"), s.sem("adj_steps"), s.sem("adj_ready"), s.sem("adj_added")
        with nc.Block() as block:
            @block.sync
            def _(sp):
                def load(w, b):
                    sp.dma_start(krow[:, b, :], dram.keys[bass.ds(w * WE, WE)].partition_broadcast(B)).then_inc(k_in[b], 16)

                load(0, 0)
                load(1, 1)
                with sp.Fori(0, NW // 2 - 1) as i:
                    for b in range(2):
                        sp.wait_ge(counted, 8 * i + 4 * b + 6)
                        load(2 * i + 2 + b, b)

            @block.vector
            def _(dve):
                v = nc.vector
                step = Steps(dve, own)
                dve.sem_inc(counted, 2)
                with dve.Fori(0, NW // 2) as i:
                    for b in range(2):
                        dve.wait_ge(k_in[b], 16 * i + 16)
                        for j in range(WC):
                            at = bass.ds(2 * WC * i + WC * b + j, 1)
                            m = (j + 1) * B
                            dve.wait_ge(counted, 2 * WC * i + WC * b + j + 1)
                            v.tensor_scalar(junk[:, j % 2, 0, :], krow[:, b, :], c.key_c[:, at], None, ALU.is_equal, ALU.add, accum_out=cnt[:, at])
                            v.scalar_tensor_tensor(junk[:, j % 2, 1, 0:m], krow[:, b, 0:m], c.key_c[:, at], c.before[:, WE - m:WE],
                                                   ALU.is_equal, ALU.mult, accum_out=bef[:, at]).then_inc(counted, 1)
                dve.wait_ge(counted, EC + 2)
                step(v.tensor_scalar(bef[:], bef[:], 0.0, None, ALU.is_gt))
                chunks = lambda a: a.rearrange("p (w j) -> p w j", j=WC)
                step(v.tensor_tensor(chunks(t[:]), chunks(c.key_c[:]), c.spare_f[0:B, :].unsqueeze(1).to_broadcast([B, NW, WC]), ALU.subtract))
                step(v.tensor_tensor(t[:], t[:], bef[:], ALU.mult))
                step(v.tensor_tensor(t[:], c.key_c[:], t[:], ALU.subtract))
                step(v.tensor_copy(idx[:], t[:]))
                step(v.tensor_scalar(bef[:], bef[:], -1.0, 1.0, ALU.mult, ALU.add))
                v.tensor_tensor(val[:], cnt[:], bef[:], ALU.mult).then_inc(ready, 1)

            @block.gpsimd
            def _(pool):
                pool.wait_ge(ready, 1)
                for w in range(NW):
                    for j in range(WC):
                        k = WC * w + j
                        nc.gpsimd.indirect_dma_start(dram.adj_flat, bass.IndirectOffsetOnAxis(ap=idx[:, k:k + 1], axis=0),
                                                     val[:, k:k + 1], None, compute_op=ALU.add).then_inc(added, 16)
                    pool.wait_ge(added, 16 * WC * (w + 1))


def mix1(nc, c, w, qT, ctx):
    NQ = NT
    with Scope(nc, "mix1") as s:
        sq = s.sb("sq", [P, 2, KH, T])
        rr = s.sb("rr", [P, 2, T])
        kT = s.sb("kT", [P, NP])
        et = s.sb("et", [B, NB, P])
        vt = s.sb("vt", [B, NB, P])
        qt = s.sb("qt", [B, NB, P])
        mx8 = s.sb("mx8", [P, NT + 1])
        nmx = s.sb("nmx", [P, 1])
        sums = s.sb("sums", [P, 2])
        km = s.sb("km", [P, MEM])
        memT = s.sb("memT", [MEM, 2, P])
        qm = s.sb("qm", [B, NB * HEADS1])
        g16 = s.sb("g16", [P, KH])
        ps = c.ps
        at = lambda t: slice(t * T, (t + 1) * T)
        tok = lambda j: slice(B * j, B * (j + 1))
        own = s.sem("m1_steps")
        ss_done, sq_ready, sd_ready, xr_ready = s.sem("ss_done"), s.sem("m_sq"), s.sem("m_sd"), s.sem("xr_ready")
        k_done, k_out, qv_done, q_out, v_out = s.sem("k_done"), s.sem("k_out"), s.sem("qv_done"), s.sem("q_out"), s.sem("v_out")
        mx_ready, e_ready, et_turned, et_out = s.sem("mx_ready"), s.sem("e_ready"), s.sem("et_turned"), s.sem("et_out")
        q_ready, q_exp, q_norm, q_turned, qT_out = s.sem("q_ready"), s.sem("q_exp"), s.sem("q_norm"), s.sem("q_turned"), s.sem("qT_out")
        mem_turned, mem_out, ctx_done, ctx_ready = s.sem("mem_turned"), s.sem("mem_out"), s.sem("ctx_done"), s.sem("ctx_ready")
        w_ready = s.sem("w_ready")
        G4 = -(-NB // 4)
        with nc.Block() as block:
            @block.scalar
            def _(act):
                a = nc.scalar.activation
                for t in range(NT + 1):
                    if t < NT:
                        if t >= 2:
                            act.wait_ge(ss_done, t - 1)
                        a(sq[:, t % 2], c.yn[:, :, at(t)], ACT.Square).then_inc(sq_ready, 1)
                    if t >= 1:
                        act.wait_ge(ss_done, t)
                        if t >= 3:
                            act.wait_ge(xr_ready, t - 2)
                        a(rr[:, (t - 1) % 2], ps[(t - 1) % 2][:, 0:T], ACT.Sqrt).then_inc(sd_ready, 1)
                for j in range(NB):
                    act.wait_ge(qv_done, j + 1)
                    nc.scalar.copy(vt[:, j, :], ps[6 + j % 2][0:B, 0:P]).then_inc(v_out, 1)
                act.wait_ge(mx_ready, 1)
                a(kT[:, 0:N], kT[:, 0:N], ACT.Exp, bias=nmx[:, 0:1], accum_out=sums[:, 0:1]).then_inc(e_ready, 1)
                a(km[:], w.mk[:], ACT.Exp, bias=nmx[:, 0:1], accum_out=sums[:, 1:2]).then_inc(e_ready, 1)
                act.wait_ge(q_ready, 1)
                a(qt[:], qt[:], ACT.Exp).then_inc(q_exp, 1)
                for g in range(G4):
                    n = min(4, NB - 4 * g)
                    act.wait_ge(et_turned, g + 1)
                    nc.scalar.copy(et[:, 4 * g:4 * g + n, :], ps[g % 2][0:B, 0:n * P].rearrange("p (j d) -> p j d", d=P)).then_inc(et_out, 1)

            @block.vector
            def _(dve):
                v = nc.vector
                step = Steps(dve, own)
                dve.wait_ge(w.loaded, w.total)
                step(v.tensor_scalar(g16[:], w.gpre[:], float(D) ** 0.5, None, ALU.mult))
                for k in range(KH):
                    ins = v.tensor_scalar(w.mqkv[:, k, :], w.mqkv[:, k, :], g16[:, k:k + 1], None, ALU.mult)
                ins.then_inc(w_ready, 1)
                for t in range(NT):
                    r = rr[:, t % 2]
                    dve.wait_ge(sd_ready, t + 1)
                    step(v.tensor_scalar(r, r, 1e-12, None, ALU.max))
                    step(v.reciprocal(r, r))
                    v.tensor_tensor(c.a[:, 0, at(t)], c.yn[:, 0, at(t)], r, ALU.mult)
                    v.tensor_tensor(c.a[:, 1, at(t)], c.yn[:, 1, at(t)], r, ALU.mult).then_inc(xr_ready, 1)
                for t in range(NT):
                    dve.wait_ge(k_done, t + 1)
                    n = min(T, N - t * T)
                    v.tensor_copy(kT[:, at(t)], ps[2 + t % 2][:, 0:T])
                    v.tensor_reduce(mx8[:, t:t + 1], ps[2 + t % 2][:, 0:n], AX.X, ALU.max).then_inc(k_out, 1)
                for j in range(NB):
                    dve.wait_ge(qv_done, j + 1)
                    v.tensor_copy(qt[:, j, :], ps[4 + j % 2][0:B, 0:P]).then_inc(q_out, 1)
                v.tensor_reduce(mx8[:, NT:NT + 1], w.mk[:], AX.X, ALU.max).then_inc(k_out, 1)
                dve.wait_ge(k_out, NT + 1)
                step(v.tensor_reduce(nmx[:], mx8[:], AX.X, ALU.max))
                v.tensor_scalar(nmx[:], nmx[:], -1.0, None, ALU.mult).then_inc(mx_ready, 1)
                q3 = qt[:].rearrange("p j (h d) -> p (j h) d", d=HD1)
                wide = qm[:].unsqueeze(2).to_broadcast([B, NB * HEADS1, HD1])
                dve.wait_ge(q_out, NB)
                step(v.tensor_reduce(qm[:], q3, AX.X, ALU.max))
                v.tensor_tensor(q3, q3, wide, ALU.subtract).then_inc(q_ready, 1)
                dve.wait_ge(q_exp, 1)
                step(v.tensor_reduce(qm[:], q3, AX.X, ALU.add))
                step(v.reciprocal(qm[:], qm[:]))
                step(v.tensor_scalar(qm[:], qm[:], HD1 ** -0.5, None, ALU.mult))
                v.tensor_tensor(q3, q3, wide, ALU.mult).then_inc(q_norm, 1)
                step(v.memset(qT[:, N:NP], 0.0))
                step(v.memset(ctx[:], 0.0))
                dve.wait_ge(mem_turned, 1)
                v.tensor_copy(memT[:, 0, :], ps[2][0:MEM, 0:P])
                v.tensor_copy(memT[:, 1, :], ps[2][0:MEM, P:2 * P]).then_inc(mem_out, 1)
                for g in range(G4):
                    n = min(4, NB - 4 * g) * B
                    dve.wait_ge(q_turned, g + 1)
                    v.tensor_copy(qT[:, 4 * B * g:4 * B * g + n], ps[4 + g % 2][:, 0:n]).then_inc(qT_out, 1)
                dve.wait_ge(e_ready, 2)
                step(v.tensor_tensor(sums[:, 0:1], sums[:, 0:1], sums[:, 1:2], ALU.add))
                step(v.reciprocal(sums[:, 0:1], sums[:, 0:1]))
                dve.wait_ge(ctx_done, 1)
                for h in range(HEADS1):
                    r = slice(h * HD1, (h + 1) * HD1)
                    ins = v.tensor_scalar(ctx[r, r], ps[3][r, r], sums[r, 0:1], None, ALU.mult)
                ins.then_inc(ctx_ready, 1)

            @block.tensor
            def _(pe):
                mm = nc.tensor.matmul
                for t in range(NT):
                    pe.wait_ge(sq_ready, t + 1)
                    if t >= 2:
                        pe.wait_ge(sd_ready, t - 1)
                    product(nc, ps[t % 2][:, 0:T], [c.ones[:]] * KH, [sq[:, t % 2, k, :] for k in range(KH)]).then_inc(ss_done, 1)
                pe.wait_ge(w_ready, 1)
                H = HEADS1 * HD1
                for t in range(NT):
                    pe.wait_ge(xr_ready, t + 1)
                    if t >= 2:
                        pe.wait_ge(k_out, t - 1)
                    product(nc, ps[2 + t % 2][:, 0:T], [w.mqkv[:, k, H:2 * H] for k in range(KH)], [c.a[:, k, at(t)] for k in range(KH)]).then_inc(k_done, 1)
                for j in range(NB):
                    if j >= 2:
                        pe.wait_ge(q_out, j - 1)
                        pe.wait_ge(v_out, j - 1)
                    product(nc, ps[4 + j % 2][0:B, 0:P], [c.a[:, k, tok(j)] for k in range(KH)], [w.mqkv[:, k, 0:H] for k in range(KH)])
                    product(nc, ps[6 + j % 2][0:B, 0:P], [c.a[:, k, tok(j)] for k in range(KH)], [w.mqkv[:, k, 2 * H:3 * H] for k in range(KH)]).then_inc(qv_done, 1)
                pe.wait_ge(e_ready, 2)
                pe.wait_ge(k_out, NT)
                nc.tensor.transpose(ps[2][0:MEM, 0:P], km[:], c.ident[:])
                nc.tensor.transpose(ps[2][0:MEM, P:2 * P], w.mv[:], c.ident[:]).then_inc(mem_turned, 1)
                pe.wait_ge(sd_ready, NT)
                for g in range(G4):
                    n = min(4, NB - 4 * g)
                    if g >= 2:
                        pe.wait_ge(et_out, g - 1)
                    for i in range(n):
                        ins = nc.tensor.transpose(ps[g % 2][0:B, P * i:P * (i + 1)], kT[:, tok(4 * g + i)], c.ident[:])
                    ins.then_inc(et_turned, 1)
                pe.wait_ge(q_norm, 1)
                pe.wait_ge(q_out, NB)
                pe.wait_ge(v_out, NB)
                for g in range(G4):
                    n = min(4, NB - 4 * g)
                    if g >= 2:
                        pe.wait_ge(qT_out, g - 1)
                    for i in range(n):
                        ins = nc.tensor.transpose(ps[4 + g % 2][:, B * i:B * (i + 1)], qt[:, 4 * g + i, :], c.ident[0:B, 0:B])
                    ins.then_inc(q_turned, 1)
                pe.wait_ge(et_out, G4)
                pe.wait_ge(mem_out, 1)
                for j in range(NB):
                    mm(ps[3][:, 0:P], et[:, j, :], vt[:, j, :], start=(j == 0), stop=False)
                mm(ps[3][:, 0:P], memT[:, 0, :], memT[:, 1, :], start=False, stop=True).then_inc(ctx_done, 1)
                pe.wait_ge(ctx_ready, 1)
                pe.wait_ge(qT_out, G4)


def mix1_out(nc, c, w, qT, ctx):
    with Scope(nc, "mix1_out") as s:
        sq = s.sb("sq", [P, KH, T])
        rr = s.sb("rr", [P, T])
        yo = s.sb("yo", [P, KH, T])
        oT = s.sb("oT", [P, T])
        g16 = s.sb("g16", [P, KH])
        ps = c.ps
        own, pe_s, act_s = s.sem("mo_steps"), s.sem("mo_pe"), s.sem("mo_act")
        PE_N, ACT_N, DVE_N = 3, 2, 10
        with nc.Block() as block:
            @block.tensor
            def _(pe):
                with pe.Fori(0, NT) as t:
                    pe.wait_ge(own, DVE_N * t + 1)
                    product(nc, ps[4][:, 0:T], [ctx[:]], [qT[:, cols(t)]]).then_inc(pe_s, 1)
                    pe.wait_ge(own, DVE_N * t + 2)
                    for h in range(KH):
                        ins = product(nc, ps[h][:, 0:T], [w.wout[:, half(h)]], [oT[:]])
                    ins.then_inc(pe_s, 1)
                    pe.wait_ge(act_s, ACT_N * t + 1)
                    product(nc, ps[6][:, 0:T], [c.ones[:]] * KH, [sq[:, k, :] for k in range(KH)]).then_inc(pe_s, 1)

            @block.scalar
            def _(act):
                with act.Fori(0, NT) as t:
                    act.wait_ge(own, DVE_N * t + 4)
                    nc.scalar.activation(sq[:], yo[:], ACT.Square).then_inc(act_s, 1)
                    act.wait_ge(pe_s, PE_N * t + 3)
                    nc.scalar.activation(rr[:], ps[6][:, 0:T], ACT.Sqrt).then_inc(act_s, 1)

            @block.vector
            def _(dve):
                v = nc.vector
                step = Steps(dve, own)
                step(v.tensor_scalar(g16[:], w.gout[:], float(D) ** 0.5, None, ALU.mult))
                with dve.Fori(0, NT) as t:
                    step.turn(t, DVE_N)
                    step.n = 1
                    dve.wait_ge(pe_s, PE_N * t + 1)
                    step(v.tensor_copy(oT[:], ps[4][:, 0:T]))
                    dve.wait_ge(pe_s, PE_N * t + 2)
                    for h in range(KH):
                        step(v.tensor_scalar(yo[:, h, :], ps[h][:, 0:T], w.bout[:, h:h + 1], None, ALU.add))
                    dve.wait_ge(act_s, ACT_N * t + 2)
                    step(v.tensor_scalar(rr[:], rr[:], 1e-12, None, ALU.max))
                    step(v.reciprocal(rr[:], rr[:]))
                    for h in range(KH):
                        step(v.scalar_tensor_tensor(yo[:, h, :], yo[:, h, :], g16[:, h:h + 1], rr[:], ALU.mult, ALU.mult))
                    for h in range(KH):
                        step(v.tensor_tensor(yo[:, h, :], yo[:, h, :], c.yn[:, h, cols(t)], ALU.add))
                    step(v.tensor_tensor(c.xT[:, :, cols(t)], c.xT[:, :, cols(t)], yo[:], ALU.add))


def sage(nc, c, w, dram, src, out, layer):
    SG = 5
    JG = NB // SG
    with Scope(nc, f"sage{layer}") as s:
        zh = s.sb("zh", [B, NB, D], F16)
        zl = s.sb("zl", [B, NB, D], F16)
        adj = [s.sb(f"adj{g}", [B, JG, T], F16) for g in range(SG)]
        rd = s.sb("rd", [P, NP])
        u = s.sb("u", [P, KH, T])
        ps = c.ps
        z_done, zh_out, zl_out = s.sem("z_done"), s.sem("zh_out"), s.sem("zl_out")
        adj_in = [s.sem(f"adj_in{g}") for g in range(SG)]
        adj_used, rd_in = s.sem("adj_used"), s.sem("rd_in")
        summed, own_done, own = s.sem("summed"), s.sem("self_done"), s.sem("sage_steps")
        Wl, Wr, bl = w.gl[:, layer], w.gr[:, layer], w.gb[:, layer]
        DVE_N = 8
        with nc.Block() as block:
            @block.sync
            def _(sp):
                sp.wait_ge(own, 1)
                sp.dma_start(rd[:, 0:N], dram.rdeg[0:N].partition_broadcast(P)).then_inc(rd_in, 16)

                def load(t, g):
                    rows = dram.adj[B * JG * g:B * JG * (g + 1), cols(t)]
                    sp.dma_start(adj[g][:], rows.rearrange("(j p) d -> p j d", p=B)).then_inc(adj_in[g], 16)

                for g in range(SG):
                    load(0, g)
                with sp.Fori(1, NT) as t:
                    for g in range(SG):
                        sp.wait_ge(adj_used, SG * (t - 1) + g + 1)
                        load(t, g)

            @block.tensor
            def _(pe):
                mm = nc.tensor.matmul
                for j in range(NB):
                    if j >= 4:
                        pe.wait_ge(zl_out, j - 3)
                    product(nc, ps[j % 4][0:B, 0:D], [src[:, k, B * j:B * (j + 1)] for k in range(KH)],
                            [Wl[:, k, :] for k in range(KH)]).then_inc(z_done, 1)
                pe.wait_ge(zl_out, NB)
                with pe.Fori(0, NT) as t:
                    pe.wait_ge(own, DVE_N * t + 1)
                    for g in range(SG):
                        pe.wait_ge(adj_in[g], 16 * t + 16)
                        for j in range(JG):
                            for h in range(KH):
                                for z in (zh, zl):
                                    ins = mm(ps[4 + h][:, 0:T], z[:, g * JG + j, half(h)], adj[g][:, j, :],
                                             start=(g == 0 and j == 0 and z is zh), stop=(g == SG - 1 and j == JG - 1 and z is zl))
                        ins.then_inc(adj_used, 1)
                    for h in range(KH):
                        ins = product(nc, ps[6 + h][:, 0:T], [Wr[:, k, half(h)] for k in range(KH)], [src[:, k, cols(t)] for k in range(KH)])
                    ins.then_inc(own_done, 1)

            @block.scalar
            def _(act):
                for j in range(NB):
                    act.wait_ge(z_done, j + 1)
                    nc.scalar.copy(zh[:, j, :], ps[j % 4][0:B, 0:D]).then_inc(zh_out, 1)

            @block.vector
            def _(dve):
                v = nc.vector
                step = Steps(dve, own)
                step(v.memset(rd[:, N:NP], 0.0))
                for j in range(NB):
                    dve.wait_ge(zh_out, j + 1)
                    v.tensor_tensor(zl[:, j, :], ps[j % 4][0:B, 0:D], zh[:, j, :], ALU.subtract).then_inc(zl_out, 1)
                dve.wait_ge(rd_in, 16)
                with dve.Fori(0, NT) as t:
                    step.turn(t, DVE_N)
                    step.n = 1
                    at = cols(t)
                    dve.wait_ge(adj_used, SG * t + SG)
                    for h in range(KH):
                        step(v.tensor_tensor(u[:, h, :], ps[4 + h][:, 0:T], rd[:, at], ALU.mult))
                    dve.wait_ge(own_done, t + 1)
                    for h in range(KH):
                        step(v.scalar_tensor_tensor(u[:, h, :], ps[6 + h][:, 0:T], bl[:, h:h + 1], u[:, h, :], ALU.add, ALU.add))
                    for h in range(KH):
                        if layer < 2:
                            step(v.tensor_scalar(out[:, h, at], u[:, h, :], 0.0, None, ALU.max))
                        else:
                            step(v.tensor_tensor(out[:, h, at], out[:, h, at], u[:, h, :], ALU.add))
                    for h in range(2):
                        dve.sem_inc(own, 1)


def ffn1(nc, c, w, dram, out):
    M1 = HID1 // P
    with Scope(nc, "ffn1") as s:
        wrow = s.sb("wrow", [P, NP])
        sel = s.sb("sel", [P, NP])
        wc = s.sb("wc", [B, NB])
        rank = s.sb("rank", [B, 3, NB])
        junk = s.sb("junk", [B, 2, N], BF16)
        tie = s.sb("tie", [B, 2, B], BF16)
        ranked = s.sem("ranked")
        sT = s.sb("sT", [NB, B])
        hid = s.sb("hid", [P, M1, T])
        wrep = s.sb("wrep", [P, KH, P])
        ob = s.sb("ob", [B, 4, D])
        ps = c.ps
        own, sc_done, sc_out, wc_done, sel_done, sT_out, sel_st, sel_in = (s.sem(n) for n in (
            "f_steps", "sc_done", "sc_out", "wc_done", "sel_done", "sT_out", "sel_stored", "sel_in"))
        rep, f1, g1, f2, y_out, fin = (s.sem(n) for n in ("wrep_ready", "f_fc1", "f_gelu", "f_fc2", "y_out", "x_final"))
        turned, copied = s.sem("o_turned"), s.sem("o_copied")
        stored = [s.sem(f"o_stored{k}") for k in range(4)]
        at = lambda t: slice(t * T, (t + 1) * T)
        with nc.Block() as block:
            @block.tensor
            def _(pe):
                mm = nc.tensor.matmul
                pe.wait_ge(rep, 1)
                for t in range(NT):
                    if t >= 4:
                        pe.wait_ge(sc_out, t - 3)
                    product(nc, ps[t % 4][:, 0:T], [wrep[:, k, :] for k in range(KH)], [c.yn[:, k, at(t)] for k in range(KH)]).then_inc(sc_done, 1)
                pe.wait_ge(sc_out, NT)
                for j in range(NB):
                    ins = nc.tensor.transpose(ps[4][0:B, j:j + 1], wrow[0:1, B * j:B * (j + 1)], c.ident[0:1, 0:1])
                ins.then_inc(wc_done, 1)
                pe.wait_ge(own, 1)
                with pe.Fori(0, NT) as t:
                    tile = [c.yn[:, k, cols(t)] for k in range(KH)]
                    pe.wait_ge(y_out, KH * t + 1)

                    def up(m):
                        pe.wait_ge(g1, M1 * t + m + 1)
                        product(nc, ps[m % 6][:, 0:T], [w.w1[:, k, m * P:(m + 1) * P] for k in range(KH)], tile).then_inc(f1, 1)

                    def down(m):
                        pe.wait_ge(g1, M1 * t + m + 7)
                        for h in range(KH):
                            ins = mm(ps[6 + h][:, 0:T], w.w2[:, m, half(h)], hid[:, m, :], start=(m == 0), stop=(m == M1 - 1))
                        ins.then_inc(f2, 1)

                    for m in range(M1 + 2):
                        if m < M1:
                            up(m)
                        if m >= 2:
                            down(m - 2)
                pe.wait_ge(sel_done, 1)
                pe.wait_ge(y_out, KH * NT + 1)
                nc.tensor.transpose(ps[5][0:NB, 0:B], rank[:, 0, :], c.ident[0:B, 0:B]).then_inc(wc_done, 1)
                for j in range(NB):
                    pe.wait_ge(fin, min(NT, (B * (j + 1) - 1) // T + 1))
                    if j >= 4:
                        pe.wait_ge(copied, j - 3)
                    for h in range(KH):
                        ins = nc.tensor.transpose(ps[j % 4][0:B, half(h)], c.xT[:, h, B * j:B * (j + 1)], c.ident[:])
                    ins.then_inc(turned, 1)

            @block.scalar
            def _(act):
                act.sem_inc(g1, 6)
                with act.Fori(0, NT) as t:
                    act.wait_ge(f2, M1 * t + 1)
                    for m in range(M1):
                        act.wait_ge(f1, M1 * t + m + 1)
                        nc.scalar.activation(hid[:, m, :], ps[m % 6][:, 0:T], ACT.Gelu_apprx_tanh, bias=w.b1f[:, m:m + 1]).then_inc(g1, 1)
                    act.wait_ge(f2, M1 * t + M1 + 1)
                    for h in range(KH):
                        nc.scalar.activation(c.a[:, h, cols(t)], ps[6 + h][:, 0:T], ACT.Identity, bias=w.b2f[:, h:h + 1]).then_inc(y_out, 1)

            @block.sync
            def _(sp):
                sp.wait_ge(sT_out, 1)
                sp.dma_start(dram.sel.rearrange("(a p) -> a p", p=B), sT[:]).then_inc(sel_st, 16)
                sp.wait_ge(sel_st, 16)
                sp.dma_start(sel[:, 0:N], dram.sel.partition_broadcast(P)).then_inc(sel_in, 16)
                for j in range(NB):
                    sp.wait_ge(copied, j + 1)
                    sp.dma_start(out[B * j:B * (j + 1), :], ob[:, j % 4, :]).then_inc(stored[j % 4], 16)
                for k in range(4):
                    sp.wait_ge(stored[k], 16 * len(range(k, NB, 4)))

            @block.vector
            def _(dve):
                v = nc.vector
                step = Steps(dve, own)
                dve.sem_inc(f2, 1)
                dve.sem_inc(y_out, 1)
                v.memset(sel[:, N:NP], 0.0)
                dve.wait_ge(w.loaded, w.total)
                v.tensor_copy(wrep[:], w.wr1[:].to_broadcast([P, KH, P])).then_inc(rep, 1)
                for t in range(NT):
                    dve.wait_ge(sc_done, t + 1)
                    v.tensor_scalar(wrow[:, at(t)], ps[t % 4][:, 0:T], w.br1[:, 0:1], None, ALU.add).then_inc(sc_out, 1)
                dve.wait_ge(wc_done, 1)
                step(v.tensor_copy(wc[:], ps[4][0:B, 0:NB]))
                dve.wait_ge(sc_out, NT)
                step(v.memset(rank[:], 0.0))
                for j in range(NB):
                    me = wc[:, j:j + 1]
                    lo = B * j
                    if j >= 2:
                        dve.wait_ge(ranked, j - 1)
                    if j:
                        v.tensor_scalar(junk[:, j % 2, 0:lo], wrow[0:B, 0:lo], me, None, ALU.is_ge, ALU.add, accum_out=rank[:, 0, j:j + 1])
                    v.scalar_tensor_tensor(tie[:, j % 2, :], wrow[0:B, lo:lo + B], me, c.before[:, WE - B:WE], ALU.is_equal, ALU.mult, accum_out=rank[:, 1, j:j + 1])
                    v.tensor_scalar(junk[:, j % 2, lo:N], wrow[0:B, lo:N], me, None, ALU.is_gt, ALU.add, accum_out=rank[:, 2, j:j + 1]).then_inc(ranked, 1)
                dve.wait_ge(ranked, NB)
                step(v.tensor_tensor(rank[:, 0], rank[:, 0], rank[:, 1], ALU.add))
                step(v.tensor_tensor(rank[:, 0], rank[:, 0], rank[:, 2], ALU.add))
                v.tensor_scalar(rank[:, 0], rank[:, 0], float(TOPK), None, ALU.is_lt).then_inc(sel_done, 1)
                dve.wait_ge(wc_done, 2)
                v.tensor_copy(sT[:], ps[5][0:NB, 0:B]).then_inc(sT_out, 1)
                dve.wait_ge(sel_in, 16)
                step(v.tensor_tensor(sel[:], sel[:], wrow[:], ALU.mult))
                dve.wait_ge(y_out, KH * NT + 1)
                for t in range(NT):
                    for h in range(KH):
                        ins = v.tensor_tensor(c.a[:, h, at(t)], c.a[:, h, at(t)], sel[:, at(t)], ALU.mult)
                    step(v.tensor_tensor(c.xT[:, :, at(t)], c.xT[:, :, at(t)], c.yn[:, :, at(t)], ALU.add))
                    v.tensor_tensor(c.xT[:, :, at(t)], c.xT[:, :, at(t)], c.a[:, :, at(t)], ALU.add).then_inc(fin, 1)
                for j in range(NB):
                    dve.wait_ge(turned, j + 1)
                    if j >= 4:
                        dve.wait_ge(stored[j % 4], 16 * (j // 4))
                    v.tensor_copy(ob[:, j % 4, :], ps[j % 4][0:B, 0:D]).then_inc(copied, 1)


class Names:
    pass


def load_weights(nc, s, w, plan):
    with nc.Block() as block:
        @block.sync
        def _(sp):
            with nc.allow_non_contiguous_dma(reason="weights in blocks of 128 rows"):
                for dst, src in plan:
                    sp.dma_start(dst, src).then_inc(w.loaded, 16)
    w.total = 16 * len(plan)


def rows128(a):
    return a.rearrange("(k p) m -> p k m", p=P)


def build(nc, i, out):
    dram = Names()
    internal = lambda name, shape, dt=F32: nc.dram_tensor(name, shape, dt, kind="Internal").ap()
    dram.adj = internal("adjacency", (N + 1, NP), F16)
    dram.adj_flat = dram.adj.rearrange("a (b o) -> (a b) o", o=1)
    dram.rows = internal("b_rows", (N, D))
    dram.runs = internal("run_max", (E, D))
    dram.keys = internal("edge_keys", (E,))
    dram.reset = internal("edge_resets", (E,), BF16)
    dram.rdeg = internal("degree_inverse", (N,))
    dram.gate = internal("gate_rows", (NEXP, NP))
    dram.sel = internal("selected", (N,))
    with Scope(nc, "all") as s:
        c = Names()
        c.ps = [s.enter_context(nc.psum_tensor(f"bank{b}", [P, 512], F32)) for b in range(8)]
        c.spare = s.sb("spare", [P, WC], I32)
        c.spare_f = s.sb("spare_f", [P, WC])
        c.row = s.sb("row", [P, P])
        c.row_b = s.sb("row_b", [B, B], BF16)
        c.ident = s.sb("ident", [P, P])
        c.upto = s.sb("upto", [P, P])
        c.before = s.sb("before", [B, WE], BF16)
        c.ones = s.sb("ones", [P, P])
        c.mean_w = s.sb("mean_w", [P, P])
        c.eps5 = s.sb("eps5", [P, 1])
        c.eps3 = s.sb("eps3", [P, 1])
        c.src_idx = s.sb("src_idx", [B, EC], I32)
        c.key_c = s.sb("key_c", [B, EC])
        c.has = s.sb("has", [B, NB])
        c.lack = s.sb("lack", [B, NB])
        c.last_idx = s.sb("last_idx", [B, NB], I32)
        c.xT = s.sb("xT", [P, KH, NP])
        c.yn = s.sb("yn", [P, KH, NP])
        c.a = s.sb("a", [P, KH, NP])
        c.attT = s.sb("attT", [P, KH, P])
        constants(nc, c)
        edges(nc, c, i.src, i.dst, dram)

        with Scope(nc, "w0") as g:
            w = Names()
            w.loaded = g.sem("w0_loaded")
            w.theta, w.phi = g.sb("theta", [P, KH, D]), g.sb("phi", [P, KH, D])
            w.qkv, w.fc1, w.fc2 = g.sb("qkv", [P, KH, 3 * D]), g.sb("fc1", [P, KH, HID0]), g.sb("fc2", [P, HID0 // P, D])
            w.bqkv_row = g.sb("bqkv_row", [1, 3 * D])
            w.tb, w.pb, w.bq, w.ng, w.nb, w.b2 = (g.sb(n, [P, KH]) for n in ("tb", "pb", "bq", "ng", "nb", "b2"))
            w.b1 = g.sb("b1", [P, HID0 // P])
            load_weights(nc, g, w, [
                (w.theta[:], rows128(i.theta)), (w.phi[:], rows128(i.phi)), (w.qkv[:], rows128(i.qkv)),
                (w.fc1[:], rows128(i.fc1)), (w.fc2[:], rows128(i.fc2)), (w.bqkv_row[:], i.bqkv_row),
                (w.tb[:], i.theta_b), (w.pb[:], i.phi_b), (w.bq[:], i.bqkv[:, 0:KH]), (w.ng[:], i.norm_g),
                (w.nb[:], i.norm_b), (w.b2[:], i.b_fc2), (w.b1[:], i.b_fc1)])
            nodes(nc, c, i.x, dram, w)
            segment_max(nc, c, dram)
            mix0(nc, c, w)
        join_max(nc, c, dram)
        norm(nc, c, c.yn, 1)
        with Scope(nc, "w1") as g:
            w = Names()
            w.loaded = g.sem("w1_loaded")
            w.Wr, w.br, w.bo = g.sb("Wr", [P, KH, NEXP]), g.sb("br", [1, NEXP]), g.sb("bo", [NEXP, D])
            w.W1, w.W2, w.Wo = (g.sb(n, [P, NEXP, KH, D]) for n in ("W1", "W2", "Wo"))
            w.bn = g.sb("bn", [P, 2, 5, KH, NEXP])
            w.scale, w.shift = g.sb("scale", [P, 2, KH, NEXP]), g.sb("shift", [P, 2, KH, NEXP])
            blocks = lambda a: a.rearrange("e (k p) m -> p e k m", p=P)
            load_weights(nc, g, w, [
                (w.Wr[:], rows128(i.Wr)), (w.br[:], i.br), (w.bo[:], i.bo), (w.bn[:], i.bn),
                *((t[:, e], blocks(a)[:, e]) for t, a in ((w.W1, i.W1), (w.W2, i.W2), (w.Wo, i.Wo)) for e in range(NEXP))])
            fold(nc, c, w)
            gate(nc, c, w, dram)
            experts(nc, c, w, dram)
        adjacency(nc, c, dram)
        norm(nc, c, c.yn, 2)
        with Scope(nc, "w2") as g:
            w = Names()
            w.loaded = g.sem("w2_loaded")
            H = HEADS1 * HD1
            w.mqkv, w.wout = g.sb("mqkv", [P, KH, 3 * H]), g.sb("wout", [P, D])
            w.mk, w.mv = g.sb("mk", [P, MEM]), g.sb("mv", [P, MEM])
            w.gpre, w.gout, w.bout = (g.sb(n, [P, KH]) for n in ("gpre", "gout", "bout"))
            load_weights(nc, g, w, [
                (w.mqkv[:], rows128(i.mqkv)), (w.wout[:], i.wout), (w.mk[:], i.mk), (w.mv[:], i.mv),
                (w.gpre[:], i.gpre), (w.gout[:], i.gout), (w.bout[:], i.bout)])
            qT = g.sb("qT", [P, NP])
            ctx = g.sb("ctx", [P, P])
            mix1(nc, c, w, qT, ctx)
            mix1_out(nc, c, w, qT, ctx)
        with Scope(nc, "w3") as g:
            w = Names()
            w.loaded = g.sem("w3_loaded")
            w.gl, w.gr, w.gb = g.sb("gl", [P, 3, KH, D]), g.sb("gr", [P, 3, KH, D]), g.sb("gbias", [P, 3, KH])
            load_weights(nc, g, w, [
                *((t[:, n], rows128(a[n])) for t, a in ((w.gl, i.gl), (w.gr, i.gr)) for n in range(3)), (w.gb[:], i.gb)])
            wait_for(nc, w)
            sage(nc, c, w, dram, c.yn, c.a, 0)
            sage(nc, c, w, dram, c.a, c.a, 1)
            sage(nc, c, w, dram, c.a, c.xT, 2)
        norm(nc, c, c.yn, 3)
        with Scope(nc, "w4") as g:
            w = Names()
            w.loaded = g.sem("w4_loaded")
            w.w1, w.w2 = g.sb("w1", [P, KH, HID1]), g.sb("w2", [P, HID1 // P, D])
            w.b1f, w.b2f = g.sb("b1f", [P, HID1 // P]), g.sb("b2f", [P, KH])
            w.wr1, w.br1 = g.sb("wr1", [P, KH, 1]), g.sb("br1", [P, 1])
            load_weights(nc, g, w, [
                (w.w1[:], rows128(i.w1)), (w.w2[:], rows128(i.w2)), (w.b1f[:], i.b1f), (w.b2f[:], i.b2f),
                (w.wr1[:], rows128(i.wr1)), (w.br1[:], i.br1.partition_broadcast(P))])
            ffn1(nc, c, w, dram, out)


def wait_for(nc, w):
    with nc.Block() as block:
        @block.tensor
        def _(pe):
            pe.wait_ge(w.loaded, w.total)

        @block.vector
        def _(dve):
            dve.wait_ge(w.loaded, w.total)


def kernel(**a):
    import numpy as np
    import concourse.bacc as bacc
    from concourse.bass_utils import run_bass_kernel_spmd as run

    nc = bacc.Bacc("TRN2", target_bir_lowering=False, num_devices=1)
    col = lambda v: v.reshape(-1, P).T
    bn = lambda n: np.stack([a[f"L0_ffn_{k}{n}"].reshape(NEXP, KH, P).transpose(2, 1, 0) for k in ("b", "g", "be", "m", "v")], axis=1)
    laid = {
        "x": a["x"], "src": a["src"], "dst": a["dst"],
        "theta": a["L0_gnn_theta_w"].T, "phi": a["L0_gnn_phi_w"].T,
        "theta_b": col(a["L0_gnn_theta_b"]), "phi_b": col(a["L0_gnn_phi_b"]),
        "qkv": a["L0_mix_w_qkv"], "bqkv": col(a["L0_mix_b_qkv"]), "bqkv_row": a["L0_mix_b_qkv"][None],
        "norm_g": col(a["L0_mix_norm_g"]), "norm_b": col(a["L0_mix_norm_b"]),
        "fc1": a["L0_mix_w_fc1"], "b_fc1": col(a["L0_mix_b_fc1"]), "fc2": a["L0_mix_w_fc2"], "b_fc2": col(a["L0_mix_b_fc2"]),
        "Wr": a["L0_ffn_Wr"], "br": a["L0_ffn_br"][None], "bo": a["L0_ffn_bo"],
        "W1": a["L0_ffn_W1"], "W2": a["L0_ffn_W2"], "Wo": a["L0_ffn_Wo"], "bn": np.stack([bn(1), bn(2)], axis=1),
        "gl": np.stack([a[f"L1_gnn_W{n}l"].T for n in (1, 2, 3)]), "gr": np.stack([a[f"L1_gnn_W{n}r"].T for n in (1, 2, 3)]),
        "gb": np.stack([col(a[f"L1_gnn_b{n}l"]) for n in (1, 2, 3)], axis=1),
        "mqkv": a["L1_mix_w_qkv"], "wout": a["L1_mix_w_out"], "mk": a["L1_mix_mem_kv"][0].reshape(P, MEM),
        "mv": a["L1_mix_mem_kv"][1].reshape(P, MEM), "gpre": col(a["L1_mix_g_pre"]), "gout": col(a["L1_mix_g_out"]),
        "bout": col(a["L1_mix_b_out"]),
        "w1": a["L1_ffn_w1"], "b1f": col(a["L1_ffn_b1"]), "w2": a["L1_ffn_w2"], "b2f": col(a["L1_ffn_b2"]),
        "wr1": a["L1_ffn_wr"], "br1": a["L1_ffn_br"],
    }
    arrays = {f"in_{k}": np.ascontiguousarray(v) for k, v in laid.items()}
    i = Names()
    for k, v in arrays.items():
        i.__dict__[k[3:]] = nc.dram_tensor(k, v.shape, mybir.dt.from_np(v.dtype), kind="ExternalInput").ap()
    out = nc.dram_tensor("out_x", (N, D), F32, kind="ExternalOutput").ap()
    build(nc, i, out)
    r = run(nc, [arrays], core_ids=[0])
    return r.results[0]["out_x"]
```

```python
from contextlib import ExitStack

import concourse.bass as bass
from concourse import mybir

F32 = mybir.dt.float32
F16 = mybir.dt.float16
BF16 = mybir.dt.bfloat16
I32 = mybir.dt.int32
ALU = mybir.AluOpType
ACT = mybir.ActivationFunctionType
AX = mybir.AxisListType

N = 3125
E = 50000
D = 256
P = 128
KH = D // P
B = 125
NB = N // B
T = 448
NT = -(-N // T)
NP = NT * T
EC = E // B
WC = 4
WE = WC * B
NW = EC // WC
HEADS0, HD0 = 4, 64
HEADS1, HD1, MEM = 4, 32, 4
HID0 = 3 * D
NEXP = 8
HID1 = 4 * D
TOPK = int(0.5 * N) - 1
BIG = 3.3895313892515355e38
ROUND = 12582912.0


class Steps:

    def __init__(self, eng, sem):
        self.eng, self.sem, self.base, self.n = eng, sem, 0, 0

    def __call__(self, ins):
        self.n += 1
        ins.then_inc(self.sem, 1)
        self.eng.wait_ge(self.sem, self.base + self.n)

    def turn(self, t, per_turn):
        self.base, self.n = t * per_turn, 0


class Scope(ExitStack):

    def __init__(self, nc, stage):
        super().__init__()
        self.nc, self.stage, self.sems = nc, stage, []

    def sb(self, name, shape, dt=F32):
        return self.enter_context(self.nc.sbuf_tensor(f"{self.stage}_{name}", shape, dt))

    def sem(self, name):
        self.sems.append(self.nc.alloc_semaphore(f"{self.stage}_{name}"))
        return self.sems[-1]

    def __exit__(self, *error):
        if self.sems and not error[0]:
            self.nc.clear_and_free_semaphores(self.sems)
            self.nc.all_engine_barrier()
        return super().__exit__(*error)


def constants(nc, c):
    with Scope(nc, "constants") as s:
        row_i = s.sb("row_i", [P, P], I32)
        col_i = s.sb("col_i", [P, 1], I32)
        col_f = s.sb("col_f", [P, 1])
        made = s.sem("iota_made")
        own = s.sem("const_steps")
        with nc.Block() as block:
            @block.gpsimd
            def _(pool):
                nc.gpsimd.iota(row_i[:], [[1, P]], base=0, channel_multiplier=0).then_inc(made, 1)
                nc.gpsimd.iota(col_i[:], [[0, 1]], base=0, channel_multiplier=1).then_inc(made, 1)
                nc.gpsimd.iota(c.spare[:], [[B, WC]], base=N * NP, channel_multiplier=1).then_inc(made, 1)

            @block.vector
            def _(dve):
                step = Steps(dve, own)
                v = nc.vector
                v.memset(c.ones[:], 1.0)
                v.memset(c.mean_w[:], 1.0 / D)
                dve.wait_ge(made, 3)
                v.tensor_copy(c.spare_f[:], c.spare[:])
                step(v.tensor_copy(c.row[:], row_i[:]))
                step(v.tensor_copy(col_f[:], col_i[:]))
                v.tensor_scalar(c.ident[:], c.row[:], col_f[:, 0:1], None, ALU.is_equal)
                v.tensor_scalar(c.upto[:], c.row[:], col_f[:, 0:1], None, ALU.is_ge)
                v.memset(c.before[:, WE:2 * WE - B], 1.0)
                v.memset(c.before[:, 0:WE - B], 1025.0)
                step(v.tensor_scalar(c.eps5[:], col_f[:, 0:1], 0.0, 1e-5, ALU.mult, ALU.add))
                step(v.tensor_scalar(c.tri[:], c.row[0:B, 0:B], col_f[0:B, 0:1], None, ALU.is_lt))
                step(v.tensor_scalar(c.before[:, WE - B:WE], c.tri[:], 1024.0, 1.0, ALU.mult, ALU.add))
                step(v.tensor_copy(c.row_b[:], c.row[0:B, 0:B]))


def edges(nc, c, src, dst, dram):
    A = EC // 100
    with Scope(nc, "edges") as s:
        src_r = s.sb("src_r", [100, A, B], I32)
        dst_r = s.sb("dst_r", [100, A, B], I32)
        prev_r = s.sb("prev_r", [100, A, B], I32)
        f_r = s.sb("f_r", [100, 3, A, B])
        same = s.sb("same", [100, A, B])
        reset = s.sb("reset", [100, A, B], BF16)
        dst_c = s.sb("dst_c", [B, EC])
        hi = s.sb("hi", [B, EC])
        hi_r = s.sb("hi_r", [B, EC])
        lo = s.sb("lo", [B, EC])
        oh_hi = s.sb("oh_hi", [B, EC, NB], BF16)
        oh_lo = s.sb("oh_lo", [B, 2, 16, B], BF16)
        deg = s.sb("deg", [B, NB])
        tot = s.sb("tot", [B, NB])
        off = s.sb("off", [B, NB])
        last = s.sb("last", [B, NB])
        rdeg = s.sb("rdeg", [B, NB])
        rdeg_t = s.sb("rdeg_t", [NB, B])
        zero = s.sb("zero", [B, NP], F16)
        ps = c.ps
        loaded = s.sem("edges_loaded")
        prev0 = s.sem("prev_cleared")
        own = s.sem("edge_steps")
        rows_ready = s.sem("rows_ready")
        turned = s.sem("rows_turned")
        hot_ready = s.sem("onehot_ready")
        hot_used = s.sem("onehot_used")
        deg_ready = s.sem("deg_ready")
        cum = s.sem("cum_done")
        rd = s.sem("rdeg_ready")
        rdt = s.sem("rdeg_turned")
        rdo = s.sem("rdeg_row_ready")
        stored = s.sem("edges_stored")
        z_ready = s.sem("zero_ready")
        zeroed = s.sem("adj_zeroed")
        HOT = 16
        NH = EC // HOT
        view = lambda a: a.rearrange("(a c p) -> c a p", c=100, p=B)
        with nc.Block() as block:
            @block.sync
            def _(sp):
                with nc.allow_non_contiguous_dma(reason="rows of 500 bytes"):
                    sp.dma_start(src_r[:], view(src)).then_inc(loaded, 16)
                    sp.dma_start(dst_r[:], view(dst)).then_inc(loaded, 16)
                    sp.wait_ge(prev0, 1)
                    sp.dma_start(prev_r[0:1, 0, 1:B], dst[0:B - 1].rearrange("(o p) -> o p", o=1)).then_inc(loaded, 16)
                    sp.dma_start(prev_r[1:100, 0, :], dst[B - 1:B - 1 + 99 * B].rearrange("(c p) -> c p", p=B)).then_inc(loaded, 16)
                    sp.dma_start(prev_r[:, 1:A, :], dst[100 * B - 1:E - 1].rearrange("(a c p) -> c a p", c=100, p=B)).then_inc(loaded, 16)
                    sp.wait_ge(z_ready, 1)
                    for j in range(NB):
                        sp.dma_start(dram.adj[B * j:B * (j + 1), :], zero[:]).then_inc(zeroed, 16)
                    sp.dma_start(dram.adj[N:N + 1, :], zero[0:1, :]).then_inc(zeroed, 16)
                    sp.wait_ge(rows_ready, 2)
                    sp.dma_start(view(dram.keys), f_r[:, 2]).then_inc(stored, 16)
                    sp.dma_start(view(dram.reset), reset[:]).then_inc(stored, 16)
                    sp.wait_ge(rdo, 1)
                    sp.dma_start(dram.rdeg.rearrange("(a p) -> a p", p=B), rdeg_t[:]).then_inc(stored, 16)
                    sp.wait_ge(stored, 48)
                    sp.wait_ge(zeroed, 16 * (NB + 1))

            @block.vector
            def _(dve):
                step = Steps(dve, own)
                v = nc.vector
                v.memset(prev_r[:], -1).then_inc(prev0, 1)
                v.memset(zero[:], 0.0).then_inc(z_ready, 1)
                dve.wait_ge(loaded, 80)
                v.tensor_copy(f_r[:, 0], src_r[:])
                step(v.tensor_copy(f_r[:, 1], dst_r[:]))
                step(v.scalar_tensor_tensor(f_r[:, 2], f_r[:, 0], float(NP), f_r[:, 1], ALU.mult, ALU.add))
                dve.sem_inc(rows_ready, 1)
                step(v.tensor_tensor(same[:], dst_r[:], prev_r[:], ALU.is_equal))
                step(v.tensor_scalar(same[:], same[:], 2.0, 1.0, ALU.mult, ALU.subtract))
                v.tensor_scalar(reset[:], same[:], BIG, None, ALU.mult).then_inc(rows_ready, 1)
                dve.wait_ge(turned, 1)
                v.tensor_copy(c.src_idx[:], ps[0][0:B, 0:EC])
                step(v.tensor_copy(dst_c[:], ps[1][0:B, 0:EC]))
                step(v.tensor_copy(c.key_c[:], ps[2][0:B, 0:EC]))
                step(v.tensor_scalar(hi[:], dst_c[:], (B - 1) / 2.0, 1.0 / B, ALU.subtract, ALU.mult))
                step(v.tensor_scalar(hi_r[:], hi[:], ROUND, None, ALU.add))
                step(v.tensor_scalar(hi[:], hi_r[:], ROUND, None, ALU.subtract))
                step(v.scalar_tensor_tensor(lo[:], hi[:], -float(B), dst_c[:], ALU.mult, ALU.add))
                step(v.tensor_tensor(oh_hi[:], hi[:].unsqueeze(2).to_broadcast([B, EC, NB]),
                                     c.row[0:B, 0:NB].unsqueeze(1).to_broadcast([B, EC, NB]), ALU.is_equal))
                for g in range(NH):
                    if g >= 2:
                        dve.wait_ge(hot_used, g - 1)
                    v.tensor_tensor(oh_lo[:, g % 2], lo[:, g * HOT:(g + 1) * HOT].unsqueeze(2).to_broadcast([B, HOT, B]),
                                    c.row_b[:].unsqueeze(1).to_broadcast([B, HOT, B]), ALU.is_equal).then_inc(hot_ready, 1)
                dve.wait_ge(hot_used, NH)
                step(v.tensor_copy(deg[:], ps[3][0:B, 0:NB]))
                v.tensor_scalar(c.has[:], deg[:], 0.0, None, ALU.is_gt)
                v.tensor_scalar(rdeg[:], deg[:], 1.0, None, ALU.max).then_inc(deg_ready, 1)
                dve.wait_ge(deg_ready, 1)
                step(v.tensor_scalar(c.lack[:], c.has[:], 1.0, BIG, ALU.subtract, ALU.mult))
                v.reciprocal(rdeg[:], rdeg[:]).then_inc(rd, 1)
                dve.wait_ge(cum, 1)
                step(v.tensor_copy(tot[:], ps[5][0:B, 0:NB]))
                step(v.tensor_tensor_scan(off[:], tot[:], tot[:], 0.0, ALU.add, ALU.max))
                step(v.tensor_tensor(off[:], off[:], tot[:], ALU.subtract))
                step(v.tensor_tensor(last[:], off[:], ps[4][0:B, 0:NB], ALU.add))
                step(v.tensor_scalar(last[:], last[:], 1.0, 0.0, ALU.subtract, ALU.max))
                step(v.tensor_copy(c.last_idx[:], last[:]))
                dve.wait_ge(rdt, 1)
                v.tensor_copy(rdeg_t[:], ps[6][0:NB, 0:B]).then_inc(rdo, 1)

            @block.tensor
            def _(pe):
                pe.wait_ge(rows_ready, 1)
                for k in range(3):
                    for a in range(A):
                        mm = nc.tensor.transpose(ps[k][0:B, 100 * a:100 * (a + 1)], f_r[:, k, a, :], c.ident[0:100, 0:100])
                mm.then_inc(turned, 1)
                for g in range(NH):
                    pe.wait_ge(hot_ready, g + 1)
                    for k in range(HOT):
                        e = g * HOT + k
                        mm = nc.tensor.matmul(ps[3][0:B, 0:NB], oh_lo[:, g % 2, k, :], oh_hi[:, e, :],
                                              start=(e == 0), stop=(e == EC - 1))
                    mm.then_inc(hot_used, 1)
                pe.wait_ge(deg_ready, 1)
                nc.tensor.matmul(ps[4][0:B, 0:NB], c.upto[0:B, 0:B], deg[:], start=True, stop=True)
                nc.tensor.matmul(ps[5][0:B, 0:NB], c.ones[0:B, 0:B], deg[:], start=True, stop=True).then_inc(cum, 1)
                pe.wait_ge(rd, 1)
                nc.tensor.transpose(ps[6][0:NB, 0:B], rdeg[:], c.ident[0:B, 0:B]).then_inc(rdt, 1)


def cols(t, width=T):
    return bass.ds(t * width, width)


def half(h):
    return slice(h * P, (h + 1) * P)


def nodes(nc, c, x, dram, w):
    with Scope(nc, "nodes") as s:
        xt = s.sb("xt", [B, NB, D])
        xn = s.sb("xn", [B, NB, D + 1])
        stats = s.sb("stats", [B, NB, 6])
        mv = s.sb("mv", [B, NB, 2])
        sd = s.sb("sd", [B, NB])
        rs = s.sb("rs", [B, NB])
        wb = s.sb("wb", [P, KH, D])
        bo = s.sb("bo", [B, 4, D])
        gram = s.sb("gram", [P, KH, D + 1])
        uu = s.sb("uu", [P, KH, D])
        csum = s.sb("csum", [1, D])
        rr = s.sb("rr", [1, D])
        cnt = s.sb("cnt", [1, 1])
        gs = s.sb("gs", [P, KH, P])
        mx = s.sb("mx", [P, KH])
        sm = s.sb("sm", [P, KH])
        att = s.sb("att", [P, KH, P])
        ps = c.ps
        loaded = s.sem("x_loaded")
        own = s.sem("node_steps")
        var_ready, sd_ready = s.sem("var_ready"), s.sem("sd_ready")
        xn_ready = s.sem("xn_ready")
        turned, taken_v, taken_a = s.sem("turned"), s.sem("taken_v"), s.sem("taken_a")
        gram_done, gram_out = s.sem("gram_done"), s.sem("gram_out")
        b_done, b_out = s.sem("b_done"), s.sem("b_out")
        b_stored = [s.sem(f"b_stored{k}") for k in range(4)]
        wb_ready = s.sem("wb_ready")
        att_pe, att_v, att_a = s.sem("att_pe"), s.sem("att_v"), s.sem("att_a")
        G4 = -(-NB // 4)
        groups = [(g, min(4, NB - 4 * g)) for g in range(G4)]
        with nc.Block() as block:
            @block.sync
            def _(sp):
                sp.dma_start(xt[:], x.rearrange("(j p) f -> p j f", p=B)).then_inc(loaded, 16)
                for j in range(NB):
                    sp.wait_ge(b_out, j + 1)
                    sp.dma_start(dram.rows[B * j:B * (j + 1), :], bo[:, j % 4, :]).then_inc(b_stored[j % 4], 16)
                for k in range(4):
                    sp.wait_ge(b_stored[k], 16 * len(range(k, NB, 4)))

            @block.scalar
            def _(act):
                act.wait_ge(var_ready, 1)
                nc.scalar.activation(sd[:], mv[:, :, 1], ACT.Sqrt, bias=c.eps5[0:B, 0:1]).then_inc(sd_ready, 1)
                for g, n in groups:
                    for h in range(KH):
                        k = 4 * g + 2 + h
                        act.wait_ge(turned, k + 1)
                        nc.scalar.copy(c.yn[:, h, 4 * B * g:4 * B * g + n * B], ps[k % 4][:, 0:n * B]).then_inc(taken_a, 1)
                act.wait_ge(att_v, 2)
                nc.scalar.activation(att[:], gs[:], ACT.Exp).then_inc(att_a, 1)

            @block.vector
            def _(dve):
                step = Steps(dve, own)
                v = nc.vector
                v.memset(c.xT[:, :, N:NP], 0.0)
                v.memset(c.yn[:, :, N:NP], 0.0)
                v.memset(cnt[:], float(N))
                step(v.memset(xn[:, :, D:D + 1], 1.0))
                dve.wait_ge(w.loaded, w.total)
                v.tensor_tensor(wb[:], w.phi[:], w.theta[:], ALU.subtract).then_inc(wb_ready, 1)
                dve.wait_ge(loaded, 16)
                for j in range(NB):
                    ins = v.bn_stats(stats[:, j, :], xt[:, j, :])
                step(ins)
                for j in range(NB):
                    ins = v.bn_aggr(mv[:, j, :], stats[:, j, :])
                ins.then_inc(var_ready, 1)
                dve.wait_ge(sd_ready, 1)
                dve.wait_ge(var_ready, 1)
                step(v.reciprocal(rs[:], sd[:]))
                for j in range(NB):
                    v.tensor_scalar(xn[:, j, 0:D], xt[:, j, :], mv[:, j, 0:1], rs[:, j:j + 1],
                                    ALU.subtract, ALU.mult).then_inc(xn_ready, 1)
                for g, n in groups:
                    for h in range(KH):
                        k = 4 * g + h
                        dve.wait_ge(turned, k + 1)
                        v.tensor_copy(c.xT[:, h, 4 * B * g:4 * B * g + n * B], ps[k % 4][:, 0:n * B]).then_inc(taken_v, 1)
                for j in range(NB):
                    dve.wait_ge(b_done, j + 1)
                    if j >= 4:
                        dve.wait_ge(b_stored[j % 4], 16 * (j // 4))
                    v.tensor_copy(bo[:, j % 4, :], ps[j % 4][0:B, 0:D]).then_inc(b_out, 1)
                dve.wait_ge(gram_done, 1)
                v.tensor_copy(gram[:, 0, :], ps[4][:, 0:D + 1])
                v.tensor_copy(gram[:, 1, :], ps[5][:, 0:D + 1])
                v.tensor_copy(csum[:], ps[6][0:1, 0:D]).then_inc(gram_out, 1)
                dve.wait_ge(att_pe, 1)
                v.tensor_copy(uu[:, 0, :], ps[0][:, 0:D])
                v.tensor_copy(uu[:, 1, :], ps[1][:, 0:D])
                v.tensor_copy(rr[:], ps[2][0:1, 0:D]).then_inc(att_v, 1)
                dve.wait_ge(att_pe, 2)
                scale = HD0 ** -0.5
                v.tensor_scalar(gs[:, 0, :], ps[3][:, 0:P], scale, None, ALU.mult)
                step(v.tensor_scalar(gs[:, 1, :], ps[4][:, P:2 * P], scale, None, ALU.mult))
                for h in range(KH):
                    for q in range(2):
                        r = slice(q * HD0, (q + 1) * HD0)
                        ins = v.tensor_reduce(mx[r, h:h + 1], gs[r, h, r], AX.X, ALU.max)
                step(ins)
                step(v.tensor_copy(sm[:], mx[:]))
                for h in range(KH):
                    ins = v.tensor_scalar(gs[:, h, :], gs[:, h, :], mx[:, h:h + 1], 0.0, ALU.subtract, ALU.min)
                ins.then_inc(att_v, 1)
                dve.wait_ge(att_a, 1)
                for h in range(KH):
                    v.memset(att[0:HD0, h, HD0:P], 0.0)
                    step(v.memset(att[HD0:P, h, 0:HD0], 0.0))
                step(v.tensor_reduce(sm[:], att[:], AX.X, ALU.add))
                step(v.reciprocal(sm[:], sm[:]))
                for h in range(KH):
                    ins = v.tensor_scalar(att[:, h, :], att[:, h, :], sm[:, h:h + 1], None, ALU.mult)
                ins.then_inc(att_v, 1)
                dve.wait_ge(att_pe, 3)
                v.tensor_copy(c.attT[:, 0, :], ps[0][:, 0:P])
                v.tensor_copy(c.attT[:, 1, :], ps[1][:, 0:P])

            @block.tensor
            def _(pe):
                mm = nc.tensor.matmul
                pe.wait_ge(loaded, 16)
                for g, n in groups:
                    pe.wait_ge(xn_ready, 4 * g + n)
                    for k, (a, h) in enumerate(((xt, 0), (xt, 1), (xn, 0), (xn, 1))):
                        if g >= 1:
                            if k < 2:
                                pe.wait_ge(taken_v, 2 * (g - 1) + k + 1)
                            else:
                                pe.wait_ge(taken_a, 2 * (g - 1) + k - 1)
                        for i in range(n):
                            ins = nc.tensor.transpose(ps[k][:, B * i:B * (i + 1)], a[:, 4 * g + i, half(h)], c.ident[0:B, 0:B])
                        ins.then_inc(turned, 1)
                pe.wait_ge(taken_v, 2 * G4)
                pe.wait_ge(taken_a, 2 * G4)
                pe.wait_ge(wb_ready, 1)
                for j in range(NB):
                    if j >= 4:
                        pe.wait_ge(b_out, j - 3)
                    for k in range(KH):
                        ins = mm(ps[j % 4][0:B, 0:D], c.yn[:, k, B * j:B * (j + 1)], wb[:, k, :], start=(k == 0), stop=(k == KH - 1))
                    ins.then_inc(b_done, 1)
                for j in range(NB):
                    for h in range(KH):
                        mm(ps[4 + h][:, 0:D + 1], xn[:, j, half(h)], xn[:, j, :], start=(j == 0), stop=(j == NB - 1))
                    ins = mm(ps[6][0:1, 0:D], c.ones[0:B, 0:1], xn[:, j, 0:D], start=(j == 0), stop=(j == NB - 1))
                ins.then_inc(gram_done, 1)
                pe.wait_ge(gram_out, 1)
                pe.wait_ge(b_out, NB)
                for h in range(KH):
                    for k in range(KH):
                        mm(ps[h][:, 0:D], gram[:, k, half(h)], w.qkv[:, k, 2 * D:3 * D], start=(k == 0), stop=False)
                    mm(ps[h][:, 0:D], csum[0:1, half(h)], w.bqkv_row[0:1, 2 * D:3 * D], start=False, stop=True)
                for k in range(KH):
                    mm(ps[2][0:1, 0:D], gram[:, k, D:D + 1], w.qkv[:, k, 2 * D:3 * D], start=(k == 0), stop=False)
                mm(ps[2][0:1, 0:D], cnt[0:1, 0:1], w.bqkv_row[0:1, 2 * D:3 * D], start=False, stop=True).then_inc(att_pe, 1)
                pe.wait_ge(att_v, 1)
                for h in range(KH):
                    for k in range(KH):
                        mm(ps[3 + h][:, 0:D], w.qkv[:, k, D + h * P:D + (h + 1) * P], uu[:, k, :], start=(k == 0), stop=False)
                    ins = mm(ps[3 + h][:, 0:D], w.bqkv_row[0:1, D + h * P:D + (h + 1) * P], rr[0:1, :], start=False, stop=True)
                ins.then_inc(att_pe, 1)
                pe.wait_ge(att_v, 3)
                for h in range(KH):
                    ins = nc.tensor.transpose(ps[h][:, 0:P], att[:, h, :], c.ident[:])
                ins.then_inc(att_pe, 1)


def edges_and_mix0(nc, c, dram, w):
    SLOTS = NW // NT
    assert SLOTS == 14 and WC * WE + 2 * WE < 1 << 24
    M1 = HID0 // P
    with Scope(nc, "mix0") as s:
        got = [s.sb(f"got{i}", [B, D]) for i in range(2 * WC)]
        rst = s.sb("rst", [P, 2, WE], BF16)
        scan = s.sb("scan", [P, 2, KH, WE])
        back = s.sb("back", [B, 2, WC, D])
        krow = s.sb("krow", [B, 2, WE])
        junk = s.sb("junk", [B, 2, WE], F16)
        cell = s.sb("cell", [B, EC])
        dup = s.sb("dup", [B, EC])
        q = s.sb("q", [P, KH, T])
        sx = s.sb("sx", [P, KH, T])
        cen = s.sb("cen", [P, KH, T])
        sd = s.sb("sd", [P, T])
        hn = s.sb("hn", [P, KH, T])
        hid = s.sb("hid", [P, M1, T])
        ab = s.sb("ab", [P, KH])
        ps = c.ps
        gathered = [s.sem(f"gathered{i}") for i in range(2 * WC)]
        rst_in = [s.sem(f"rst_in{b}") for b in range(2)]
        krow_in = [s.sem(f"krow_in{b}") for b in range(2)]
        stored = [s.sem(f"run_stored{b}") for b in range(2)]
        turned, scanned, turned_back, copied = s.sem("turned"), s.sem("scanned"), s.sem("turned_back"), s.sem("copied")
        counted, own_c = s.sem("counted"), s.sem("count_steps")
        pe_done, act_done, own = s.sem("mix_pe"), s.sem("mix_act"), s.sem("mix_steps")
        PE_N, ACT_N, DVE_N = 7 + M1, 3 + M1, 14
        runs = dram.runs.rearrange("(w c p) f -> w p c f", c=WC, p=B)
        with nc.Block() as block:
            @block.gpsimd
            def _(pool):
                for n in range(NW):
                    for j in range(WC):
                        if n >= 2:
                            pool.wait_ge(turned, WC * (n - 2) + j + 1)
                        i, k = WC * (n % 2) + j, WC * n + j
                        nc.gpsimd.indirect_dma_start(got[i][:, :], None, dram.rows[:, :],
                                                     bass.IndirectOffsetOnAxis(ap=c.src_idx[:, k:k + 1], axis=0)).then_inc(gathered[i], 16)

            @block.sync
            def _(sp):
                def load(n, b):
                    sp.wait_ge(counted, WC * n - WC + 2)
                    sp.dma_start(rst[:, b, :], dram.reset[bass.ds(n * WE, WE)].partition_broadcast(P)).then_inc(rst_in[b], 16)
                    sp.dma_start(krow[:, b, :], dram.keys[bass.ds(n * WE, WE)].partition_broadcast(B)).then_inc(krow_in[b], 16)

                def store(n, b):
                    sp.wait_ge(copied, 2 * n + 4)
                    sp.dma_start(runs[bass.ds(n, 1)].rearrange("o p c f -> (o p) c f"), back[:, b]).then_inc(stored[b], 16)

                for b in range(2):
                    sp.sem_inc(stored[b], 16)
                    sp.wait_ge(scanned, 2)
                    sp.dma_start(rst[:, b, :], dram.reset[b * WE:(b + 1) * WE].partition_broadcast(P)).then_inc(rst_in[b], 16)
                    sp.dma_start(krow[:, b, :], dram.keys[b * WE:(b + 1) * WE].partition_broadcast(B)).then_inc(krow_in[b], 16)
                with sp.Fori(0, NW // 2 - 1) as i:
                    for b in range(2):
                        store(2 * i + b, b)
                        load(2 * i + 2 + b, b)
                for b in range(2):
                    store(NW - 2 + b, b)
                for b in range(2):
                    sp.wait_ge(stored[b], 16 * (NW // 2 + 1))

            @block.tensor
            def _(pe):
                def forward(n, b):
                    pe.wait_ge(scanned, 2 * n + 2)
                    for j in range(WC):
                        pe.wait_ge(gathered[WC * b + j], 8 * (n - b) + 16)
                        for h in range(KH):
                            ins = nc.tensor.transpose(ps[2 * b + h][:, B * j:B * (j + 1)], got[WC * b + j][:, half(h)], c.ident[0:B, 0:B])
                        ins.then_inc(turned, 1)

                def backward(n, b):
                    pe.wait_ge(scanned, 2 * n + 6)
                    pe.wait_ge(copied, 2 * n + 2)
                    for j in range(WC):
                        for h in range(KH):
                            at = D * (j % 2) + P * h
                            ins = nc.tensor.transpose(ps[4 + j // 2][0:B, at:at + P], scan[:, b, h, B * j:B * (j + 1)], c.ident[:])
                        if j % 2:
                            ins.then_inc(turned_back, 1)

                def piece(t, k):
                    tile = [c.yn[:, i, cols(t)] for i in range(KH)]
                    pe_wait = lambda sem, per, n: pe.wait_ge(sem, t * per + n)
                    if k == 0:
                        pe_wait(own, DVE_N, 1)
                        for h in range(KH):
                            ins = product(nc, ps[6 + h][:, 0:T], [w.qkv[:, i, half(h)] for i in range(KH)], tile)
                        ins.then_inc(pe_done, 1)
                    elif k == 1:
                        pe_wait(act_done, ACT_N, 1)
                        for h in range(KH):
                            ins = product(nc, ps[6 + h][:, 0:T], [w.theta[:, i, half(h)] for i in range(KH)], tile)
                        ins.then_inc(pe_done, 1)
                    elif k == 2:
                        pe_wait(own, DVE_N, 3)
                        for h in range(KH):
                            ins = product(nc, ps[6 + h][:, 0:T], [c.attT[:, h, :]], [q[:, h, :]])
                        ins.then_inc(pe_done, 1)
                    elif k == 3:
                        pe_wait(own, DVE_N, 5)
                        product(nc, ps[6][:, 0:T], [c.mean_w[:]] * KH, [sx[:, i, :] for i in range(KH)]).then_inc(pe_done, 1)
                    elif k == 4:
                        pe_wait(act_done, ACT_N, 2)
                        product(nc, ps[7][:, 0:T], [c.mean_w[:]] * KH, [hid[:, i, :] for i in range(KH)]).then_inc(pe_done, 1)
                    elif 6 <= k < 6 + M1:
                        m = k - 6
                        if m == 0:
                            pe_wait(own, DVE_N, 12)
                        if m >= 2:
                            pe_wait(act_done, ACT_N, 3 + m - 1)
                        product(nc, ps[6 + m % 2][:, 0:T], [w.fc1[:, i, m * P:(m + 1) * P] for i in range(KH)],
                                [hn[:, i, :] for i in range(KH)]).then_inc(pe_done, 1)
                    elif k >= 6 + M1:
                        h = k - 6 - M1
                        pe_wait(act_done, ACT_N, 3 + M1)
                        product(nc, ps[6 + h][:, 0:T], [w.fc2[:, m, half(h)] for m in range(M1)],
                                [hid[:, m, :] for m in range(M1)]).then_inc(pe_done, 1)

                pe.sem_inc(turned_back, 4)
                with pe.Fori(0, NT) as t:
                    for k in range(SLOTS):
                        forward(SLOTS * t + k, k % 2)
                        piece(t, k)
                        backward(SLOTS * t + k, k % 2)
                for n in range(SLOTS * NT, NW):
                    forward(n, n % 2)
                    backward(n, n % 2)

            @block.scalar
            def _(act):
                a = nc.scalar.activation

                def copy(n, b):
                    act.wait_ge(stored[b], 8 * (n - b) + 16)
                    for i in range(2):
                        act.wait_ge(turned_back, 2 * n + 5 + i)
                        nc.scalar.copy(back[:, b, 2 * i:2 * i + 2, :], ps[4 + i][0:B, 0:2 * D]).then_inc(copied, 1)

                def piece(t, k):
                    if k == 0:
                        act.wait_ge(pe_done, t * PE_N + 1)
                        for h in range(KH):
                            ins = a(q[:, h, :], ps[6 + h][:, 0:T], ACT.Identity, bias=w.bq[:, h:h + 1])
                        ins.then_inc(act_done, 1)
                    elif k == 3:
                        act.wait_ge(own, t * DVE_N + 7)
                        a(hid[:, 0:KH, :], cen[:], ACT.Square).then_inc(act_done, 1)
                    elif k == 4:
                        act.wait_ge(pe_done, t * PE_N + 5)
                        a(sd[:], ps[7][:, 0:T], ACT.Sqrt, bias=c.eps5[:, 0:1]).then_inc(act_done, 1)
                    elif 6 <= k < 6 + M1:
                        m = k - 6
                        act.wait_ge(pe_done, t * PE_N + 6 + m)
                        a(hid[:, m, :], ps[6 + m % 2][:, 0:T], ACT.Gelu, bias=w.b1[:, m:m + 1]).then_inc(act_done, 1)

                act.sem_inc(copied, 2)
                with act.Fori(0, NT) as t:
                    for k in range(SLOTS):
                        piece(t, k)
                        copy(SLOTS * t + k, k % 2)
                for n in range(SLOTS * NT, NW):
                    copy(n, n % 2)

            @block.vector
            def _(dve):
                v = nc.vector
                step = Steps(dve, own)

                def scans(n, b):
                    dve.wait_ge(rst_in[b], 8 * (n - b) + 16)
                    dve.wait_ge(turned, WC * n + WC)
                    dve.wait_ge(turned_back, 2 * n + 2)
                    for h in range(KH):
                        dve.wait_ge(scanned, 2 * n + 3 + h)
                        v.tensor_tensor_scan(scan[:, b, h, :], rst[:, b, :], ps[2 * b + h][:, 0:WE],
                                             scan[:, 1 - b, h, WE - 1:WE], ALU.min, ALU.max).then_inc(scanned, 1)

                def count(n, b):
                    dve.wait_ge(krow_in[b], 8 * (n - b) + 16)
                    for j in range(WC):
                        at = bass.ds(WC * n + j, 1)
                        dve.wait_ge(counted, WC * n + j + 1)
                        v.scalar_tensor_tensor(junk[:, j % 2, :], krow[:, b, :], c.key_c[:, at],
                                               c.before[:, WE - B * (j + 1):2 * WE - B * (j + 1)],
                                               ALU.is_equal, ALU.mult, accum_out=c.cnt[:, at]).then_inc(counted, 1)

                def piece(t, k):
                    at = cols(t)
                    if k == 1:
                        dve.wait_ge(pe_done, t * PE_N + 2)
                        for h in range(KH):
                            step(v.tensor_scalar(c.a[:, h, at], ps[6 + h][:, 0:T], ab[:, h:h + 1], None, ALU.add))
                    elif k == 2:
                        dve.wait_ge(pe_done, t * PE_N + 3)
                        for h in range(KH):
                            step(v.tensor_tensor(sx[:, h, :], ps[6 + h][:, 0:T], c.yn[:, h, at], ALU.add))
                    elif k == 3:
                        dve.wait_ge(pe_done, t * PE_N + 4)
                        for h in range(KH):
                            step(v.tensor_tensor(cen[:, h, :], sx[:, h, :], ps[6][:, 0:T], ALU.subtract))
                    elif k == 5:
                        dve.wait_ge(act_done, t * ACT_N + 3)
                        step(v.reciprocal(sd[:], sd[:]))
                        for h in range(KH):
                            step(v.tensor_tensor(cen[:, h, :], cen[:, h, :], sd[:], ALU.mult))
                        for h in range(KH):
                            step(v.tensor_scalar(hn[:, h, :], cen[:, h, :], w.ng[:, h:h + 1], w.nb[:, h:h + 1], ALU.mult, ALU.add))
                        step(v.tensor_tensor(c.xT[:, :, at], c.xT[:, :, at], sx[:], ALU.add))
                    elif k >= 6 + M1:
                        h = k - 6 - M1
                        dve.wait_ge(pe_done, t * PE_N + 6 + M1 + h)
                        step(v.scalar_tensor_tensor(c.xT[:, h, at], ps[6 + h][:, 0:T], w.b2[:, h:h + 1], c.xT[:, h, at], ALU.add, ALU.add))

                v.memset(scan[:, 1, :, :], -BIG).then_inc(scanned, 4)
                dve.sem_inc(counted, 2)
                step(v.tensor_tensor(ab[:], w.tb[:], w.pb[:], ALU.add))
                step.n = 1
                with dve.Fori(0, NT) as t:
                    step.turn(t, DVE_N)
                    step.n = 1
                    for k in range(SLOTS):
                        scans(SLOTS * t + k, k % 2)
                        piece(t, k)
                        count(SLOTS * t + k, k % 2)
                for n in range(SLOTS * NT, NW):
                    scans(n, n % 2)
                    count(n, n % 2)
                cs = Steps(dve, own_c)
                dve.wait_ge(counted, EC + 2)
                cs(v.tensor_scalar(dup[:], c.cnt[:], 1024.0, None, ALU.is_ge))
                chunks = lambda z: z.rearrange("p (w j) -> p w j", j=WC)
                cs(v.tensor_tensor(chunks(cell[:]), chunks(c.key_c[:]), c.spare_f[0:B, :].unsqueeze(1).to_broadcast([B, NW, WC]), ALU.subtract))
                cs(v.tensor_tensor(cell[:], cell[:], dup[:], ALU.mult))
                cs(v.tensor_tensor(cell[:], c.key_c[:], cell[:], ALU.subtract))
                cs(v.tensor_copy(c.cell_idx[:], cell[:]))
                cs(v.tensor_scalar(dup[:], dup[:], -1.0, 1.0, ALU.mult, ALU.add))
                cs(v.tensor_tensor(c.cell_val[:], c.cnt[:], dup[:], ALU.mult))


def add_cells(nc, c, dram, pool, first, last):
    for n in range(first, last):
        if n:
            pool.wait_ge(c.added, 16 * WC * n)
        for j in range(WC):
            k = WC * n + j
            nc.gpsimd.indirect_dma_start(dram.adj_flat, bass.IndirectOffsetOnAxis(ap=c.cell_idx[:, k:k + 1], axis=0),
                                         c.cell_val[:, k:k + 1], None, compute_op=ALU.add).then_inc(c.added, 16)
    if last == NW:
        pool.wait_ge(c.added, 16 * WC * NW)


def join_max(nc, c, dram):
    with Scope(nc, "join_max") as s:
        m = s.sb("m", [B, NB, D])
        mm_ = s.sb("mm_", [B, NB, D])
        t1 = s.sb("t1", [P, 2, 4 * B])
        got = [s.sem(f"m_got{i}") for i in range(NB)]
        masked, turned, summed, own = s.sem("m_masked"), s.sem("m_turned"), s.sem("m_summed"), s.sem("join_steps")
        G4 = -(-NB // 4)
        with nc.Block() as block:
            @block.gpsimd
            def _(pool):
                for j in range(NB):
                    nc.gpsimd.indirect_dma_start(m[:, j, :], None, dram.runs[:, :],
                                                 bass.IndirectOffsetOnAxis(ap=c.last_idx[:, j:j + 1], axis=0)).then_inc(got[j], 16)

            @block.vector
            def _(dve):
                v = nc.vector
                step = Steps(dve, own)
                for j in range(NB):
                    dve.wait_ge(got[j], 16)
                    v.tensor_scalar(mm_[:, j, :], m[:, j, :], c.has[:, j:j + 1], c.lack[:, j:j + 1], ALU.mult, ALU.add).then_inc(masked, 1)
                for g in range(G4):
                    n = min(4, NB - 4 * g) * B
                    at = slice(4 * B * g, 4 * B * g + n)
                    for h in range(KH):
                        k = 2 * g + h
                        dve.wait_ge(turned, k + 1)
                        v.tensor_tensor(t1[:, h, 0:n], c.ps[k % 8][:, 0:n], c.a[:, h, at], ALU.add).then_inc(summed, 1)
                        dve.wait_ge(summed, k + 1)
                        step(v.scalar_tensor_tensor(c.xT[:, h, at], t1[:, h, 0:n], 0.0, c.xT[:, h, at], ALU.max, ALU.add))

            @block.tensor
            def _(pe):
                for g in range(G4):
                    n = min(4, NB - 4 * g)
                    pe.wait_ge(masked, 4 * g + n)
                    for h in range(KH):
                        k = 2 * g + h
                        if k >= 8:
                            pe.wait_ge(summed, k - 7)
                        for i in range(n):
                            ins = nc.tensor.transpose(c.ps[k % 8][:, B * i:B * (i + 1)], mm_[:, 4 * g + i, half(h)], c.ident[0:B, 0:B])
                        ins.then_inc(turned, 1)


def product(nc, out, lhs, rhs, chain=True):
    for k, (a, b) in enumerate(zip(lhs, rhs)):
        ins = nc.tensor.matmul(out, a, b, start=(k == 0), stop=(k == len(lhs) - 1))
    return ins


def norm(nc, c, out, n, beside=None):
    with Scope(nc, f"norm{n}") as s:
        sq = s.sb("sq", [P, 2, KH, T])
        sd = s.sb("sd", [P, 2, T])
        ps = c.ps
        mean_done, var_done = s.sem("mean_done"), s.sem("var_done")
        cen_ready, sq_ready, sd_ready, sd_used = s.sem("cen_ready"), s.sem("sq_ready"), s.sem("sd_ready"), s.sem("sd_used")
        own = s.sem("norm_steps")
        at = lambda t: slice(t * T, (t + 1) * T)
        with nc.Block() as block:
            if beside:
                block.gpsimd(beside)

            @block.tensor
            def _(pe):
                def mean(t):
                    if t >= 4:
                        pe.wait_ge(cen_ready, t - 3)
                    product(nc, ps[t % 4][:, 0:T], [c.mean_w[:]] * KH, [c.xT[:, k, at(t)] for k in range(KH)]).then_inc(mean_done, 1)

                def var(t):
                    if t >= 4:
                        pe.wait_ge(sd_ready, t - 3)
                    pe.wait_ge(sq_ready, t + 1)
                    product(nc, ps[4 + t % 4][:, 0:T], [c.mean_w[:]] * KH, [sq[:, t % 2, k, :] for k in range(KH)]).then_inc(var_done, 1)

                for t in range(NT + 2):
                    if t < NT:
                        mean(t)
                    if t >= 2:
                        var(t - 2)

            @block.scalar
            def _(act):
                for t in range(NT + 1):
                    if t < NT:
                        act.wait_ge(cen_ready, t + 1)
                        if t >= 2:
                            act.wait_ge(var_done, t - 1)
                        nc.scalar.activation(sq[:, t % 2], out[:, :, at(t)], ACT.Square).then_inc(sq_ready, 1)
                    if t >= 1:
                        act.wait_ge(var_done, t)
                        if t >= 3:
                            act.wait_ge(sd_used, t - 2)
                        nc.scalar.activation(sd[:, (t - 1) % 2], ps[4 + (t - 1) % 4][:, 0:T], ACT.Sqrt, bias=c.eps5[:, 0:1]).then_inc(sd_ready, 1)

            @block.vector
            def _(dve):
                v = nc.vector
                step = Steps(dve, own)
                for t in range(NT + 1):
                    if t < NT:
                        dve.wait_ge(mean_done, t + 1)
                        v.tensor_tensor(out[:, 0, at(t)], c.xT[:, 0, at(t)], ps[t % 4][:, 0:T], ALU.subtract)
                        v.tensor_tensor(out[:, 1, at(t)], c.xT[:, 1, at(t)], ps[t % 4][:, 0:T], ALU.subtract).then_inc(cen_ready, 1)
                    if t >= 1:
                        dve.wait_ge(sd_ready, t)
                        step(v.reciprocal(sd[:, (t - 1) % 2], sd[:, (t - 1) % 2]))
                        dve.wait_ge(sq_ready, t)
                        v.tensor_tensor(out[:, 0, at(t - 1)], out[:, 0, at(t - 1)], sd[:, (t - 1) % 2], ALU.mult)
                        v.tensor_tensor(out[:, 1, at(t - 1)], out[:, 1, at(t - 1)], sd[:, (t - 1) % 2], ALU.mult).then_inc(sd_used, 1)


def gate(nc, c, w, dram, beside=None):
    with Scope(nc, "gate") as s:
        lg = s.sb("lg", [B, NB, NEXP])
        mx = s.sb("mx", [B, NB])
        wT = s.sb("wT", [NEXP, NP])
        ps = c.ps
        G4 = -(-NB // 4)
        logits, ready, ex, own = s.sem("logits"), s.sem("lg_ready"), s.sem("lg_exp"), s.sem("gate_steps")
        turned, copied, stored = s.sem("wg_turned"), s.sem("wg_copied"), s.sem("wg_stored")
        with nc.Block() as block:
            if beside:
                block.gpsimd(beside)

            @block.tensor
            def _(pe):
                for j in range(NB):
                    at = slice(B * j, B * (j + 1))
                    out = ps[0][0:B, NEXP * j:NEXP * (j + 1)]
                    for k in range(KH):
                        nc.tensor.matmul(out, c.yn[:, k, at], w.Wr[:, k, :], start=(k == 0), stop=False)
                    ins = nc.tensor.matmul(out, c.ones[0:1, 0:B], w.br[:, :], start=False, stop=True)
                ins.then_inc(logits, 1)
                pe.wait_ge(ready, 2)
                for g in range(G4):
                    n = min(4, NB - 4 * g)
                    for i in range(n):
                        ins = nc.tensor.transpose(ps[1 + g][0:NEXP, B * i:B * (i + 1)], lg[:, 4 * g + i, :], c.ident[0:B, 0:B])
                    ins.then_inc(turned, 1)

            @block.vector
            def _(dve):
                v = nc.vector
                step = Steps(dve, own)
                v.memset(wT[:, N:NP], 0.0)
                dve.wait_ge(logits, 1)
                step(v.tensor_copy(lg[:], ps[0][0:B, 0:NB * NEXP].rearrange("p (j e) -> p j e", e=NEXP)))
                wide = mx[:].unsqueeze(2).to_broadcast([B, NB, NEXP])
                step(v.tensor_reduce(mx[:], lg[:], AX.X, ALU.max))
                v.tensor_tensor(lg[:], lg[:], wide, ALU.subtract).then_inc(ready, 1)
                dve.wait_ge(ex, 1)
                step(v.tensor_reduce(mx[:], lg[:], AX.X, ALU.add))
                step(v.reciprocal(mx[:], mx[:]))
                v.tensor_tensor(lg[:], lg[:], wide, ALU.mult).then_inc(ready, 1)
                for g in range(G4):
                    n = min(4, NB - 4 * g) * B
                    dve.wait_ge(turned, g + 1)
                    v.tensor_copy(wT[:, 4 * B * g:4 * B * g + n], ps[1 + g][0:NEXP, 0:n]).then_inc(copied, 1)

            @block.scalar
            def _(act):
                act.wait_ge(ready, 1)
                nc.scalar.activation(lg[:], lg[:], ACT.Exp).then_inc(ex, 1)

            @block.sync
            def _(sp):
                sp.wait_ge(copied, G4)
                sp.dma_start(dram.gate[:, :], wT[:]).then_inc(stored, 16)
                sp.wait_ge(stored, 16)


def fold(nc, c, w):
    with Scope(nc, "fold") as s:
        sd, own = s.sem("bn_sd"), s.sem("bn_steps")
        with nc.Block() as block:
            @block.scalar
            def _(act):
                act.wait_ge(w.loaded, w.total)
                act.wait_ge(own, 1)
                for i in range(2):
                    nc.scalar.activation(w.bn[:, i, 4], w.bn[:, i, 4], ACT.Sqrt, bias=c.eps3[:, 0:1]).then_inc(sd, 1)

            @block.vector
            def _(dve):
                v = nc.vector
                step = Steps(dve, own)
                step(v.memset(c.eps3[:], 1e-3))
                dve.wait_ge(sd, 2)
                for i in range(2):
                    b, g, be, m, sv = (w.bn[:, i, k] for k in range(5))
                    step(v.reciprocal(sv, sv))
                    step(v.tensor_tensor(w.scale[:, i], g, sv, ALU.mult))
                    step(v.tensor_tensor(b, b, m, ALU.subtract))
                    step(v.tensor_tensor(b, b, w.scale[:, i], ALU.mult))
                    step(v.tensor_tensor(w.shift[:, i], b, be, ALU.add))


def experts(nc, c, w, dram, beside=None):
    with Scope(nc, "experts") as s:
        gb = [s.sb(f"gb{e}", [P, T]) for e in range(NEXP)]
        gT = s.sb("gT", [NEXP, NP])
        h1 = s.sb("h1", [P, 2, KH, T])
        h2 = s.sb("h2", [P, 2, KH, T])
        hw = s.sb("hw", [P, 2, KH, T])
        ps = c.ps
        gb_in = [s.sem(f"gb_in{e}") for e in range(NEXP)]
        gt_in = s.sem("gt_in")
        l1, l2, lo = s.sem("e_l1"), s.sem("e_l2"), s.sem("e_out")
        a1, a2, dw, dx = s.sem("e_relu1"), s.sem("e_relu2"), s.sem("e_weighted"), s.sem("e_added")
        K = NEXP
        with nc.Block() as block:
            if beside:
                block.gpsimd(beside)

            @block.sync
            def _(sp):
                sp.dma_start(gT[:], dram.gate[:, :]).then_inc(gt_in, 16)
                for e in range(K):
                    sp.dma_start(gb[e][:], dram.gate[e, 0:T].partition_broadcast(P)).then_inc(gb_in[e], 16)
                with sp.Fori(1, NT) as t:
                    for e in range(K):
                        sp.wait_ge(dw, K * (t - 1) + e + 1)
                        sp.dma_start(gb[e][:], dram.gate[e, cols(t)].partition_broadcast(P)).then_inc(gb_in[e], 16)

            @block.tensor
            def _(pe):
                pe.wait_ge(w.loaded, w.total)
                pe.wait_ge(gt_in, 16)
                pe.wait_ge(dx, 1)
                with pe.Fori(0, NT) as t:
                    tile = [c.yn[:, k, cols(t)] for k in range(KH)]

                    def first(e):
                        pe.wait_ge(a1, K * t + e + 1)
                        for h in range(KH):
                            ins = product(nc, ps[2 * (e % 2) + h][:, 0:T], [w.W1[:, e, k, half(h)] for k in range(KH)], tile)
                        ins.then_inc(l1, 1)

                    def second(e):
                        pe.wait_ge(a1, K * t + e + 3)
                        pe.wait_ge(a2, K * t + e + 2)
                        for h in range(KH):
                            ins = product(nc, ps[4 + h][:, 0:T], [w.W2[:, e, k, half(h)] for k in range(KH)], [h1[:, e % 2, k, :] for k in range(KH)])
                        ins.then_inc(l2, 1)

                    def last(e):
                        if e == 0:
                            pe.wait_ge(dx, KH * t + 1)
                            for h in range(KH):
                                nc.tensor.matmul(ps[6 + h][:, 0:T], w.bo[:, half(h)], gT[:, cols(t)], start=True, stop=False)
                        pe.wait_ge(dw, K * t + e + 1)
                        for h in range(KH):
                            for k in range(KH):
                                ins = nc.tensor.matmul(ps[6 + h][:, 0:T], w.Wo[:, e, k, half(h)], hw[:, e % 2, k, :],
                                                       start=False, stop=(e == K - 1 and k == KH - 1))
                        ins.then_inc(lo, 1)

                    for e in range(K + 3):
                        if e < K:
                            first(e)
                        if 1 <= e <= K:
                            second(e - 1)
                        if e >= 3:
                            last(e - 3)

            @block.scalar
            def _(act):
                a = nc.scalar.activation
                act.sem_inc(a1, 2)
                act.sem_inc(a2, 2)
                with act.Fori(0, NT) as t:
                    for e in range(K + 1):
                        if e < K:
                            act.wait_ge(l1, K * t + e + 1)
                            if e >= 2:
                                act.wait_ge(l2, K * t + e - 1)
                            for h in range(KH):
                                ins = a(h1[:, e % 2, h, :], ps[2 * (e % 2) + h][:, 0:T], ACT.Relu,
                                        bias=w.shift[:, 0, h, e:e + 1], scale=w.scale[:, 0, h, e:e + 1])
                            ins.then_inc(a1, 1)
                        if e >= 1:
                            f = e - 1
                            act.wait_ge(l2, K * t + f + 1)
                            if f >= 2:
                                act.wait_ge(dw, K * t + f - 1)
                            for h in range(KH):
                                ins = a(h2[:, f % 2, h, :], ps[4 + h][:, 0:T], ACT.Relu,
                                        bias=w.shift[:, 1, h, f:f + 1], scale=w.scale[:, 1, h, f:f + 1])
                            ins.then_inc(a2, 1)

            @block.vector
            def _(dve):
                v = nc.vector
                dve.sem_inc(dx, 1)
                with dve.Fori(0, NT) as t:
                    for e in range(K):
                        dve.wait_ge(gb_in[e], 16 * (t + 1))
                        dve.wait_ge(a2, K * t + e + 3)
                        if e >= 2:
                            dve.wait_ge(lo, K * t + e - 1)
                        v.tensor_tensor(hw[:, e % 2], h2[:, e % 2], gb[e][:].unsqueeze(1).to_broadcast([P, KH, T]), ALU.mult).then_inc(dw, 1)
                    dve.wait_ge(lo, K * t + K)
                    for h in range(KH):
                        v.tensor_tensor(c.xT[:, h, cols(t)], c.xT[:, h, cols(t)], ps[6 + h][:, 0:T], ALU.add).then_inc(dx, 1)


def mix1(nc, c, w, qT, ctx):
    NQ = NT
    with Scope(nc, "mix1") as s:
        sq = s.sb("sq", [P, 2, KH, T])
        rr = s.sb("rr", [P, 2, T])
        kT = s.sb("kT", [P, NP])
        et = s.sb("et", [B, NB, P])
        vt = s.sb("vt", [B, NB, P])
        qt = s.sb("qt", [B, NB, P])
        mx8 = s.sb("mx8", [P, NT + 1])
        nmx = s.sb("nmx", [P, 1])
        sums = s.sb("sums", [P, 2])
        km = s.sb("km", [P, MEM])
        memT = s.sb("memT", [MEM, 2, P])
        qm = s.sb("qm", [B, NB * HEADS1])
        g16 = s.sb("g16", [P, KH])
        ps = c.ps
        at = lambda t: slice(t * T, (t + 1) * T)
        tok = lambda j: slice(B * j, B * (j + 1))
        own = s.sem("m1_steps")
        ss_done, sq_ready, sd_ready, xr_ready = s.sem("ss_done"), s.sem("m_sq"), s.sem("m_sd"), s.sem("xr_ready")
        k_done, k_out, qv_done, q_out, v_out = s.sem("k_done"), s.sem("k_out"), s.sem("qv_done"), s.sem("q_out"), s.sem("v_out")
        mx_ready, e_ready, et_turned, et_out = s.sem("mx_ready"), s.sem("e_ready"), s.sem("et_turned"), s.sem("et_out")
        q_ready, q_exp, q_norm, q_turned, qT_out = s.sem("q_ready"), s.sem("q_exp"), s.sem("q_norm"), s.sem("q_turned"), s.sem("qT_out")
        mem_turned, mem_out, ctx_done, ctx_ready = s.sem("mem_turned"), s.sem("mem_out"), s.sem("ctx_done"), s.sem("ctx_ready")
        w_ready = s.sem("w_ready")
        G4 = -(-NB // 4)
        with nc.Block() as block:
            @block.scalar
            def _(act):
                a = nc.scalar.activation
                for t in range(NT + 1):
                    if t < NT:
                        if t >= 2:
                            act.wait_ge(ss_done, t - 1)
                        a(sq[:, t % 2], c.yn[:, :, at(t)], ACT.Square).then_inc(sq_ready, 1)
                    if t >= 1:
                        act.wait_ge(ss_done, t)
                        if t >= 3:
                            act.wait_ge(xr_ready, t - 2)
                        a(rr[:, (t - 1) % 2], ps[(t - 1) % 2][:, 0:T], ACT.Sqrt).then_inc(sd_ready, 1)
                for j in range(NB):
                    act.wait_ge(qv_done, j + 1)
                    nc.scalar.copy(vt[:, j, :], ps[6 + j % 2][0:B, 0:P]).then_inc(v_out, 1)
                act.wait_ge(mx_ready, 1)
                a(kT[:, 0:N], kT[:, 0:N], ACT.Exp, bias=nmx[:, 0:1], accum_out=sums[:, 0:1]).then_inc(e_ready, 1)
                a(km[:], w.mk[:], ACT.Exp, bias=nmx[:, 0:1], accum_out=sums[:, 1:2]).then_inc(e_ready, 1)
                act.wait_ge(q_ready, 1)
                a(qt[:], qt[:], ACT.Exp).then_inc(q_exp, 1)
                for g in range(G4):
                    n = min(4, NB - 4 * g)
                    act.wait_ge(et_turned, g + 1)
                    nc.scalar.copy(et[:, 4 * g:4 * g + n, :], ps[g % 2][0:B, 0:n * P].rearrange("p (j d) -> p j d", d=P)).then_inc(et_out, 1)

            @block.vector
            def _(dve):
                v = nc.vector
                step = Steps(dve, own)
                dve.wait_ge(w.loaded, w.total)
                step(v.tensor_scalar(g16[:], w.gpre[:], float(D) ** 0.5, None, ALU.mult))
                for k in range(KH):
                    ins = v.tensor_scalar(w.mqkv[:, k, :], w.mqkv[:, k, :], g16[:, k:k + 1], None, ALU.mult)
                ins.then_inc(w_ready, 1)
                for t in range(NT):
                    r = rr[:, t % 2]
                    dve.wait_ge(sd_ready, t + 1)
                    step(v.tensor_scalar(r, r, 1e-12, None, ALU.max))
                    step(v.reciprocal(r, r))
                    v.tensor_tensor(c.a[:, 0, at(t)], c.yn[:, 0, at(t)], r, ALU.mult)
                    v.tensor_tensor(c.a[:, 1, at(t)], c.yn[:, 1, at(t)], r, ALU.mult).then_inc(xr_ready, 1)
                for t in range(NT):
                    dve.wait_ge(k_done, t + 1)
                    n = min(T, N - t * T)
                    v.tensor_copy(kT[:, at(t)], ps[2 + t % 2][:, 0:T])
                    v.tensor_reduce(mx8[:, t:t + 1], ps[2 + t % 2][:, 0:n], AX.X, ALU.max).then_inc(k_out, 1)
                for j in range(NB):
                    dve.wait_ge(qv_done, j + 1)
                    v.tensor_copy(qt[:, j, :], ps[4 + j % 2][0:B, 0:P]).then_inc(q_out, 1)
                v.tensor_reduce(mx8[:, NT:NT + 1], w.mk[:], AX.X, ALU.max).then_inc(k_out, 1)
                dve.wait_ge(k_out, NT + 1)
                step(v.tensor_reduce(nmx[:], mx8[:], AX.X, ALU.max))
                v.tensor_scalar(nmx[:], nmx[:], -1.0, None, ALU.mult).then_inc(mx_ready, 1)
                q3 = qt[:].rearrange("p j (h d) -> p (j h) d", d=HD1)
                wide = qm[:].unsqueeze(2).to_broadcast([B, NB * HEADS1, HD1])
                dve.wait_ge(q_out, NB)
                step(v.tensor_reduce(qm[:], q3, AX.X, ALU.max))
                v.tensor_tensor(q3, q3, wide, ALU.subtract).then_inc(q_ready, 1)
                dve.wait_ge(q_exp, 1)
                step(v.tensor_reduce(qm[:], q3, AX.X, ALU.add))
                step(v.reciprocal(qm[:], qm[:]))
                step(v.tensor_scalar(qm[:], qm[:], HD1 ** -0.5, None, ALU.mult))
                v.tensor_tensor(q3, q3, wide, ALU.mult).then_inc(q_norm, 1)
                step(v.memset(qT[:, N:NP], 0.0))
                step(v.memset(ctx[:], 0.0))
                dve.wait_ge(mem_turned, 1)
                v.tensor_copy(memT[:, 0, :], ps[2][0:MEM, 0:P])
                v.tensor_copy(memT[:, 1, :], ps[2][0:MEM, P:2 * P]).then_inc(mem_out, 1)
                for g in range(G4):
                    n = min(4, NB - 4 * g) * B
                    dve.wait_ge(q_turned, g + 1)
                    v.tensor_copy(qT[:, 4 * B * g:4 * B * g + n], ps[4 + g % 2][:, 0:n]).then_inc(qT_out, 1)
                dve.wait_ge(e_ready, 2)
                step(v.tensor_tensor(sums[:, 0:1], sums[:, 0:1], sums[:, 1:2], ALU.add))
                step(v.reciprocal(sums[:, 0:1], sums[:, 0:1]))
                dve.wait_ge(ctx_done, 1)
                for h in range(HEADS1):
                    r = slice(h * HD1, (h + 1) * HD1)
                    ins = v.tensor_scalar(ctx[r, r], ps[3][r, r], sums[r, 0:1], None, ALU.mult)
                ins.then_inc(ctx_ready, 1)

            @block.tensor
            def _(pe):
                mm = nc.tensor.matmul
                for t in range(NT):
                    pe.wait_ge(sq_ready, t + 1)
                    if t >= 2:
                        pe.wait_ge(sd_ready, t - 1)
                    product(nc, ps[t % 2][:, 0:T], [c.ones[:]] * KH, [sq[:, t % 2, k, :] for k in range(KH)]).then_inc(ss_done, 1)
                pe.wait_ge(w_ready, 1)
                H = HEADS1 * HD1
                for t in range(NT):
                    pe.wait_ge(xr_ready, t + 1)
                    if t >= 2:
                        pe.wait_ge(k_out, t - 1)
                    product(nc, ps[2 + t % 2][:, 0:T], [w.mqkv[:, k, H:2 * H] for k in range(KH)], [c.a[:, k, at(t)] for k in range(KH)]).then_inc(k_done, 1)
                for j in range(NB):
                    if j >= 2:
                        pe.wait_ge(q_out, j - 1)
                        pe.wait_ge(v_out, j - 1)
                    product(nc, ps[4 + j % 2][0:B, 0:P], [c.a[:, k, tok(j)] for k in range(KH)], [w.mqkv[:, k, 0:H] for k in range(KH)])
                    product(nc, ps[6 + j % 2][0:B, 0:P], [c.a[:, k, tok(j)] for k in range(KH)], [w.mqkv[:, k, 2 * H:3 * H] for k in range(KH)]).then_inc(qv_done, 1)
                pe.wait_ge(e_ready, 2)
                pe.wait_ge(k_out, NT)
                nc.tensor.transpose(ps[2][0:MEM, 0:P], km[:], c.ident[:])
                nc.tensor.transpose(ps[2][0:MEM, P:2 * P], w.mv[:], c.ident[:]).then_inc(mem_turned, 1)
                pe.wait_ge(sd_ready, NT)
                for g in range(G4):
                    n = min(4, NB - 4 * g)
                    if g >= 2:
                        pe.wait_ge(et_out, g - 1)
                    for i in range(n):
                        ins = nc.tensor.transpose(ps[g % 2][0:B, P * i:P * (i + 1)], kT[:, tok(4 * g + i)], c.ident[:])
                    ins.then_inc(et_turned, 1)
                pe.wait_ge(q_norm, 1)
                pe.wait_ge(q_out, NB)
                pe.wait_ge(v_out, NB)
                for g in range(G4):
                    n = min(4, NB - 4 * g)
                    if g >= 2:
                        pe.wait_ge(qT_out, g - 1)
                    for i in range(n):
                        ins = nc.tensor.transpose(ps[4 + g % 2][:, B * i:B * (i + 1)], qt[:, 4 * g + i, :], c.ident[0:B, 0:B])
                    ins.then_inc(q_turned, 1)
                pe.wait_ge(et_out, G4)
                pe.wait_ge(mem_out, 1)
                for j in range(NB):
                    mm(ps[3][:, 0:P], et[:, j, :], vt[:, j, :], start=(j == 0), stop=False)
                mm(ps[3][:, 0:P], memT[:, 0, :], memT[:, 1, :], start=False, stop=True).then_inc(ctx_done, 1)
                pe.wait_ge(ctx_ready, 1)
                pe.wait_ge(qT_out, G4)


def mix1_out(nc, c, w, qT, ctx):
    with Scope(nc, "mix1_out") as s:
        sq = s.sb("sq", [P, KH, T])
        rr = s.sb("rr", [P, T])
        yo = s.sb("yo", [P, KH, T])
        oT = s.sb("oT", [P, T])
        g16 = s.sb("g16", [P, KH])
        ps = c.ps
        own, pe_s, act_s = s.sem("mo_steps"), s.sem("mo_pe"), s.sem("mo_act")
        PE_N, ACT_N, DVE_N = 3, 2, 10
        with nc.Block() as block:
            @block.tensor
            def _(pe):
                with pe.Fori(0, NT) as t:
                    pe.wait_ge(own, DVE_N * t + 1)
                    product(nc, ps[4][:, 0:T], [ctx[:]], [qT[:, cols(t)]]).then_inc(pe_s, 1)
                    pe.wait_ge(own, DVE_N * t + 2)
                    for h in range(KH):
                        ins = product(nc, ps[h][:, 0:T], [w.wout[:, half(h)]], [oT[:]])
                    ins.then_inc(pe_s, 1)
                    pe.wait_ge(act_s, ACT_N * t + 1)
                    product(nc, ps[6][:, 0:T], [c.ones[:]] * KH, [sq[:, k, :] for k in range(KH)]).then_inc(pe_s, 1)

            @block.scalar
            def _(act):
                with act.Fori(0, NT) as t:
                    act.wait_ge(own, DVE_N * t + 4)
                    nc.scalar.activation(sq[:], yo[:], ACT.Square).then_inc(act_s, 1)
                    act.wait_ge(pe_s, PE_N * t + 3)
                    nc.scalar.activation(rr[:], ps[6][:, 0:T], ACT.Sqrt).then_inc(act_s, 1)

            @block.vector
            def _(dve):
                v = nc.vector
                step = Steps(dve, own)
                step(v.tensor_scalar(g16[:], w.gout[:], float(D) ** 0.5, None, ALU.mult))
                with dve.Fori(0, NT) as t:
                    step.turn(t, DVE_N)
                    step.n = 1
                    dve.wait_ge(pe_s, PE_N * t + 1)
                    step(v.tensor_copy(oT[:], ps[4][:, 0:T]))
                    dve.wait_ge(pe_s, PE_N * t + 2)
                    for h in range(KH):
                        step(v.tensor_scalar(yo[:, h, :], ps[h][:, 0:T], w.bout[:, h:h + 1], None, ALU.add))
                    dve.wait_ge(act_s, ACT_N * t + 2)
                    step(v.tensor_scalar(rr[:], rr[:], 1e-12, None, ALU.max))
                    step(v.reciprocal(rr[:], rr[:]))
                    for h in range(KH):
                        step(v.scalar_tensor_tensor(yo[:, h, :], yo[:, h, :], g16[:, h:h + 1], rr[:], ALU.mult, ALU.mult))
                    for h in range(KH):
                        step(v.tensor_tensor(yo[:, h, :], yo[:, h, :], c.yn[:, h, cols(t)], ALU.add))
                    step(v.tensor_tensor(c.xT[:, :, cols(t)], c.xT[:, :, cols(t)], yo[:], ALU.add))


def sage(nc, c, w, dram, src, out, layer):
    SG = 5
    JG = NB // SG
    with Scope(nc, f"sage{layer}") as s:
        zh = s.sb("zh", [B, NB, D], F16)
        zl = s.sb("zl", [B, NB, D], F16)
        adj = [s.sb(f"adj{g}", [B, JG, T], F16) for g in range(SG)]
        rd = s.sb("rd", [P, NP])
        u = s.sb("u", [P, KH, T])
        ps = c.ps
        z_done, zh_out, zl_out = s.sem("z_done"), s.sem("zh_out"), s.sem("zl_out")
        adj_in = [s.sem(f"adj_in{g}") for g in range(SG)]
        adj_used, rd_in = s.sem("adj_used"), s.sem("rd_in")
        summed, own_done, own = s.sem("summed"), s.sem("self_done"), s.sem("sage_steps")
        Wl, Wr, bl = w.gl[:, layer], w.gr[:, layer], w.gb[:, layer]
        DVE_N = 8
        with nc.Block() as block:
            @block.sync
            def _(sp):
                sp.wait_ge(own, 1)
                sp.dma_start(rd[:, 0:N], dram.rdeg[0:N].partition_broadcast(P)).then_inc(rd_in, 16)

                def load(t, g):
                    rows = dram.adj[B * JG * g:B * JG * (g + 1), cols(t)]
                    sp.dma_start(adj[g][:], rows.rearrange("(j p) d -> p j d", p=B)).then_inc(adj_in[g], 16)

                for g in range(SG):
                    load(0, g)
                with sp.Fori(1, NT) as t:
                    for g in range(SG):
                        sp.wait_ge(adj_used, SG * (t - 1) + g + 1)
                        load(t, g)

            @block.tensor
            def _(pe):
                mm = nc.tensor.matmul
                for j in range(NB):
                    if j >= 4:
                        pe.wait_ge(zl_out, j - 3)
                    product(nc, ps[j % 4][0:B, 0:D], [src[:, k, B * j:B * (j + 1)] for k in range(KH)],
                            [Wl[:, k, :] for k in range(KH)]).then_inc(z_done, 1)
                pe.wait_ge(zl_out, NB)
                with pe.Fori(0, NT) as t:
                    pe.wait_ge(own, DVE_N * t + 1)
                    for g in range(SG):
                        pe.wait_ge(adj_in[g], 16 * t + 16)
                        for j in range(JG):
                            for h in range(KH):
                                for z in (zh, zl):
                                    ins = mm(ps[4 + h][:, 0:T], z[:, g * JG + j, half(h)], adj[g][:, j, :],
                                             start=(g == 0 and j == 0 and z is zh), stop=(g == SG - 1 and j == JG - 1 and z is zl))
                        ins.then_inc(adj_used, 1)
                    for h in range(KH):
                        ins = product(nc, ps[6 + h][:, 0:T], [Wr[:, k, half(h)] for k in range(KH)], [src[:, k, cols(t)] for k in range(KH)])
                    ins.then_inc(own_done, 1)

            @block.scalar
            def _(act):
                for j in range(NB):
                    act.wait_ge(z_done, j + 1)
                    nc.scalar.copy(zh[:, j, :], ps[j % 4][0:B, 0:D]).then_inc(zh_out, 1)

            @block.vector
            def _(dve):
                v = nc.vector
                step = Steps(dve, own)
                step(v.memset(rd[:, N:NP], 0.0))
                for j in range(NB):
                    dve.wait_ge(zh_out, j + 1)
                    v.tensor_tensor(zl[:, j, :], ps[j % 4][0:B, 0:D], zh[:, j, :], ALU.subtract).then_inc(zl_out, 1)
                dve.wait_ge(rd_in, 16)
                with dve.Fori(0, NT) as t:
                    step.turn(t, DVE_N)
                    step.n = 1
                    at = cols(t)
                    dve.wait_ge(adj_used, SG * t + SG)
                    for h in range(KH):
                        step(v.tensor_tensor(u[:, h, :], ps[4 + h][:, 0:T], rd[:, at], ALU.mult))
                    dve.wait_ge(own_done, t + 1)
                    for h in range(KH):
                        step(v.scalar_tensor_tensor(u[:, h, :], ps[6 + h][:, 0:T], bl[:, h:h + 1], u[:, h, :], ALU.add, ALU.add))
                    for h in range(KH):
                        if layer < 2:
                            step(v.tensor_scalar(out[:, h, at], u[:, h, :], 0.0, None, ALU.max))
                        else:
                            step(v.tensor_tensor(out[:, h, at], out[:, h, at], u[:, h, :], ALU.add))
                    for h in range(2):
                        dve.sem_inc(own, 1)


def ffn1(nc, c, w, dram, out):
    M1 = HID1 // P
    with Scope(nc, "ffn1") as s:
        wrow = s.sb("wrow", [P, NP])
        sel = s.sb("sel", [P, NP])
        wc = s.sb("wc", [B, NB])
        rank = s.sb("rank", [B, 3, NB])
        junk = s.sb("junk", [B, 2, N], BF16)
        tie = s.sb("tie", [B, 2, B], BF16)
        ranked = s.sem("ranked")
        sT = s.sb("sT", [NB, B])
        hid = s.sb("hid", [P, M1, T])
        wrep = s.sb("wrep", [P, KH, P])
        ob = s.sb("ob", [B, 4, D])
        ps = c.ps
        own, sc_done, sc_out, wc_done, sel_done, sT_out, sel_st, sel_in = (s.sem(n) for n in (
            "f_steps", "sc_done", "sc_out", "wc_done", "sel_done", "sT_out", "sel_stored", "sel_in"))
        rep, f1, g1, f2, y_out, fin = (s.sem(n) for n in ("wrep_ready", "f_fc1", "f_gelu", "f_fc2", "y_out", "x_final"))
        turned, copied = s.sem("o_turned"), s.sem("o_copied")
        stored = [s.sem(f"o_stored{k}") for k in range(4)]
        at = lambda t: slice(t * T, (t + 1) * T)
        with nc.Block() as block:
            @block.tensor
            def _(pe):
                mm = nc.tensor.matmul
                pe.wait_ge(rep, 1)
                for t in range(NT):
                    if t >= 4:
                        pe.wait_ge(sc_out, t - 3)
                    product(nc, ps[t % 4][:, 0:T], [wrep[:, k, :] for k in range(KH)], [c.yn[:, k, at(t)] for k in range(KH)]).then_inc(sc_done, 1)
                pe.wait_ge(sc_out, NT)
                for j in range(NB):
                    ins = nc.tensor.transpose(ps[4][0:B, j:j + 1], wrow[0:1, B * j:B * (j + 1)], c.ident[0:1, 0:1])
                ins.then_inc(wc_done, 1)
                pe.wait_ge(own, 1)
                with pe.Fori(0, NT) as t:
                    tile = [c.yn[:, k, cols(t)] for k in range(KH)]
                    pe.wait_ge(y_out, KH * t + 1)

                    def up(m):
                        pe.wait_ge(g1, M1 * t + m + 1)
                        product(nc, ps[m % 6][:, 0:T], [w.w1[:, k, m * P:(m + 1) * P] for k in range(KH)], tile).then_inc(f1, 1)

                    def down(m):
                        pe.wait_ge(g1, M1 * t + m + 7)
                        for h in range(KH):
                            ins = mm(ps[6 + h][:, 0:T], w.w2[:, m, half(h)], hid[:, m, :], start=(m == 0), stop=(m == M1 - 1))
                        ins.then_inc(f2, 1)

                    for m in range(M1 + 2):
                        if m < M1:
                            up(m)
                        if m >= 2:
                            down(m - 2)
                pe.wait_ge(sel_done, 1)
                pe.wait_ge(y_out, KH * NT + 1)
                nc.tensor.transpose(ps[5][0:NB, 0:B], rank[:, 0, :], c.ident[0:B, 0:B]).then_inc(wc_done, 1)
                for j in range(NB):
                    pe.wait_ge(fin, min(NT, (B * (j + 1) - 1) // T + 1))
                    if j >= 4:
                        pe.wait_ge(copied, j - 3)
                    for h in range(KH):
                        ins = nc.tensor.transpose(ps[j % 4][0:B, half(h)], c.xT[:, h, B * j:B * (j + 1)], c.ident[:])
                    ins.then_inc(turned, 1)

            @block.scalar
            def _(act):
                act.sem_inc(g1, 6)
                with act.Fori(0, NT) as t:
                    act.wait_ge(f2, M1 * t + 1)
                    for m in range(M1):
                        act.wait_ge(f1, M1 * t + m + 1)
                        nc.scalar.activation(hid[:, m, :], ps[m % 6][:, 0:T], ACT.Gelu_apprx_tanh, bias=w.b1f[:, m:m + 1]).then_inc(g1, 1)
                    act.wait_ge(f2, M1 * t + M1 + 1)
                    for h in range(KH):
                        nc.scalar.activation(c.a[:, h, cols(t)], ps[6 + h][:, 0:T], ACT.Identity, bias=w.b2f[:, h:h + 1]).then_inc(y_out, 1)

            @block.sync
            def _(sp):
                sp.wait_ge(sT_out, 1)
                sp.dma_start(dram.sel.rearrange("(a p) -> a p", p=B), sT[:]).then_inc(sel_st, 16)
                sp.wait_ge(sel_st, 16)
                sp.dma_start(sel[:, 0:N], dram.sel.partition_broadcast(P)).then_inc(sel_in, 16)
                for j in range(NB):
                    sp.wait_ge(copied, j + 1)
                    sp.dma_start(out[B * j:B * (j + 1), :], ob[:, j % 4, :]).then_inc(stored[j % 4], 16)
                for k in range(4):
                    sp.wait_ge(stored[k], 16 * len(range(k, NB, 4)))

            @block.vector
            def _(dve):
                v = nc.vector
                step = Steps(dve, own)
                dve.sem_inc(f2, 1)
                dve.sem_inc(y_out, 1)
                v.memset(sel[:, N:NP], 0.0)
                dve.wait_ge(w.loaded, w.total)
                v.tensor_copy(wrep[:], w.wr1[:].to_broadcast([P, KH, P])).then_inc(rep, 1)
                for t in range(NT):
                    dve.wait_ge(sc_done, t + 1)
                    v.tensor_scalar(wrow[:, at(t)], ps[t % 4][:, 0:T], w.br1[:, 0:1], None, ALU.add).then_inc(sc_out, 1)
                dve.wait_ge(wc_done, 1)
                step(v.tensor_copy(wc[:], ps[4][0:B, 0:NB]))
                dve.wait_ge(sc_out, NT)
                step(v.memset(rank[:], 0.0))
                for j in range(NB):
                    me = wc[:, j:j + 1]
                    lo = B * j
                    if j >= 2:
                        dve.wait_ge(ranked, j - 1)
                    if j:
                        v.tensor_scalar(junk[:, j % 2, 0:lo], wrow[0:B, 0:lo], me, None, ALU.is_ge, ALU.add, accum_out=rank[:, 0, j:j + 1])
                    v.scalar_tensor_tensor(tie[:, j % 2, :], wrow[0:B, lo:lo + B], me, c.tri[:], ALU.is_equal, ALU.mult, accum_out=rank[:, 1, j:j + 1])
                    v.tensor_scalar(junk[:, j % 2, lo:N], wrow[0:B, lo:N], me, None, ALU.is_gt, ALU.add, accum_out=rank[:, 2, j:j + 1]).then_inc(ranked, 1)
                dve.wait_ge(ranked, NB)
                step(v.tensor_tensor(rank[:, 0], rank[:, 0], rank[:, 1], ALU.add))
                step(v.tensor_tensor(rank[:, 0], rank[:, 0], rank[:, 2], ALU.add))
                v.tensor_scalar(rank[:, 0], rank[:, 0], float(TOPK), None, ALU.is_lt).then_inc(sel_done, 1)
                dve.wait_ge(wc_done, 2)
                v.tensor_copy(sT[:], ps[5][0:NB, 0:B]).then_inc(sT_out, 1)
                dve.wait_ge(sel_in, 16)
                step(v.tensor_tensor(sel[:], sel[:], wrow[:], ALU.mult))
                dve.wait_ge(y_out, KH * NT + 1)
                for t in range(NT):
                    for h in range(KH):
                        ins = v.tensor_tensor(c.a[:, h, at(t)], c.a[:, h, at(t)], sel[:, at(t)], ALU.mult)
                    step(v.tensor_tensor(c.xT[:, :, at(t)], c.xT[:, :, at(t)], c.yn[:, :, at(t)], ALU.add))
                    v.tensor_tensor(c.xT[:, :, at(t)], c.xT[:, :, at(t)], c.a[:, :, at(t)], ALU.add).then_inc(fin, 1)
                for j in range(NB):
                    dve.wait_ge(turned, j + 1)
                    if j >= 4:
                        dve.wait_ge(stored[j % 4], 16 * (j // 4))
                    v.tensor_copy(ob[:, j % 4, :], ps[j % 4][0:B, 0:D]).then_inc(copied, 1)


class Names:
    pass


def load_weights(nc, s, w, plan):
    with nc.Block() as block:
        @block.sync
        def _(sp):
            with nc.allow_non_contiguous_dma(reason="weights in blocks of 128 rows"):
                for dst, src in plan:
                    sp.dma_start(dst, src).then_inc(w.loaded, 16)
    w.total = 16 * len(plan)


def rows128(a):
    return a.rearrange("(k p) m -> p k m", p=P)


def build(nc, i, out):
    dram = Names()
    internal = lambda name, shape, dt=F32: nc.dram_tensor(name, shape, dt, kind="Internal").ap()
    dram.adj = internal("adjacency", (N + 1, NP), F16)
    dram.adj_flat = dram.adj.rearrange("a (b o) -> (a b) o", o=1)
    dram.rows = internal("b_rows", (N, D))
    dram.runs = internal("run_max", (E, D))
    dram.keys = internal("edge_keys", (E,))
    dram.reset = internal("edge_resets", (E,), BF16)
    dram.rdeg = internal("degree_inverse", (N,))
    dram.gate = internal("gate_rows", (NEXP, NP))
    dram.sel = internal("selected", (N,))
    with Scope(nc, "all") as s:
        c = Names()
        c.ps = [s.enter_context(nc.psum_tensor(f"bank{b}", [P, 512], F32)) for b in range(8)]
        c.spare = s.sb("spare", [P, WC], I32)
        c.spare_f = s.sb("spare_f", [P, WC])
        c.row = s.sb("row", [P, P])
        c.row_b = s.sb("row_b", [B, B], BF16)
        c.ident = s.sb("ident", [P, P])
        c.upto = s.sb("upto", [P, P])
        c.before = s.sb("before", [B, 2 * WE - B], F16)
        c.tri = s.sb("tri", [B, B], BF16)
        c.cnt = s.sb("cnt", [B, EC])
        c.cell_idx = s.sb("cell_idx", [B, EC], I32)
        c.cell_val = s.sb("cell_val", [B, EC], F16)
        c.added = s.sem("cells_added")
        c.ones = s.sb("ones", [P, P])
        c.mean_w = s.sb("mean_w", [P, P])
        c.eps5 = s.sb("eps5", [P, 1])
        c.eps3 = s.sb("eps3", [P, 1])
        c.src_idx = s.sb("src_idx", [B, EC], I32)
        c.key_c = s.sb("key_c", [B, EC])
        c.has = s.sb("has", [B, NB])
        c.lack = s.sb("lack", [B, NB])
        c.last_idx = s.sb("last_idx", [B, NB], I32)
        c.xT = s.sb("xT", [P, KH, NP])
        c.yn = s.sb("yn", [P, KH, NP])
        c.a = s.sb("a", [P, KH, NP])
        c.attT = s.sb("attT", [P, KH, P])
        constants(nc, c)
        edges(nc, c, i.src, i.dst, dram)

        with Scope(nc, "w0") as g:
            w = Names()
            w.loaded = g.sem("w0_loaded")
            w.theta, w.phi = g.sb("theta", [P, KH, D]), g.sb("phi", [P, KH, D])
            w.qkv, w.fc1, w.fc2 = g.sb("qkv", [P, KH, 3 * D]), g.sb("fc1", [P, KH, HID0]), g.sb("fc2", [P, HID0 // P, D])
            w.bqkv_row = g.sb("bqkv_row", [1, 3 * D])
            w.tb, w.pb, w.bq, w.ng, w.nb, w.b2 = (g.sb(n, [P, KH]) for n in ("tb", "pb", "bq", "ng", "nb", "b2"))
            w.b1 = g.sb("b1", [P, HID0 // P])
            load_weights(nc, g, w, [
                (w.theta[:], rows128(i.theta)), (w.phi[:], rows128(i.phi)), (w.qkv[:], rows128(i.qkv)),
                (w.fc1[:], rows128(i.fc1)), (w.fc2[:], rows128(i.fc2)), (w.bqkv_row[:], i.bqkv_row),
                (w.tb[:], i.theta_b), (w.pb[:], i.phi_b), (w.bq[:], i.bqkv[:, 0:KH]), (w.ng[:], i.norm_g),
                (w.nb[:], i.norm_b), (w.b2[:], i.b_fc2), (w.b1[:], i.b_fc1)])
            nodes(nc, c, i.x, dram, w)
            edges_and_mix0(nc, c, dram, w)
        with Scope(nc, "w1") as g:
            w = Names()
            w.loaded = g.sem("w1_loaded")
            w.Wr, w.br, w.bo = g.sb("Wr", [P, KH, NEXP]), g.sb("br", [1, NEXP]), g.sb("bo", [NEXP, D])
            w.W1, w.W2, w.Wo = (g.sb(n, [P, NEXP, KH, D]) for n in ("W1", "W2", "Wo"))
            w.bn = g.sb("bn", [P, 2, 5, KH, NEXP])
            w.scale, w.shift = g.sb("scale", [P, 2, KH, NEXP]), g.sb("shift", [P, 2, KH, NEXP])
            blocks = lambda a: a.rearrange("e (k p) m -> p e k m", p=P)
            load_weights(nc, g, w, [
                (w.Wr[:], rows128(i.Wr)), (w.br[:], i.br), (w.bo[:], i.bo), (w.bn[:], i.bn),
                *((t[:, e], blocks(a)[:, e]) for t, a in ((w.W1, i.W1), (w.W2, i.W2), (w.Wo, i.Wo)) for e in range(NEXP))])
            join_max(nc, c, dram)
            norm(nc, c, c.yn, 1, lambda pool: add_cells(nc, c, dram, pool, 0, 7))
            fold(nc, c, w)
            gate(nc, c, w, dram, lambda pool: add_cells(nc, c, dram, pool, 7, 14))
            experts(nc, c, w, dram, lambda pool: add_cells(nc, c, dram, pool, 14, NW))
        norm(nc, c, c.yn, 2)
        with Scope(nc, "w2") as g:
            w = Names()
            w.loaded = g.sem("w2_loaded")
            H = HEADS1 * HD1
            w.mqkv, w.wout = g.sb("mqkv", [P, KH, 3 * H]), g.sb("wout", [P, D])
            w.mk, w.mv = g.sb("mk", [P, MEM]), g.sb("mv", [P, MEM])
            w.gpre, w.gout, w.bout = (g.sb(n, [P, KH]) for n in ("gpre", "gout", "bout"))
            load_weights(nc, g, w, [
                (w.mqkv[:], rows128(i.mqkv)), (w.wout[:], i.wout), (w.mk[:], i.mk), (w.mv[:], i.mv),
                (w.gpre[:], i.gpre), (w.gout[:], i.gout), (w.bout[:], i.bout)])
            qT = g.sb("qT", [P, NP])
            ctx = g.sb("ctx", [P, P])
            mix1(nc, c, w, qT, ctx)
            mix1_out(nc, c, w, qT, ctx)
        with Scope(nc, "w3") as g:
            w = Names()
            w.loaded = g.sem("w3_loaded")
            w.gl, w.gr, w.gb = g.sb("gl", [P, 3, KH, D]), g.sb("gr", [P, 3, KH, D]), g.sb("gbias", [P, 3, KH])
            load_weights(nc, g, w, [
                *((t[:, n], rows128(a[n])) for t, a in ((w.gl, i.gl), (w.gr, i.gr)) for n in range(3)), (w.gb[:], i.gb)])
            wait_for(nc, w)
            sage(nc, c, w, dram, c.yn, c.a, 0)
            sage(nc, c, w, dram, c.a, c.a, 1)
            sage(nc, c, w, dram, c.a, c.xT, 2)
        norm(nc, c, c.yn, 3)
        with Scope(nc, "w4") as g:
            w = Names()
            w.loaded = g.sem("w4_loaded")
            w.w1, w.w2 = g.sb("w1", [P, KH, HID1]), g.sb("w2", [P, HID1 // P, D])
            w.b1f, w.b2f = g.sb("b1f", [P, HID1 // P]), g.sb("b2f", [P, KH])
            w.wr1, w.br1 = g.sb("wr1", [P, KH, 1]), g.sb("br1", [P, 1])
            load_weights(nc, g, w, [
                (w.w1[:], rows128(i.w1)), (w.w2[:], rows128(i.w2)), (w.b1f[:], i.b1f), (w.b2f[:], i.b2f),
                (w.wr1[:], rows128(i.wr1)), (w.br1[:], i.br1.partition_broadcast(P))])
            ffn1(nc, c, w, dram, out)


def wait_for(nc, w):
    with nc.Block() as block:
        @block.tensor
        def _(pe):
            pe.wait_ge(w.loaded, w.total)

        @block.vector
        def _(dve):
            dve.wait_ge(w.loaded, w.total)


def kernel(**a):
    import numpy as np
    import concourse.bacc as bacc
    from concourse.bass_utils import run_bass_kernel_spmd as run

    nc = bacc.Bacc("TRN2", target_bir_lowering=False, num_devices=1)
    col = lambda v: v.reshape(-1, P).T
    bn = lambda n: np.stack([a[f"L0_ffn_{k}{n}"].reshape(NEXP, KH, P).transpose(2, 1, 0) for k in ("b", "g", "be", "m", "v")], axis=1)
    laid = {
        "x": a["x"], "src": a["src"], "dst": a["dst"],
        "theta": a["L0_gnn_theta_w"].T, "phi": a["L0_gnn_phi_w"].T,
        "theta_b": col(a["L0_gnn_theta_b"]), "phi_b": col(a["L0_gnn_phi_b"]),
        "qkv": a["L0_mix_w_qkv"], "bqkv": col(a["L0_mix_b_qkv"]), "bqkv_row": a["L0_mix_b_qkv"][None],
        "norm_g": col(a["L0_mix_norm_g"]), "norm_b": col(a["L0_mix_norm_b"]),
        "fc1": a["L0_mix_w_fc1"], "b_fc1": col(a["L0_mix_b_fc1"]), "fc2": a["L0_mix_w_fc2"], "b_fc2": col(a["L0_mix_b_fc2"]),
        "Wr": a["L0_ffn_Wr"], "br": a["L0_ffn_br"][None], "bo": a["L0_ffn_bo"],
        "W1": a["L0_ffn_W1"], "W2": a["L0_ffn_W2"], "Wo": a["L0_ffn_Wo"], "bn": np.stack([bn(1), bn(2)], axis=1),
        "gl": np.stack([a[f"L1_gnn_W{n}l"].T for n in (1, 2, 3)]), "gr": np.stack([a[f"L1_gnn_W{n}r"].T for n in (1, 2, 3)]),
        "gb": np.stack([col(a[f"L1_gnn_b{n}l"]) for n in (1, 2, 3)], axis=1),
        "mqkv": a["L1_mix_w_qkv"], "wout": a["L1_mix_w_out"], "mk": a["L1_mix_mem_kv"][0].reshape(P, MEM),
        "mv": a["L1_mix_mem_kv"][1].reshape(P, MEM), "gpre": col(a["L1_mix_g_pre"]), "gout": col(a["L1_mix_g_out"]),
        "bout": col(a["L1_mix_b_out"]),
        "w1": a["L1_ffn_w1"], "b1f": col(a["L1_ffn_b1"]), "w2": a["L1_ffn_w2"], "b2f": col(a["L1_ffn_b2"]),
        "wr1": a["L1_ffn_wr"], "br1": a["L1_ffn_br"],
    }
    arrays = {f"in_{k}": np.ascontiguousarray(v) for k, v in laid.items()}
    i = Names()
    for k, v in arrays.items():
        i.__dict__[k[3:]] = nc.dram_tensor(k, v.shape, mybir.dt.from_np(v.dtype), kind="ExternalInput").ap()
    out = nc.dram_tensor("out_x", (N, D), F32, kind="ExternalOutput").ap()
    build(nc, i, out)
    r = run(nc, [arrays], core_ids=[0])
    return r.results[0]["out_x"]
```

```python
from contextlib import ExitStack

import concourse.bass as bass
from concourse import mybir

F32 = mybir.dt.float32
F16 = mybir.dt.float16
BF16 = mybir.dt.bfloat16
I32 = mybir.dt.int32
ALU = mybir.AluOpType
ACT = mybir.ActivationFunctionType
AX = mybir.AxisListType

N = 3125
E = 50000
D = 256
P = 128
KH = D // P
B = 125
NB = N // B
T = 448
NT = -(-N // T)
NP = NT * T
EC = E // B
WS = 64.0
WC = 4
WE = WC * B
NW = EC // WC
EARLY = 44
HEADS0, HD0 = 4, 64
HEADS1, HD1, MEM = 4, 32, 4
HID0 = 3 * D
NEXP = 8
HID1 = 4 * D
TOPK = int(0.5 * N) - 1
BIG = 3.3895313892515355e38
ROUND = 12582912.0


class Steps:

    def __init__(self, eng, sem):
        self.eng, self.sem, self.base, self.n = eng, sem, 0, 0

    def __call__(self, ins):
        self.n += 1
        ins.then_inc(self.sem, 1)
        self.eng.wait_ge(self.sem, self.base + self.n)

    def turn(self, t, per_turn):
        self.base, self.n = t * per_turn, 0


class Scope(ExitStack):

    def __init__(self, nc, stage):
        super().__init__()
        self.nc, self.stage, self.sems = nc, stage, []

    def sb(self, name, shape, dt=F32):
        return self.enter_context(self.nc.sbuf_tensor(f"{self.stage}_{name}", shape, dt))

    def sem(self, name):
        self.sems.append(self.nc.alloc_semaphore(f"{self.stage}_{name}"))
        return self.sems[-1]

    def __exit__(self, *error):
        if self.sems and not error[0]:
            self.nc.clear_and_free_semaphores(self.sems)
            self.nc.all_engine_barrier()
        return super().__exit__(*error)


def constants(nc, c):
    with Scope(nc, "constants") as s:
        row_i = s.sb("row_i", [P, P], I32)
        col_i = s.sb("col_i", [P, 1], I32)
        col_f = s.sb("col_f", [P, 1])
        made = s.sem("iota_made")
        own = s.sem("const_steps")
        with nc.Block() as block:
            @block.gpsimd
            def _(pool):
                nc.gpsimd.iota(row_i[:], [[1, P]], base=0, channel_multiplier=0).then_inc(made, 1)
                nc.gpsimd.iota(col_i[:], [[0, 1]], base=0, channel_multiplier=1).then_inc(made, 1)
                nc.gpsimd.iota(c.spare[:], [[B, WC]], base=N * NP, channel_multiplier=1).then_inc(made, 1)

            @block.vector
            def _(dve):
                step = Steps(dve, own)
                v = nc.vector
                v.memset(c.ones[:], 1.0)
                v.memset(c.mean_w[:], 1.0 / D)
                dve.wait_ge(made, 3)
                v.tensor_copy(c.spare_f[:], c.spare[:])
                step(v.tensor_copy(c.row[:], row_i[:]))
                step(v.tensor_copy(col_f[:], col_i[:]))
                v.tensor_scalar(c.ident[:], c.row[:], col_f[:, 0:1], None, ALU.is_equal)
                v.tensor_scalar(c.upto[:], c.row[:], col_f[:, 0:1], None, ALU.is_ge)
                v.memset(c.before[:, WE:2 * WE - B], 1.0)
                v.memset(c.before[:, 0:WE - B], 1025.0)
                step(v.tensor_scalar(c.eps5[:], col_f[:, 0:1], 0.0, 1e-5, ALU.mult, ALU.add))
                step(v.tensor_scalar(c.tri[:], c.row[0:B, 0:B], col_f[0:B, 0:1], None, ALU.is_lt))
                step(v.tensor_scalar(c.before[:, WE - B:WE], c.tri[:], 1024.0, 1.0, ALU.mult, ALU.add))
                step(v.tensor_copy(c.row_b[:], c.row[0:B, 0:B]))


def cols(t, width=T):
    return bass.ds(t * width, width)


def half(h):
    return slice(h * P, (h + 1) * P)


def edges_and_nodes(nc, c, src, dst, x, dram, w, loads):
    A = EC // 100
    with Scope(nc, "start") as s:
        src_r = s.sb("src_r", [100, A, B], I32)
        dst_r = s.sb("dst_r", [100, A, B], I32)
        prev_r = s.sb("prev_r", [100, A, B], I32)
        f_r = s.sb("f_r", [100, 3, A, B])
        same = prev_r[:].bitcast(F32)
        reset = s.sb("reset", [100, A, B], BF16)
        dst_c = s.sb("dst_c", [B, EC])
        hi = s.sb("hi", [B, EC])
        hi_r = s.sb("hi_r", [B, EC])
        lo = s.sb("lo", [B, EC])
        free = c.a.rearrange("p k n -> p (k n)")
        oh_hi = free[0:B, 0:EC * NB // 2].bitcast(BF16).rearrange("p (e n) -> p e n", n=NB)
        free = free[:, EC * NB // 2:]
        uu = free[:, 0:KH * D].rearrange("p (k f) -> p k f", f=D)
        gram = free[:, KH * D:KH * D + KH * (D + 1)].rearrange("p (k f) -> p k f", f=D + 1)
        oh_lo = s.sb("oh_lo", [B, 2, 16, B], BF16)
        deg = s.sb("deg", [B, NB])
        tot = s.sb("tot", [B, NB])
        off = s.sb("off", [B, NB])
        last = s.sb("last", [B, NB])
        rdeg = s.sb("rdeg", [B, NB])
        rdeg_t = s.sb("rdeg_t", [NB, B])
        zero = s.sb("zero", [B, NP], F16)
        xt = s.sb("xt", [B, NB, D])
        xn = s.sb("xn", [B, NB, D + 1])
        stats = s.sb("stats", [B, NB, 6])
        mv = s.sb("mv", [B, NB, 2])
        sd = s.sb("sd", [B, NB])
        rs = s.sb("rs", [B, NB])
        wb = s.sb("wb", [P, KH, D])
        bo = s.sb("bo", [B, 4, D])
        csum = s.sb("csum", [1, D])
        rr = s.sb("rr", [1, D])
        cnt = s.sb("cnt", [1, 1])
        gs = s.sb("gs", [P, KH, P])
        mx = s.sb("mx", [P, KH])
        sm = s.sb("sm", [P, KH])
        att = s.sb("att", [P, KH, P])
        ps = c.ps
        edges_in = s.sem("edges_loaded")
        prev0 = s.sem("prev_cleared")
        rows_ready = s.sem("rows_ready")
        cols_turned, cols_out = s.sem("cols_turned"), s.sem("cols_out")
        hot_ready = s.sem("onehot_ready")
        hot_used = s.sem("onehot_used")
        deg_ready = s.sem("deg_ready")
        cum = s.sem("cum_done")
        rd = s.sem("rdeg_ready")
        rdt = s.sem("rdeg_turned")
        rdo = s.sem("rdeg_row_ready")
        stored = s.sem("edges_stored")
        z_ready = s.sem("zero_ready")
        zeroed = s.sem("adj_zeroed")
        HOT = 16
        NH = EC // HOT
        view = lambda a: a.rearrange("(a c p) -> c a p", c=100, p=B)
        x_in = s.sem("x_loaded")
        own = s.sem("node_steps")
        var_ready, sd_ready = s.sem("var_ready"), s.sem("sd_ready")
        xn_ready = s.sem("xn_ready")
        turned, taken = s.sem("turned"), s.sem("taken")
        gram_done, gram_out = s.sem("gram_done"), s.sem("gram_out")
        b_done, b_out = s.sem("b_done"), s.sem("b_out")
        b_stored = [s.sem(f"b_stored{k}") for k in range(4)]
        wb_ready = s.sem("wb_ready")
        att_pe, att_v, att_a = s.sem("att_pe"), s.sem("att_v"), s.sem("att_a")
        G4 = -(-NB // 4)
        groups = [(g, min(4, NB - 4 * g)) for g in range(G4)]
        assert NH == NB
        with nc.Block() as block:
            @block.sync
            def _(sp):
                with nc.allow_non_contiguous_dma(reason="rows of 500 bytes, blocks of 128 rows of weights"):
                    sp.dma_start(src_r[:], view(src)).then_inc(edges_in, 16)
                    sp.dma_start(dst_r[:], view(dst)).then_inc(edges_in, 16)
                    sp.wait_ge(prev0, 1)
                    sp.dma_start(prev_r[0:1, 0, 1:B], dst[0:B - 1].rearrange("(o p) -> o p", o=1)).then_inc(edges_in, 16)
                    sp.dma_start(prev_r[1:100, 0, :], dst[B - 1:B - 1 + 99 * B].rearrange("(c p) -> c p", p=B)).then_inc(edges_in, 16)
                    sp.dma_start(prev_r[:, 1:A, :], dst[100 * B - 1:E - 1].rearrange("(a c p) -> c a p", c=100, p=B)).then_inc(edges_in, 16)
                    sp.dma_start(xt[:], x.rearrange("(j p) f -> p j f", p=B)).then_inc(x_in, 16)
                    for to, from_ in loads:
                        sp.dma_start(to, from_).then_inc(w.loaded, 16)
                    sp.wait_ge(z_ready, 1)
                    for j in range(NB):
                        sp.dma_start(dram.adj[B * j:B * (j + 1), :], zero[:]).then_inc(zeroed, 16)
                    sp.dma_start(dram.adj[N:N + 1, :], zero[0:1, :]).then_inc(zeroed, 16)
                    sp.wait_ge(rows_ready, 2)
                    sp.dma_start(view(dram.keys), f_r[:, 2]).then_inc(stored, 16)
                    sp.dma_start(view(dram.reset), reset[:]).then_inc(stored, 16)
                    for j in range(NB):
                        sp.wait_ge(b_out, j + 1)
                        sp.dma_start(dram.rows[B * j:B * (j + 1), :], bo[:, j % 4, :]).then_inc(b_stored[j % 4], 16)
                    sp.wait_ge(rdo, 1)
                    sp.dma_start(dram.rdeg[0:N].rearrange("(a p) -> a p", p=B), rdeg_t[:]).then_inc(stored, 16)
                    sp.dma_start(dram.rdeg[N:NP].rearrange("(o p) -> o p", o=1), c.ones[0:1, 0:NP - N]).then_inc(stored, 16)
                    sp.wait_ge(stored, 64)
                    sp.wait_ge(zeroed, 16 * (NB + 1))
                    for k in range(4):
                        sp.wait_ge(b_stored[k], 16 * len(range(k, NB, 4)))

            @block.scalar
            def _(act):
                act.wait_ge(var_ready, 1)
                nc.scalar.activation(sd[:], mv[:, :, 1], ACT.Sqrt, bias=c.eps5[0:B, 0:1]).then_inc(sd_ready, 1)
                for g, n in groups:
                    for k, (out, h) in enumerate(((c.xT, 0), (c.xT, 1), (c.yn, 0), (c.yn, 1))):
                        act.wait_ge(turned, 4 * g + k + 1)
                        nc.scalar.copy(out[:, h, 4 * B * g:4 * B * g + n * B], ps[k][:, 0:n * B]).then_inc(taken, 1)
                for j in range(NB):
                    act.wait_ge(b_done, j + 1)
                    if j >= 4:
                        act.wait_ge(b_stored[j % 4], 16 * (j // 4))
                    nc.scalar.copy(bo[:, j % 4, :], ps[j % 4][0:B, 0:D]).then_inc(b_out, 1)
                act.wait_ge(att_v, 2)
                nc.scalar.activation(att[:], gs[:], ACT.Exp).then_inc(att_a, 1)

            @block.vector
            def _(dve):
                step = Steps(dve, own)
                v = nc.vector
                v.memset(prev_r[:], -1).then_inc(prev0, 1)
                v.memset(zero[:], 0.0).then_inc(z_ready, 1)
                v.memset(c.xT[:, :, N:NP], 0.0)
                v.memset(c.yn[:, :, N:NP], 0.0)
                v.memset(cnt[:], float(N))
                step(v.memset(xn[:, :, D:D + 1], 1.0))
                dve.wait_ge(edges_in, 80)
                v.tensor_copy(f_r[:, 0], src_r[:])
                step(v.tensor_copy(f_r[:, 1], dst_r[:]))
                step(v.scalar_tensor_tensor(f_r[:, 2], f_r[:, 0], float(NP), f_r[:, 1], ALU.mult, ALU.add))
                dve.sem_inc(rows_ready, 1)
                step(v.tensor_tensor(same[:], dst_r[:], prev_r[:], ALU.is_equal))
                step(v.tensor_scalar(same[:], same[:], 2.0, 1.0, ALU.mult, ALU.subtract))
                v.tensor_scalar(reset[:], same[:], BIG, None, ALU.mult).then_inc(rows_ready, 1)
                dve.wait_ge(x_in, 16)
                for j in range(NB):
                    ins = v.bn_stats(stats[:, j, :], xt[:, j, :])
                step(ins)
                for j in range(NB):
                    ins = v.bn_aggr(mv[:, j, :], stats[:, j, :])
                ins.then_inc(var_ready, 1)
                dve.wait_ge(cols_turned, 1)
                v.tensor_copy(c.src_idx[:], ps[0][0:B, 0:EC])
                v.tensor_copy(c.key_c[:], ps[2][0:B, 0:EC])
                step(v.tensor_copy(dst_c[:], ps[1][0:B, 0:EC]))
                dve.sem_inc(cols_out, 1)
                dve.wait_ge(sd_ready, 1)
                dve.wait_ge(var_ready, 1)
                step(v.reciprocal(rs[:], sd[:]))
                for j in range(NB):
                    v.tensor_scalar(xn[:, j, 0:D], xt[:, j, :], mv[:, j, 0:1], rs[:, j:j + 1],
                                    ALU.subtract, ALU.mult).then_inc(xn_ready, 1)
                step(v.tensor_scalar(hi[:], dst_c[:], (B - 1) / 2.0, 1.0 / B, ALU.subtract, ALU.mult))
                step(v.tensor_scalar(hi_r[:], hi[:], ROUND, None, ALU.add))
                step(v.tensor_scalar(hi[:], hi_r[:], ROUND, None, ALU.subtract))
                step(v.scalar_tensor_tensor(lo[:], hi[:], -float(B), dst_c[:], ALU.mult, ALU.add))
                dve.wait_ge(w.loaded, w.total)
                v.tensor_tensor(wb[:], w.phi[:], w.theta[:], ALU.subtract).then_inc(wb_ready, 1)
                step(v.tensor_tensor(oh_hi[:], hi[:].unsqueeze(2).to_broadcast([B, EC, NB]),
                                     c.row[0:B, 0:NB].unsqueeze(1).to_broadcast([B, EC, NB]), ALU.is_equal))
                for g in range(NH):
                    if g >= 2:
                        dve.wait_ge(hot_used, g - 1)
                    v.tensor_tensor(oh_lo[:, g % 2], lo[:, g * HOT:(g + 1) * HOT].unsqueeze(2).to_broadcast([B, HOT, B]),
                                    c.row_b[:].unsqueeze(1).to_broadcast([B, HOT, B]), ALU.is_equal).then_inc(hot_ready, 1)
                dve.wait_ge(hot_used, NH)
                step(v.tensor_copy(deg[:], ps[7][0:B, 0:NB]))
                v.tensor_scalar(c.has[:], deg[:], 0.0, None, ALU.is_gt)
                v.tensor_scalar(rdeg[:], deg[:], 1.0, None, ALU.max).then_inc(deg_ready, 1)
                dve.wait_ge(deg_ready, 1)
                step(v.tensor_scalar(c.lack[:], c.has[:], 1.0, BIG, ALU.subtract, ALU.mult))
                v.reciprocal(rdeg[:], rdeg[:]).then_inc(rd, 1)
                dve.wait_ge(gram_done, 1)
                v.tensor_copy(gram[:, 0, :], ps[4][:, 0:D + 1])
                v.tensor_copy(gram[:, 1, :], ps[5][:, 0:D + 1])
                v.tensor_copy(csum[:], ps[6][0:1, 0:D]).then_inc(gram_out, 1)
                dve.wait_ge(cum, 1)
                dve.wait_ge(rdt, 1)
                step(v.tensor_copy(tot[:], ps[7][0:B, P:P + NB]))
                step(v.tensor_tensor_scan(off[:], tot[:], tot[:], 0.0, ALU.add, ALU.max))
                step(v.tensor_tensor(off[:], off[:], tot[:], ALU.subtract))
                step(v.tensor_tensor(last[:], off[:], ps[7][0:B, 0:NB], ALU.add))
                v.tensor_copy(rdeg_t[:], ps[7][0:NB, 2 * P:2 * P + B]).then_inc(rdo, 1)
                step(v.tensor_scalar(last[:], last[:], 1.0, 0.0, ALU.subtract, ALU.max))
                step(v.tensor_copy(c.last_idx[:], last[:]))
                dve.wait_ge(att_pe, 1)
                v.tensor_copy(uu[:, 0, :], ps[0][:, 0:D])
                v.tensor_copy(uu[:, 1, :], ps[1][:, 0:D])
                v.tensor_copy(rr[:], ps[2][0:1, 0:D]).then_inc(att_v, 1)
                dve.wait_ge(att_pe, 2)
                scale = HD0 ** -0.5
                v.tensor_scalar(gs[:, 0, :], ps[3][:, 0:P], scale, None, ALU.mult)
                step(v.tensor_scalar(gs[:, 1, :], ps[4][:, P:2 * P], scale, None, ALU.mult))
                for h in range(KH):
                    for q in range(2):
                        r = slice(q * HD0, (q + 1) * HD0)
                        ins = v.tensor_reduce(mx[r, h:h + 1], gs[r, h, r], AX.X, ALU.max)
                step(ins)
                step(v.tensor_copy(sm[:], mx[:]))
                for h in range(KH):
                    ins = v.tensor_scalar(gs[:, h, :], gs[:, h, :], mx[:, h:h + 1], 0.0, ALU.subtract, ALU.min)
                ins.then_inc(att_v, 1)
                dve.wait_ge(att_a, 1)
                for h in range(KH):
                    v.memset(att[0:HD0, h, HD0:P], 0.0)
                    step(v.memset(att[HD0:P, h, 0:HD0], 0.0))
                step(v.tensor_reduce(sm[:], att[:], AX.X, ALU.add))
                step(v.reciprocal(sm[:], sm[:]))
                for h in range(KH):
                    ins = v.tensor_scalar(att[:, h, :], att[:, h, :], sm[:, h:h + 1], None, ALU.mult)
                ins.then_inc(att_v, 1)
                dve.wait_ge(att_pe, 3)
                v.tensor_copy(c.attT[:, 0, :], ps[0][:, 0:P])
                v.tensor_copy(c.attT[:, 1, :], ps[1][:, 0:P])

            @block.tensor
            def _(pe):
                mm = nc.tensor.matmul
                pe.wait_ge(rows_ready, 1)
                for k in range(3):
                    for a in range(A):
                        ins = nc.tensor.transpose(ps[k][0:B, 100 * a:100 * (a + 1)], f_r[:, k, a, :], c.ident[0:100, 0:100])
                ins.then_inc(cols_turned, 1)
                pe.wait_ge(cols_out, 1)
                for g, n in groups:
                    pe.wait_ge(xn_ready, 4 * g + n)
                    for k, (a, h) in enumerate(((xt, 0), (xt, 1), (xn, 0), (xn, 1))):
                        if g >= 1:
                            pe.wait_ge(taken, 4 * (g - 1) + k + 1)
                        for i in range(n):
                            ins = nc.tensor.transpose(ps[k][:, B * i:B * (i + 1)], a[:, 4 * g + i, half(h)], c.ident[0:B, 0:B])
                        ins.then_inc(turned, 1)
                pe.wait_ge(taken, 4 * G4)
                pe.wait_ge(wb_ready, 1)
                for j in range(NB):
                    if j >= 4:
                        pe.wait_ge(b_out, j - 3)
                    for k in range(KH):
                        ins = mm(ps[j % 4][0:B, 0:D], c.yn[:, k, B * j:B * (j + 1)], wb[:, k, :], start=(k == 0), stop=(k == KH - 1))
                    ins.then_inc(b_done, 1)
                    for h in range(KH):
                        mm(ps[4 + h][:, 0:D + 1], xn[:, j, half(h)], xn[:, j, :], start=(j == 0), stop=(j == NB - 1))
                    ins = mm(ps[6][0:1, 0:D], c.ones[0:B, 0:1], xn[:, j, 0:D], start=(j == 0), stop=(j == NB - 1))
                    if j == NB - 1:
                        ins.then_inc(gram_done, 1)
                    pe.wait_ge(hot_ready, j + 1)
                    for k in range(HOT):
                        e = j * HOT + k
                        ins = mm(ps[7][0:B, 0:NB], oh_lo[:, j % 2, k, :], oh_hi[:, e, :], start=(e == 0), stop=(e == EC - 1))
                    ins.then_inc(hot_used, 1)
                pe.wait_ge(deg_ready, 1)
                mm(ps[7][0:B, 0:NB], c.upto[0:B, 0:B], deg[:], start=True, stop=True)
                mm(ps[7][0:B, P:P + NB], c.ones[0:B, 0:B], deg[:], start=True, stop=True).then_inc(cum, 1)
                pe.wait_ge(rd, 1)
                nc.tensor.transpose(ps[7][0:NB, 2 * P:2 * P + B], rdeg[:], c.ident[0:B, 0:B]).then_inc(rdt, 1)
                pe.wait_ge(gram_out, 1)
                pe.wait_ge(b_out, NB)
                for h in range(KH):
                    for k in range(KH):
                        mm(ps[h][:, 0:D], gram[:, k, half(h)], w.qkv[:, k, 2 * D:3 * D], start=(k == 0), stop=False)
                    mm(ps[h][:, 0:D], csum[0:1, half(h)], w.bqkv_row[0:1, 2 * D:3 * D], start=False, stop=True)
                for k in range(KH):
                    mm(ps[2][0:1, 0:D], gram[:, k, D:D + 1], w.qkv[:, k, 2 * D:3 * D], start=(k == 0), stop=False)
                mm(ps[2][0:1, 0:D], cnt[0:1, 0:1], w.bqkv_row[0:1, 2 * D:3 * D], start=False, stop=True).then_inc(att_pe, 1)
                pe.wait_ge(att_v, 1)
                for h in range(KH):
                    for k in range(KH):
                        mm(ps[3 + h][:, 0:D], w.qkv[:, k, D + h * P:D + (h + 1) * P], uu[:, k, :], start=(k == 0), stop=False)
                    ins = mm(ps[3 + h][:, 0:D], w.bqkv_row[0:1, D + h * P:D + (h + 1) * P], rr[0:1, :], start=False, stop=True)
                ins.then_inc(att_pe, 1)
                pe.wait_ge(att_v, 3)
                for h in range(KH):
                    ins = nc.tensor.transpose(ps[h][:, 0:P], att[:, h, :], c.ident[:])
                ins.then_inc(att_pe, 1)


def edges_and_mix0(nc, c, dram, w):
    SLOTS = NW // NT
    SETS = SLOTS // 2
    COUNTS = (0, 4, 6, 8, 10, 11)
    assert SLOTS == 14 and len(COUNTS) * NT + 2 == EARLY and N * NP + WE < 1 << 24
    M1 = HID0 // P
    with Scope(nc, "mix0") as s:
        got = [s.sb(f"got{i}", [B, D]) for i in range(SETS * WC)]
        rst = s.sb("rst", [P, 2, WE], BF16)
        scan = s.sb("scan", [P, 2, KH, WE])
        back = s.sb("back", [B, 2, WC, D])
        krow = s.sb("krow", [B, 2, WE])
        junk = s.sb("junk", [B, 2, WE], F16)
        cell = s.sb("cell", [B, WC * EARLY])
        dup = s.sb("dup", [B, WC * EARLY])
        q = s.sb("q", [P, KH, T])
        sx = s.sb("sx", [P, KH, T])
        cen = s.sb("cen", [P, KH, T])
        sd = s.sb("sd", [P, T])
        hn = s.sb("hn", [P, KH, T])
        hid = s.sb("hid", [P, M1, T])
        ab = s.sb("ab", [P, KH])
        ps = c.ps
        gathered = [s.sem(f"gathered{i}") for i in range(SETS * WC)]
        rst_in = [s.sem(f"rst_in{b}") for b in range(2)]
        krow_in = [s.sem(f"krow_in{b}") for b in range(2)]
        stored = [s.sem(f"run_stored{b}") for b in range(2)]
        turned, scanned, turned_back, copied = s.sem("turned"), s.sem("scanned"), s.sem("turned_back"), s.sem("copied")
        counted, own_c = s.sem("counted"), s.sem("count_steps")
        pe_done, act_done, own = s.sem("mix_pe"), s.sem("mix_act"), s.sem("mix_steps")
        PE_N, ACT_N, DVE_N = 7 + M1, 3 + M1, 14
        runs = dram.runs.rearrange("(w c p) f -> w p c f", c=WC, p=B)
        with nc.Block() as block:
            @block.gpsimd
            def _(pool):
                for n in range(NW):
                    for j in range(WC):
                        if n >= SETS:
                            pool.wait_ge(turned, WC * (n - SETS) + j + 1)
                        i, k = WC * (n % SETS) + j, WC * n + j
                        nc.gpsimd.indirect_dma_start(got[i][:, :], None, dram.rows[:, :],
                                                     bass.IndirectOffsetOnAxis(ap=c.src_idx[:, k:k + 1], axis=0)).then_inc(gathered[i], 16)

            @block.sync
            def _(sp):
                def store(n, b):
                    sp.wait_ge(copied, 2 * n + 4)
                    sp.dma_start(runs[bass.ds(n, 1)].rearrange("o p c f -> (o p) c f"), back[:, b]).then_inc(stored[b], 16)

                for b in range(2):
                    sp.sem_inc(stored[b], 16)
                    sp.wait_ge(scanned, 2)
                    sp.dma_start(rst[:, b, :], dram.reset[b * WE:(b + 1) * WE].partition_broadcast(P)).then_inc(rst_in[b], 16)
                    sp.dma_start(krow[:, b, :], dram.keys[b * WE:(b + 1) * WE].partition_broadcast(B)).then_inc(krow_in[b], 16)
                with sp.Fori(0, NT) as t:
                    for k in range(SLOTS):
                        n, b = SLOTS * t + k, k % 2
                        store(n, b)
                        sp.dma_start(rst[:, b, :], dram.reset[bass.ds((n + 2) * WE, WE)].partition_broadcast(P)).then_inc(rst_in[b], 16)
                        if k - 1 in COUNTS:
                            r = COUNTS.index(k - 1)
                            q = len(COUNTS) * t + r + 2
                            sp.dma_start(krow[:, r % 2, :], dram.keys[bass.ds(q * WE, WE)].partition_broadcast(B)).then_inc(krow_in[r % 2], 16)
                for b in range(2):
                    store(NW - 2 + b, b)
                for b in range(2):
                    sp.wait_ge(stored[b], 16 * (NW // 2 + 1))

            @block.tensor
            def _(pe):
                def forward(n, b, i, loads):
                    pe.wait_ge(scanned, 2 * n + 2)
                    for j in range(WC):
                        pe.wait_ge(gathered[WC * i + j], 16 * loads)
                        for h in range(KH):
                            ins = nc.tensor.transpose(ps[2 * b + h][:, B * j:B * (j + 1)], got[WC * i + j][:, half(h)], c.ident[0:B, 0:B])
                        ins.then_inc(turned, 1)

                def backward(n, b):
                    pe.wait_ge(scanned, 2 * n + 6)
                    pe.wait_ge(copied, 2 * n + 2)
                    for j in range(WC):
                        for h in range(KH):
                            at = D * (j % 2) + P * h
                            ins = nc.tensor.transpose(ps[4 + j // 2][0:B, at:at + P], scan[:, b, h, B * j:B * (j + 1)], c.ident[:])
                        if j % 2:
                            ins.then_inc(turned_back, 1)

                def piece(t, k):
                    tile = [c.yn[:, i, cols(t)] for i in range(KH)]
                    pe_wait = lambda sem, per, n: pe.wait_ge(sem, t * per + n)
                    if k == 0:
                        pe_wait(own, DVE_N, 1)
                        for h in range(KH):
                            ins = product(nc, ps[6 + h][:, 0:T], [w.qkv[:, i, half(h)] for i in range(KH)], tile)
                        ins.then_inc(pe_done, 1)
                    elif k == 1:
                        pe_wait(act_done, ACT_N, 1)
                        for h in range(KH):
                            ins = product(nc, ps[6 + h][:, 0:T], [w.theta[:, i, half(h)] for i in range(KH)], tile)
                        ins.then_inc(pe_done, 1)
                    elif k == 2:
                        pe_wait(own, DVE_N, 3)
                        for h in range(KH):
                            ins = product(nc, ps[6 + h][:, 0:T], [c.attT[:, h, :]], [q[:, h, :]])
                        ins.then_inc(pe_done, 1)
                    elif k == 3:
                        pe_wait(own, DVE_N, 5)
                        product(nc, ps[6][:, 0:T], [c.mean_w[:]] * KH, [sx[:, i, :] for i in range(KH)]).then_inc(pe_done, 1)
                    elif k == 4:
                        pe_wait(act_done, ACT_N, 2)
                        product(nc, ps[7][:, 0:T], [c.mean_w[:]] * KH, [hid[:, i, :] for i in range(KH)]).then_inc(pe_done, 1)
                    elif 6 <= k < 6 + M1:
                        m = k - 6
                        if m == 0:
                            pe_wait(own, DVE_N, 12)
                        if m >= 2:
                            pe_wait(act_done, ACT_N, 3 + m - 1)
                        product(nc, ps[6 + m % 2][:, 0:T], [w.fc1[:, i, m * P:(m + 1) * P] for i in range(KH)],
                                [hn[:, i, :] for i in range(KH)]).then_inc(pe_done, 1)
                    elif k >= 6 + M1:
                        h = k - 6 - M1
                        pe_wait(act_done, ACT_N, 3 + M1)
                        product(nc, ps[6 + h][:, 0:T], [w.fc2[:, m, half(h)] for m in range(M1)],
                                [hid[:, m, :] for m in range(M1)]).then_inc(pe_done, 1)

                pe.sem_inc(turned_back, 4)
                with pe.Fori(0, NT) as t:
                    for k in range(SLOTS):
                        forward(SLOTS * t + k, k % 2, k % SETS, 2 * t + k // SETS + 1)
                        piece(t, k)
                        backward(SLOTS * t + k, k % 2)
                for n in range(SLOTS * NT, NW):
                    forward(n, n % 2, n % SETS, n // SETS + 1)
                    backward(n, n % 2)

            @block.scalar
            def _(act):
                a = nc.scalar.activation

                def copy(n, b):
                    act.wait_ge(stored[b], 8 * (n - b) + 16)
                    for i in range(2):
                        act.wait_ge(turned_back, 2 * n + 5 + i)
                        nc.scalar.copy(back[:, b, 2 * i:2 * i + 2, :], ps[4 + i][0:B, 0:2 * D]).then_inc(copied, 1)

                def piece(t, k):
                    if k == 0:
                        act.wait_ge(pe_done, t * PE_N + 1)
                        for h in range(KH):
                            ins = a(q[:, h, :], ps[6 + h][:, 0:T], ACT.Identity, bias=w.bq[:, h:h + 1])
                        ins.then_inc(act_done, 1)
                    elif k == 3:
                        act.wait_ge(own, t * DVE_N + 7)
                        a(hid[:, 0:KH, :], cen[:], ACT.Square).then_inc(act_done, 1)
                    elif k == 4:
                        act.wait_ge(pe_done, t * PE_N + 5)
                        a(sd[:], ps[7][:, 0:T], ACT.Sqrt, bias=c.eps5[:, 0:1]).then_inc(act_done, 1)
                    elif 6 <= k < 6 + M1:
                        m = k - 6
                        act.wait_ge(pe_done, t * PE_N + 6 + m)
                        a(hid[:, m, :], ps[6 + m % 2][:, 0:T], ACT.Gelu, bias=w.b1[:, m:m + 1]).then_inc(act_done, 1)

                act.sem_inc(copied, 2)
                with act.Fori(0, NT) as t:
                    for k in range(SLOTS):
                        piece(t, k)
                        copy(SLOTS * t + k, k % 2)
                for n in range(SLOTS * NT, NW):
                    copy(n, n % 2)

            @block.vector
            def _(dve):
                v = nc.vector
                step = Steps(dve, own)

                def scans(n, b):
                    dve.wait_ge(rst_in[b], 8 * (n - b) + 16)
                    dve.wait_ge(turned, WC * n + WC)
                    dve.wait_ge(turned_back, 2 * n + 2)
                    for h in range(KH):
                        dve.wait_ge(scanned, 2 * n + 3 + h)
                        v.tensor_tensor_scan(scan[:, b, h, :], rst[:, b, :], ps[2 * b + h][:, 0:WE],
                                             scan[:, 1 - b, h, WE - 1:WE], ALU.min, ALU.max).then_inc(scanned, 1)

                def count(n, b):
                    dve.wait_ge(krow_in[b], 8 * (n - b) + 16)
                    count_equals(v, dve, c, n, WC * n, krow[:, b, :], junk, counted)

                def piece(t, k):
                    at = cols(t)
                    if k == 1:
                        dve.wait_ge(pe_done, t * PE_N + 2)
                        for h in range(KH):
                            step(v.tensor_scalar(c.a[:, h, at], ps[6 + h][:, 0:T], ab[:, h:h + 1], None, ALU.add))
                    elif k == 2:
                        dve.wait_ge(pe_done, t * PE_N + 3)
                        for h in range(KH):
                            step(v.tensor_tensor(sx[:, h, :], ps[6 + h][:, 0:T], c.yn[:, h, at], ALU.add))
                    elif k == 3:
                        dve.wait_ge(pe_done, t * PE_N + 4)
                        for h in range(KH):
                            step(v.tensor_tensor(cen[:, h, :], sx[:, h, :], ps[6][:, 0:T], ALU.subtract))
                    elif k == 5:
                        dve.wait_ge(act_done, t * ACT_N + 3)
                        step(v.reciprocal(sd[:], sd[:]))
                        for h in range(KH):
                            step(v.tensor_tensor(cen[:, h, :], cen[:, h, :], sd[:], ALU.mult))
                        for h in range(KH):
                            step(v.tensor_scalar(hn[:, h, :], cen[:, h, :], w.ng[:, h:h + 1], w.nb[:, h:h + 1], ALU.mult, ALU.add))
                    elif k == 7:
                        step(v.tensor_tensor(c.xT[:, :, at], c.xT[:, :, at], sx[:], ALU.add))
                    elif k >= 6 + M1:
                        h = k - 6 - M1
                        dve.wait_ge(pe_done, t * PE_N + 6 + M1 + h)
                        step(v.scalar_tensor_tensor(c.xT[:, h, at], ps[6 + h][:, 0:T], w.b2[:, h:h + 1], c.xT[:, h, at], ALU.add, ALU.add))

                v.memset(scan[:, 1, :, :], -BIG).then_inc(scanned, 4)
                dve.sem_inc(counted, 2)
                step(v.tensor_tensor(ab[:], w.tb[:], w.pb[:], ALU.add))
                step.n = 1
                with dve.Fori(0, NT) as t:
                    step.turn(t, DVE_N)
                    step.n = 1
                    for k in range(SLOTS):
                        scans(SLOTS * t + k, k % 2)
                        piece(t, k)
                        if k in COUNTS:
                            r = COUNTS.index(k)
                            count(len(COUNTS) * t + r, r % 2)
                for n in range(SLOTS * NT, NW):
                    scans(n, n % 2)
                    count(n - NW + EARLY, n % 2)
                dve.wait_ge(counted, WC * EARLY + 2)
                make_cells(v, Steps(dve, own_c), c, cell[:], dup[:], slice(0, WC * EARLY), EARLY)


def count_equals(v, dve, c, n, done, krow, junk, counted):
    for j in range(WC):
        at = bass.ds(WC * n + j, 1)
        dve.wait_ge(counted, done + j + 1)
        v.scalar_tensor_tensor(junk[:, j % 2, :], krow, c.key_c[:, at], c.before[:, WE - B * (j + 1):2 * WE - B * (j + 1)],
                               ALU.is_equal, ALU.mult, accum_out=c.cnt[:, at]).then_inc(counted, 1)


def make_cells(v, step, c, cell, dup, at, windows):
    chunks = lambda z: z.rearrange("p (w j) -> p w j", j=WC)
    step(v.tensor_scalar(dup, c.cnt[:, at], 1024.0, None, ALU.is_ge))
    step(v.tensor_tensor(chunks(cell), chunks(c.key_c[:, at]), c.spare_f[0:B, :].unsqueeze(1).to_broadcast([B, windows, WC]), ALU.subtract))
    step(v.tensor_tensor(cell, cell, dup, ALU.mult))
    step(v.tensor_tensor(cell, c.key_c[:, at], cell, ALU.subtract))
    step(v.tensor_copy(c.cell_idx[:, at], cell))
    step(v.tensor_scalar(dup, dup, -1.0, 1.0, ALU.mult, ALU.add))
    step(v.tensor_tensor(c.cell_val[:, at], c.cnt[:, at], dup, ALU.mult))


def add_cells(nc, c, dram, pool, first, last, made=None):
    for n in range(first, last):
        if made and n >= EARLY and (n - EARLY) % NEXP == 0:
            pool.wait_ge(made, (n - EARLY) // NEXP + 1)
        if n:
            pool.wait_ge(c.added, 16 * WC * n)
        for j in range(WC):
            k = WC * n + j
            nc.gpsimd.indirect_dma_start(dram.adj_flat, bass.IndirectOffsetOnAxis(ap=c.cell_idx[:, k:k + 1], axis=0),
                                         c.cell_val[:, k:k + 1], None, compute_op=ALU.add).then_inc(c.added, 16)
    if last == NW:
        pool.wait_ge(c.added, 16 * WC * NW)


def join_max(nc, c, dram, w, parts):
    with Scope(nc, "join_max") as s:
        m = s.sb("m", [B, NB, D])
        t1 = s.sb("t1", [P, 2, 4 * B])
        got = [s.sem(f"m_got{i}") for i in range(NB)]
        masked, turned, summed, own = s.sem("m_masked"), s.sem("m_turned"), s.sem("m_summed"), s.sem("join_steps")
        G4 = -(-NB // 4)
        bn_sd, high = s.sem("bn_sd"), s.sem("high")
        with nc.Block() as block:
            @block.scalar
            def _(act):
                act.wait_ge(w.loaded, w.total)
                act.wait_ge(own, 1)
                for i in range(2):
                    nc.scalar.activation(w.bn[:, i, 4], w.bn[:, i, 4], ACT.Sqrt, bias=c.eps3[:, 0:1]).then_inc(bn_sd, 1)
                split_high(nc, act, parts, high)

            @block.gpsimd
            def _(pool):
                for j in range(NB):
                    nc.gpsimd.indirect_dma_start(m[:, j, :], None, dram.runs[:, :],
                                                 bass.IndirectOffsetOnAxis(ap=c.last_idx[:, j:j + 1], axis=0)).then_inc(got[j], 16)
                add_cells(nc, c, dram, pool, 0, 4)

            @block.vector
            def _(dve):
                v = nc.vector
                step = Steps(dve, own)
                step(v.memset(c.eps3[:], 1e-3))
                dve.wait_ge(bn_sd, 2)
                for i in range(2):
                    b, g, be, m_, sv = (w.bn[:, i, k] for k in range(5))
                    step(v.reciprocal(sv, sv))
                    step(v.tensor_tensor(w.scale[:, i], g, sv, ALU.mult))
                    step(v.tensor_tensor(b, b, m_, ALU.subtract))
                    step(v.tensor_tensor(b, b, w.scale[:, i], ALU.mult))
                    step(v.tensor_tensor(w.shift[:, i], b, be, ALU.add))
                    step(v.tensor_scalar(w.scale[:, i], w.scale[:, i], 1.0 / WS, None, ALU.mult))
                v.tensor_scalar(w.bo[:], w.bo[:], WS, None, ALU.mult)
                for j in range(NB):
                    dve.wait_ge(got[j], 16)
                    v.tensor_scalar(m[:, j, :], m[:, j, :], c.has[:, j:j + 1], c.lack[:, j:j + 1], ALU.mult, ALU.add).then_inc(masked, 1)
                for g in range(G4):
                    n = min(4, NB - 4 * g) * B
                    at = slice(4 * B * g, 4 * B * g + n)
                    for h in range(KH):
                        k = 2 * g + h
                        dve.wait_ge(turned, k + 1)
                        v.tensor_tensor(t1[:, h, 0:n], c.ps[k % 8][:, 0:n], c.a[:, h, at], ALU.add).then_inc(summed, 1)
                        dve.wait_ge(summed, k + 1)
                        step(v.scalar_tensor_tensor(c.xT[:, h, at], t1[:, h, 0:n], 0.0, c.xT[:, h, at], ALU.max, ALU.add))
                split_low(nc, dve, parts, high)

            @block.tensor
            def _(pe):
                for g in range(G4):
                    n = min(4, NB - 4 * g)
                    pe.wait_ge(masked, 4 * g + n)
                    for h in range(KH):
                        k = 2 * g + h
                        if k >= 8:
                            pe.wait_ge(summed, k - 7)
                        for i in range(n):
                            ins = nc.tensor.transpose(c.ps[k % 8][:, B * i:B * (i + 1)], m[:, 4 * g + i, half(h)], c.ident[0:B, 0:B])
                        ins.then_inc(turned, 1)


def product3(nc, out, lhs, rhs, start=True, stop=True):
    n = 3 * len(lhs)
    terms = [z for (ah, al), (bh, bl) in zip(lhs, rhs) for z in ((ah, bh), (ah, bl), (al, bh))]
    for i, (a, b) in enumerate(terms):
        ins = nc.tensor.matmul(out, a, b, start=(start and i == 0), stop=(stop and i == n - 1))
    return ins


def split_high(nc, act, parts, high):
    for src, hi, lo, loaded, total in parts:
        act.wait_ge(loaded, total)
        nc.scalar.activation(hi, src, ACT.Copy, scale=WS).then_inc(high, 1)


def split_low(nc, dve, parts, high):
    for n, (src, hi, lo, _, _) in enumerate(parts):
        dve.wait_ge(high, n + 1)
        nc.vector.scalar_tensor_tensor(lo, src, WS, hi, ALU.mult, ALU.subtract)


def split_weights(nc, name, parts):
    with Scope(nc, name) as s:
        high = s.sem("high")
        with nc.Block() as block:
            @block.scalar
            def _(act):
                split_high(nc, act, parts, high)

            @block.vector
            def _(dve):
                split_low(nc, dve, parts, high)


def product(nc, out, lhs, rhs):
    for k, (a, b) in enumerate(zip(lhs, rhs)):
        ins = nc.tensor.matmul(out, a, b, start=(k == 0), stop=(k == len(lhs) - 1))
    return ins


def norm(nc, c, n, beside=None, loads=()):
    G4 = -(-NB // WC)
    with Scope(nc, f"norm{n}") as s:
        sq = s.sb("sq", [P, 2, KH, WE])
        sd, rs = s.sb("sd", [B, 2, WC]), s.sb("rs", [B, 2, WC])
        ps, out = c.ps, c.yn
        mean_done, var_done, spread = s.sem("mean_done"), s.sem("var_done"), s.sem("spread")
        centred, sq_ready, sd_ready, rs_ready = s.sem("centred"), s.sem("sq_ready"), s.sem("sd_ready"), s.sem("rs_ready")
        scaled, high = s.sem("scaled"), s.sem("high")
        size = lambda g: min(WC, NB - WC * g)
        at = lambda g: slice(WE * g, WE * g + size(g) * B)
        wide = lambda g: size(g) * B
        with nc.Block() as block:
            if beside:
                block.gpsimd(beside)

            @block.sync
            def _(sp):
                with nc.allow_non_contiguous_dma(reason="weights in blocks of 128 rows"):
                    for dst, src, sem in loads:
                        sp.dma_start(dst, src).then_inc(sem, 16)

            @block.tensor
            def _(pe):
                for t in range(G4 + 2):
                    if t < G4:
                        if t >= 3:
                            pe.wait_ge(centred, t - 2)
                        product(nc, ps[t % 3][:, 0:wide(t)], [c.mean_w[:]] * KH, [c.xT[:, k, at(t)] for k in range(KH)]).then_inc(mean_done, 1)
                    if 1 <= t <= G4:
                        g = t - 1
                        pe.wait_ge(sq_ready, g + 1)
                        if g >= 2:
                            pe.wait_ge(sd_ready, g - 1)
                        for j in range(size(g)):
                            ins = product(nc, ps[3 + g % 2][0:B, j:j + 1], [sq[:, g % 2, k, B * j:B * (j + 1)] for k in range(KH)], [c.mean_w[:, 0:1]] * KH)
                        ins.then_inc(var_done, 1)
                    if t >= 2:
                        g = t - 2
                        pe.wait_ge(rs_ready, g + 1)
                        if g >= 3:
                            pe.wait_ge(scaled, g - 2)
                        for j in range(size(g)):
                            ins = nc.tensor.transpose(ps[5 + g % 3][:, B * j:B * (j + 1)], rs[:, g % 2, j:j + 1].to_broadcast([B, P]), c.ident[0:B, 0:B])
                        ins.then_inc(spread, 1)

            @block.scalar
            def _(act):
                for t in range(G4 + 3):
                    if t < G4:
                        act.wait_ge(centred, t + 1)
                        if t >= 2:
                            act.wait_ge(var_done, t - 1)
                        nc.scalar.activation(sq[:, t % 2, :, 0:wide(t)], out[:, :, at(t)], ACT.Square).then_inc(sq_ready, 1)
                    if 1 <= t <= G4:
                        g = t - 1
                        act.wait_ge(var_done, g + 1)
                        if g >= 2:
                            act.wait_ge(rs_ready, g - 1)
                        nc.scalar.activation(sd[:, g % 2, 0:size(g)], ps[3 + g % 2][0:B, 0:size(g)], ACT.Sqrt, bias=c.eps5[0:B, 0:1]).then_inc(sd_ready, 1)
                    if t >= 3:
                        act.wait_ge(scaled, t - 2)
                        nc.scalar.copy(c.yh[:, :, at(t - 3)], out[:, :, at(t - 3)]).then_inc(high, 1)

            @block.vector
            def _(dve):
                v = nc.vector
                v.memset(c.yh[:, :, N:NP], 0.0)
                v.memset(c.yl[:, :, N:NP], 0.0)
                for t in range(G4 + 3):
                    if t < G4:
                        dve.wait_ge(mean_done, t + 1)
                        for h in range(KH):
                            ins = v.tensor_tensor(out[:, h, at(t)], c.xT[:, h, at(t)], ps[t % 3][:, 0:wide(t)], ALU.subtract)
                        ins.then_inc(centred, 1)
                    if 1 <= t <= G4:
                        g = t - 1
                        dve.wait_ge(sd_ready, g + 1)
                        if g >= 2:
                            dve.wait_ge(spread, g - 1)
                        v.reciprocal(rs[:, g % 2, 0:size(g)], sd[:, g % 2, 0:size(g)]).then_inc(rs_ready, 1)
                    if 2 <= t <= G4 + 1:
                        g = t - 2
                        dve.wait_ge(spread, g + 1)
                        for h in range(KH):
                            ins = v.tensor_tensor(out[:, h, at(g)], out[:, h, at(g)], ps[5 + g % 3][:, 0:wide(g)], ALU.mult)
                        ins.then_inc(scaled, 1)
                    if t >= 3:
                        dve.wait_ge(high, t - 2)
                        dve.wait_ge(scaled, t - 2)
                        v.tensor_tensor(c.yl[:, :, at(t - 3)], out[:, :, at(t - 3)], c.yh[:, :, at(t - 3)], ALU.subtract)


def gate(nc, c, w, dram, parts, beside):
    with Scope(nc, "gate") as s:
        lg = s.sb("lg", [B, NB, NEXP])
        mx = s.sb("mx", [B, NB])
        wT = s.sb("wT", [NEXP, NP])
        ps = c.ps
        G4 = -(-NB // 4)
        logits, ready, ex, own = s.sem("logits"), s.sem("lg_ready"), s.sem("lg_exp"), s.sem("gate_steps")
        raw, raw_out, high = s.sem("raw"), s.sem("raw_out"), s.sem("high")
        turned, copied, stored = s.sem("wg_turned"), s.sem("wg_copied"), s.sem("wg_stored")
        with nc.Block() as block:
            if beside:
                block.gpsimd(beside)

            @block.tensor
            def _(pe):
                for t in range(NT):
                    product(nc, ps[1 + t][0:NEXP, 0:T], [w.Wr[:, k, :] for k in range(KH)], [c.yn[:, k, t * T:(t + 1) * T] for k in range(KH)]).then_inc(raw, 1)
                for j in range(NB):
                    pe.wait_ge(raw_out, (B * (j + 1) - 1) // T + 1)
                    ins = nc.tensor.transpose(ps[0][0:B, NEXP * j:NEXP * (j + 1)], wT[:, B * j:B * (j + 1)], c.ident[0:NEXP, 0:NEXP])
                ins.then_inc(logits, 1)
                pe.wait_ge(ready, 2)
                for g in range(G4):
                    n = min(4, NB - 4 * g)
                    for i in range(n):
                        ins = nc.tensor.transpose(ps[1 + g][0:NEXP, B * i:B * (i + 1)], lg[:, 4 * g + i, :], c.ident[0:B, 0:B])
                    ins.then_inc(turned, 1)

            @block.vector
            def _(dve):
                v = nc.vector
                step = Steps(dve, own)
                for t in range(NT):
                    dve.wait_ge(raw, t + 1)
                    v.tensor_scalar(wT[:, t * T:(t + 1) * T], ps[1 + t][0:NEXP, 0:T], w.br[:, 0:1], None, ALU.add).then_inc(raw_out, 1)
                dve.wait_ge(logits, 1)
                step(v.tensor_copy(lg[:], ps[0][0:B, 0:NB * NEXP].rearrange("p (j e) -> p j e", e=NEXP)))
                wide = mx[:].unsqueeze(2).to_broadcast([B, NB, NEXP])
                step(v.tensor_reduce(mx[:], lg[:], AX.X, ALU.max))
                v.tensor_tensor(lg[:], lg[:], wide, ALU.subtract).then_inc(ready, 1)
                step(v.memset(wT[:, N:NP], 0.0))
                dve.wait_ge(ex, 1)
                step(v.tensor_reduce(mx[:], lg[:], AX.X, ALU.add))
                step(v.reciprocal(mx[:], mx[:]))
                v.tensor_tensor(lg[:], lg[:], wide, ALU.mult).then_inc(ready, 1)
                for g in range(G4):
                    n = min(4, NB - 4 * g) * B
                    dve.wait_ge(turned, g + 1)
                    v.tensor_copy(wT[:, 4 * B * g:4 * B * g + n], ps[1 + g][0:NEXP, 0:n]).then_inc(copied, 1)
                split_low(nc, dve, parts, high)

            @block.scalar
            def _(act):
                act.wait_ge(ready, 1)
                nc.scalar.activation(lg[:], lg[:], ACT.Exp).then_inc(ex, 1)
                split_high(nc, act, parts, high)

            @block.sync
            def _(sp):
                sp.wait_ge(copied, G4)
                sp.dma_start(dram.gate[:, :], wT[:]).then_inc(stored, 16)
                sp.wait_ge(stored, 16)


def experts(nc, c, w, dram, made, beside):
    assert NT * NEXP == NW - EARLY
    with Scope(nc, "experts") as s:
        gb = [s.sb(f"gb{e}", [P, T]) for e in range(NEXP)]
        gT = s.sb("gT", [NEXP, T])
        hf = s.sb("hf", [P, KH, T])
        krow = s.sb("krow", [B, 2, WE])
        junk = s.sb("junk", [B, 2, WE], F16)
        cell, dup = s.sb("cell", [B, WC * NEXP]), s.sb("dup", [B, WC * NEXP])
        krow_in = [s.sem(f"krow_in{b}") for b in range(2)]
        counted, own_c = s.sem("counted"), s.sem("cell_steps")
        h1h, h1l = s.sb("h1h", [P, 2, KH, T], F16), s.sb("h1l", [P, 2, KH, T], F16)
        h2 = s.sb("h2", [P, 2, KH, T])
        hwh, hwl = s.sb("hwh", [P, 2, KH, T], F16), s.sb("hwl", [P, 2, KH, T], F16)
        ps = c.ps
        gb_in = [s.sem(f"gb_in{e}") for e in range(NEXP)]
        gt_in = s.sem("gt_in")
        l1, l2, lo = s.sem("e_l1"), s.sem("e_l2"), s.sem("e_out")
        a1, low1, a2, dm, wh, dw, dx = (s.sem(n) for n in (
            "relu1", "h1_low", "relu2", "weighted", "hw_high", "hw_low", "added"))
        K = NEXP
        with nc.Block() as block:
            if beside:
                block.gpsimd(beside)

            @block.sync
            def _(sp):
                def keys(n, b):
                    at = bass.ds(WE * EARLY + n * WE, WE)
                    sp.dma_start(krow[:, b, :], dram.keys[at].partition_broadcast(B)).then_inc(krow_in[b], 16)

                for b in range(2):
                    keys(b, b)
                sp.dma_start(gT[:], dram.gate[:, 0:T]).then_inc(gt_in, 16)
                for e in range(K):
                    sp.dma_start(gb[e][:], dram.gate[e, 0:T].partition_broadcast(P)).then_inc(gb_in[e], 16)
                with sp.Fori(1, NT) as t:
                    for e in range(K):
                        sp.wait_ge(dm, K * (t - 1) + e + 1)
                        sp.dma_start(gb[e][:], dram.gate[e, cols(t)].partition_broadcast(P)).then_inc(gb_in[e], 16)
                        keys(K * (t - 1) + e + 2, e % 2)
                    sp.dma_start(gT[:], dram.gate[:, cols(t)]).then_inc(gt_in, 16)
                for e in range(K - 2):
                    sp.wait_ge(dm, K * (NT - 1) + e + 1)
                    keys(K * (NT - 1) + e + 2, e % 2)

            def back(t, e, lag):
                return not (isinstance(t, int) and t == 0 and e < lag), (e - lag) % K, K * t + e - lag

            @block.tensor
            def _(pe):
                parts = lambda W, e, h: [(W[0][:, e, k, half(h)], W[1][:, e, k, half(h)]) for k in range(KH)]
                slot = lambda hi, lo, e: [(hi[:, e % 2, k, :], lo[:, e % 2, k, :]) for k in range(KH)]

                def first(t, e):
                    pe.wait_ge(a1, K * t + e + 1)
                    for h in range(KH):
                        ins = product3(nc, ps[2 * (e % 2) + h][:, 0:T], parts(w.W1, e, h),
                                       [(c.yh[:, k, cols(t)], c.yl[:, k, cols(t)]) for k in range(KH)])
                    ins.then_inc(l1, 1)

                def second(e, n):
                    pe.wait_ge(low1, n + 2)
                    pe.wait_ge(a2, n + 2)
                    for h in range(KH):
                        ins = product3(nc, ps[4 + h][:, 0:T], parts(w.W2, e, h), slot(h1h, h1l, e))
                    ins.then_inc(l2, 1)

                def last(t, e, n):
                    if e == 0:
                        pe.wait_ge(dx, t + 1)
                        pe.wait_ge(gt_in, 16 * t + 16)
                        for h in range(KH):
                            nc.tensor.matmul(ps[6 + h][:, 0:T], w.bo[:, half(h)], gT[:], start=True, stop=False)
                    pe.wait_ge(dw, n + 1)
                    for h in range(KH):
                        ins = product3(nc, ps[6 + h][:, 0:T], parts(w.Wo, e, h), slot(hwh, hwl, e), start=False, stop=(e == K - 1))
                    ins.then_inc(lo, 1)

                def tile(t, steps=K):
                    for e in range(steps):
                        if steps == K:
                            first(t, e)
                        there, f, n = back(t, e, 3)
                        if there:
                            last(t, f, n)
                        there, f, n = back(t, e, 1)
                        if there and (steps == K or e < 1):
                            second(f, n)

                tile(0)
                with pe.Fori(1, NT) as t:
                    tile(t)
                tile(NT, 3)

            @block.scalar
            def _(act):
                a = nc.scalar.activation
                act.sem_inc(a1, 2)
                act.sem_inc(a2, 2)

                def relu(out, bank, i, h, e):
                    return a(out, ps[bank][:, 0:T], ACT.Relu, bias=w.shift[:, i, h, e:e + 1], scale=w.scale[:, i, h, e:e + 1])

                def tile(t, steps=K):
                    start = isinstance(t, int) and t == 0
                    for e in range(steps):
                        if steps == K:
                            act.wait_ge(l1, K * t + e + 1)
                            if e >= 2 or not start:
                                act.wait_ge(l2, K * t + e - 1)
                            for h in range(KH):
                                relu(h1h[:, e % 2, h, :], 2 * (e % 2) + h, 0, h, e)
                            act.wait_ge(low1, K * t + e + 1)
                            for h in range(KH):
                                ins = relu(hf[:, h, :], 2 * (e % 2) + h, 0, h, e)
                            ins.then_inc(a1, 1)
                        there, f, n = back(t, e, 2)
                        if there:
                            act.wait_ge(dm, n + 1)
                            if f >= 2 or not start:
                                act.wait_ge(lo, n - 1)
                            nc.scalar.copy(hwh[:, f % 2], h2[:, f % 2]).then_inc(wh, 1)
                        there, f, n = back(t, e, 1)
                        if there and (steps == K or e < 1):
                            act.wait_ge(l2, n + 1)
                            if f >= 2 or not start:
                                act.wait_ge(dw, n - 1)
                            for h in range(KH):
                                ins = relu(h2[:, f % 2, h, :], 4 + h, 1, h, f)
                            ins.then_inc(a2, 1)

                tile(0)
                with act.Fori(1, NT) as t:
                    tile(t)
                tile(NT, 2)

            @block.vector
            def _(dve):
                v = nc.vector
                dve.sem_inc(dx, 1)
                dve.sem_inc(low1, 1)

                def tile(t, steps=K):
                    start = isinstance(t, int) and t == 0
                    for e in range(steps):
                        if steps == K:
                            dve.wait_ge(a1, K * t + e + 3)
                            v.tensor_tensor(h1l[:, e % 2], hf[:], h1h[:, e % 2], ALU.subtract).then_inc(low1, 1)
                        there, f, n = back(t, e, 2)
                        if there and (steps == K or e < 2):
                            dve.wait_ge(wh, n + 1)
                            v.tensor_tensor(hwl[:, f % 2], h2[:, f % 2], hwh[:, f % 2], ALU.subtract).then_inc(dw, 1)
                        if e == 2 and not start:
                            dve.wait_ge(lo, K * t)
                            for h in range(KH):
                                ins = v.scalar_tensor_tensor(c.xT[:, h, cols(t - 1)], ps[6 + h][:, 0:T], 1.0 / WS, c.xT[:, h, cols(t - 1)], ALU.mult, ALU.add)
                            ins.then_inc(dx, 1)
                        there, f, n = back(t, e, 1)
                        if there and (steps == K or e < 1):
                            dve.wait_ge(gb_in[f], 16 * (t if e == 0 else t + 1))
                            dve.wait_ge(a2, n + 3)
                            v.tensor_tensor(h2[:, f % 2], h2[:, f % 2], gb[f][:].unsqueeze(1).to_broadcast([P, KH, T]), ALU.mult).then_inc(dm, 1)
                        if steps == K:
                            dve.wait_ge(krow_in[e % 2], 64 * t + 16 * (e // 2) + 16)
                            count_equals(v, dve, c, K * t + e + EARLY, WC * (K * t + e), krow[:, e % 2, :], junk, counted)
                    if steps == K:
                        step.turn(t, 7)
                        dve.wait_ge(counted, WC * K * t + WC * K + 2)
                        make_cells(v, step, c, cell[:], dup[:], bass.ds(WC * EARLY + WC * K * t, WC * K), K)
                        dve.sem_inc(made, 1)

                dve.sem_inc(counted, 2)
                step = Steps(dve, own_c)
                tile(0)
                with dve.Fori(1, NT) as t:
                    tile(t)
                tile(NT, 3)


def mix1(nc, c, w, qT, ctx, beside=None):
    NQ = NT
    with Scope(nc, "mix1") as s:
        rr = s.sb("rr", [P, 2, T])
        kT = s.sb("kT", [P, NP])
        xr = s.sb("xr", [P, KH, NP])
        et = s.sb("et", [B, NB, P])
        vt = s.sb("vt", [B, NB, P])
        qt = s.sb("qt", [B, NB, P])
        mx8 = s.sb("mx8", [P, NT + 1])
        nmx = s.sb("nmx", [P, 1])
        sums = s.sb("sums", [P, 2])
        km = s.sb("km", [P, MEM])
        memT = s.sb("memT", [MEM, 2, P])
        qm = s.sb("qm", [B, NB * HEADS1])
        g16 = s.sb("g16", [P, KH])
        ps = c.ps
        at = lambda t: slice(t * T, (t + 1) * T)
        tok = lambda j: slice(B * j, B * (j + 1))
        own = s.sem("m1_steps")
        ss_done, sq_ready, sd_ready, xr_ready = s.sem("ss_done"), s.sem("m_sq"), s.sem("m_sd"), s.sem("xr_ready")
        k_done, k_out, qv_done, q_out, v_out = s.sem("k_done"), s.sem("k_out"), s.sem("qv_done"), s.sem("q_out"), s.sem("v_out")
        mx_ready, e_ready, et_turned, et_out = s.sem("mx_ready"), s.sem("e_ready"), s.sem("et_turned"), s.sem("et_out")
        q_ready, q_exp, q_norm, q_turned, qT_out = s.sem("q_ready"), s.sem("q_exp"), s.sem("q_norm"), s.sem("q_turned"), s.sem("qT_out")
        mem_turned, mem_out, ctx_done, ctx_ready = s.sem("mem_turned"), s.sem("mem_out"), s.sem("ctx_done"), s.sem("ctx_ready")
        w_ready = s.sem("w_ready")
        G4 = -(-NB // 4)
        with nc.Block() as block:
            if beside:
                block.gpsimd(beside)

            @block.scalar
            def _(act):
                a = nc.scalar.activation
                for t in range(NT + 1):
                    if t < NT:
                        a(xr[:, :, at(t)], c.yn[:, :, at(t)], ACT.Square).then_inc(sq_ready, 1)
                    if t >= 1:
                        act.wait_ge(ss_done, t)
                        if t >= 3:
                            act.wait_ge(xr_ready, t - 2)
                        a(rr[:, (t - 1) % 2], ps[(t - 1) % 2][:, 0:T], ACT.Sqrt).then_inc(sd_ready, 1)
                for j in range(NB):
                    act.wait_ge(qv_done, j + 1)
                    nc.scalar.copy(vt[:, j, :], ps[6 + j % 2][0:B, 0:P]).then_inc(v_out, 1)
                act.wait_ge(mx_ready, 1)
                a(kT[:, 0:N], kT[:, 0:N], ACT.Exp, bias=nmx[:, 0:1], accum_out=sums[:, 0:1]).then_inc(e_ready, 1)
                a(km[:], w.mk[:], ACT.Exp, bias=nmx[:, 0:1], accum_out=sums[:, 1:2]).then_inc(e_ready, 1)
                act.wait_ge(q_ready, 1)
                a(qt[:], qt[:], ACT.Exp).then_inc(q_exp, 1)
                for g in range(G4):
                    n = min(4, NB - 4 * g)
                    act.wait_ge(et_turned, g + 1)
                    nc.scalar.copy(et[:, 4 * g:4 * g + n, :], ps[g % 2][0:B, 0:n * P].rearrange("p (j d) -> p j d", d=P)).then_inc(et_out, 1)

            @block.vector
            def _(dve):
                v = nc.vector
                step = Steps(dve, own)
                dve.wait_ge(w.loaded, w.total)
                step(v.tensor_scalar(g16[:], w.gpre[:], float(D) ** 0.5, None, ALU.mult))
                for k in range(KH):
                    ins = v.tensor_scalar(w.mqkv[:, k, :], w.mqkv[:, k, :], g16[:, k:k + 1], None, ALU.mult)
                ins.then_inc(w_ready, 1)
                for t in range(NT):
                    r = rr[:, t % 2]
                    dve.wait_ge(sd_ready, t + 1)
                    step(v.tensor_scalar(r, r, 1e-12, None, ALU.max))
                    step(v.reciprocal(r, r))
                    v.tensor_tensor(xr[:, 0, at(t)], c.yn[:, 0, at(t)], r, ALU.mult)
                    v.tensor_tensor(xr[:, 1, at(t)], c.yn[:, 1, at(t)], r, ALU.mult).then_inc(xr_ready, 1)
                for t in range(NT):
                    dve.wait_ge(k_done, t + 1)
                    n = min(T, N - t * T)
                    v.tensor_copy(kT[:, at(t)], ps[2 + t % 2][:, 0:T])
                    v.tensor_reduce(mx8[:, t:t + 1], ps[2 + t % 2][:, 0:n], AX.X, ALU.max).then_inc(k_out, 1)
                for j in range(NB):
                    dve.wait_ge(qv_done, j + 1)
                    v.tensor_copy(qt[:, j, :], ps[4 + j % 2][0:B, 0:P]).then_inc(q_out, 1)
                v.tensor_reduce(mx8[:, NT:NT + 1], w.mk[:], AX.X, ALU.max).then_inc(k_out, 1)
                dve.wait_ge(k_out, NT + 1)
                step(v.tensor_reduce(nmx[:], mx8[:], AX.X, ALU.max))
                v.tensor_scalar(nmx[:], nmx[:], -1.0, None, ALU.mult).then_inc(mx_ready, 1)
                q3 = qt[:].rearrange("p j (h d) -> p (j h) d", d=HD1)
                wide = qm[:].unsqueeze(2).to_broadcast([B, NB * HEADS1, HD1])
                dve.wait_ge(q_out, NB)
                step(v.tensor_reduce(qm[:], q3, AX.X, ALU.max))
                v.tensor_tensor(q3, q3, wide, ALU.subtract).then_inc(q_ready, 1)
                dve.wait_ge(q_exp, 1)
                step(v.tensor_reduce(qm[:], q3, AX.X, ALU.add))
                step(v.reciprocal(qm[:], qm[:]))
                step(v.tensor_scalar(qm[:], qm[:], HD1 ** -0.5, None, ALU.mult))
                v.tensor_tensor(q3, q3, wide, ALU.mult).then_inc(q_norm, 1)
                step(v.memset(qT[:, N:NP], 0.0))
                step(v.memset(ctx[:], 0.0))
                dve.wait_ge(mem_turned, 1)
                v.tensor_copy(memT[:, 0, :], ps[2][0:MEM, 0:P])
                v.tensor_copy(memT[:, 1, :], ps[2][0:MEM, P:2 * P]).then_inc(mem_out, 1)
                for g in range(G4):
                    n = min(4, NB - 4 * g) * B
                    dve.wait_ge(q_turned, g + 1)
                    v.tensor_copy(qT[:, 4 * B * g:4 * B * g + n], ps[4 + g % 2][:, 0:n]).then_inc(qT_out, 1)
                dve.wait_ge(e_ready, 2)
                step(v.tensor_tensor(sums[:, 0:1], sums[:, 0:1], sums[:, 1:2], ALU.add))
                step(v.reciprocal(sums[:, 0:1], sums[:, 0:1]))
                dve.wait_ge(ctx_done, 1)
                for h in range(HEADS1):
                    r = slice(h * HD1, (h + 1) * HD1)
                    ins = v.tensor_scalar(ctx[r, r], ps[3][r, r], sums[r, 0:1], None, ALU.mult)
                ins.then_inc(ctx_ready, 1)

            @block.tensor
            def _(pe):
                mm = nc.tensor.matmul
                for t in range(NT):
                    pe.wait_ge(sq_ready, t + 1)
                    if t >= 2:
                        pe.wait_ge(sd_ready, t - 1)
                    product(nc, ps[t % 2][:, 0:T], [c.ones[:]] * KH, [xr[:, k, at(t)] for k in range(KH)]).then_inc(ss_done, 1)
                pe.wait_ge(w_ready, 1)
                H = HEADS1 * HD1
                for t in range(NT):
                    pe.wait_ge(xr_ready, t + 1)
                    if t >= 2:
                        pe.wait_ge(k_out, t - 1)
                    product(nc, ps[2 + t % 2][:, 0:T], [w.mqkv[:, k, H:2 * H] for k in range(KH)], [xr[:, k, at(t)] for k in range(KH)]).then_inc(k_done, 1)
                for j in range(NB):
                    if j >= 2:
                        pe.wait_ge(q_out, j - 1)
                        pe.wait_ge(v_out, j - 1)
                    product(nc, ps[4 + j % 2][0:B, 0:P], [xr[:, k, tok(j)] for k in range(KH)], [w.mqkv[:, k, 0:H] for k in range(KH)])
                    product(nc, ps[6 + j % 2][0:B, 0:P], [xr[:, k, tok(j)] for k in range(KH)], [w.mqkv[:, k, 2 * H:3 * H] for k in range(KH)]).then_inc(qv_done, 1)
                pe.wait_ge(e_ready, 2)
                pe.wait_ge(k_out, NT)
                nc.tensor.transpose(ps[2][0:MEM, 0:P], km[:], c.ident[:])
                nc.tensor.transpose(ps[2][0:MEM, P:2 * P], w.mv[:], c.ident[:]).then_inc(mem_turned, 1)
                pe.wait_ge(sd_ready, NT)
                for g in range(G4):
                    n = min(4, NB - 4 * g)
                    if g >= 2:
                        pe.wait_ge(et_out, g - 1)
                    for i in range(n):
                        ins = nc.tensor.transpose(ps[g % 2][0:B, P * i:P * (i + 1)], kT[:, tok(4 * g + i)], c.ident[:])
                    ins.then_inc(et_turned, 1)
                pe.wait_ge(q_norm, 1)
                pe.wait_ge(q_out, NB)
                pe.wait_ge(v_out, NB)
                for g in range(G4):
                    n = min(4, NB - 4 * g)
                    if g >= 2:
                        pe.wait_ge(qT_out, g - 1)
                    for i in range(n):
                        ins = nc.tensor.transpose(ps[4 + g % 2][:, B * i:B * (i + 1)], qt[:, 4 * g + i, :], c.ident[0:B, 0:B])
                    ins.then_inc(q_turned, 1)
                pe.wait_ge(et_out, G4)
                pe.wait_ge(mem_out, 1)
                for j in range(NB):
                    mm(ps[3][:, 0:P], et[:, j, :], vt[:, j, :], start=(j == 0), stop=False)
                mm(ps[3][:, 0:P], memT[:, 0, :], memT[:, 1, :], start=False, stop=True).then_inc(ctx_done, 1)
                pe.wait_ge(ctx_ready, 1)
                pe.wait_ge(qT_out, G4)


def sage(nc, c, w, dram, layer, mix=None):
    SG = 5
    JG = NB // SG
    MPE, MACT, MDVE = 3, 2, 10
    with Scope(nc, f"sage{layer}") as s:
        zh = s.sb("zh", [B, NB, D], F16)
        zl = s.sb("zl", [B, NB, D], F16)
        adj = [s.sb(f"adj{g}", [B, JG, T], F16) for g in range(SG)]
        u = s.sb("u", [P, KH, T])
        b64 = s.sb("b64", [P, KH])
        ps = c.ps
        z_done, zh_out, zl_out = s.sem("z_done"), s.sem("zh_out"), s.sem("zl_out")
        adj_in = [s.sem(f"adj_in{g}") for g in range(SG)]
        adj_used, high = s.sem("adj_used"), s.sem("high")
        own_done, own, mown, mpe, mact = (s.sem(n) for n in ("self_done", "steps", "m_steps", "m_pe", "m_act"))
        if mix:
            qT, ctx = mix
            sq, yo = s.sb("sq", [P, KH, T]), s.sb("yo", [P, KH, T])
            rr, oT, g16 = s.sb("rr", [P, T]), s.sb("oT", [P, T]), s.sb("g16", [P, KH])
        DVE_N = 6
        with nc.Block() as block:
            @block.sync
            def _(sp):
                def load(t, g):
                    rows = dram.adj[B * JG * g:B * JG * (g + 1), cols(t)]
                    sp.dma_start(adj[g][:], rows.rearrange("(j p) d -> p j d", p=B)).then_inc(adj_in[g], 16)

                for g in range(SG):
                    load(0, g)
                with sp.Fori(1, NT) as t:
                    for g in range(SG):
                        sp.wait_ge(adj_used, SG * (t - 1) + g + 1)
                        load(t, g)

            @block.tensor
            def _(pe):
                mm = nc.tensor.matmul
                parts = lambda W, k, at: (W[0][:, layer, k, at], W[1][:, layer, k, at])
                for j in range(NB):
                    if j >= 4:
                        pe.wait_ge(zl_out, j - 3)
                    tok = slice(B * j, B * (j + 1))
                    product3(nc, ps[j % 4][0:B, 0:D], [(c.yh[:, k, tok], c.yl[:, k, tok]) for k in range(KH)],
                             [parts(w.gl, k, slice(0, D)) for k in range(KH)]).then_inc(z_done, 1)
                pe.wait_ge(zl_out, NB)

                def attention(t, g):
                    if g == 0:
                        pe.wait_ge(mown, MDVE * t + 1)
                        product(nc, ps[2][:, 0:T], [ctx[:]], [qT[:, cols(t)]]).then_inc(mpe, 1)
                    elif g == 1:
                        pe.wait_ge(mown, MDVE * t + 2)
                        for h in range(KH):
                            ins = product(nc, ps[3 - h][:, 0:T], [w.wout[:, half(h)]], [oT[:]])
                        ins.then_inc(mpe, 1)
                    elif g == 3:
                        pe.wait_ge(mact, MACT * t + 1)
                        product(nc, ps[3][:, 0:T], [c.ones[:]] * KH, [sq[:, k, :] for k in range(KH)]).then_inc(mpe, 1)

                def tile(t, b):
                    for g in range(SG):
                        pe.wait_ge(adj_in[g], 16 * t + 16)
                        for j in range(JG):
                            for h in range(KH):
                                for z in (zh, zl):
                                    ins = mm(ps[4 * b + h][:, 0:T], z[:, g * JG + j, half(h)], adj[g][:, j, :],
                                             start=(g == 0 and j == 0 and z is zh), stop=(g == SG - 1 and j == JG - 1 and z is zl))
                        ins.then_inc(adj_used, 1)
                        if mix:
                            attention(t, g)
                    pe.wait_ge(own, DVE_N * t + 1)
                    for h in range(KH):
                        ins = product3(nc, ps[6 + h][:, 0:T], [parts(w.gr, k, half(h)) for k in range(KH)],
                                       [(c.yh[:, k, cols(t)], c.yl[:, k, cols(t)]) for k in range(KH)])
                    ins.then_inc(own_done, 1)

                with pe.Fori(0, NT // 2) as i:
                    for b in range(2):
                        tile(2 * i + b, b)
                tile(NT - 1, 0)

            @block.scalar
            def _(act):
                for j in range(NB):
                    act.wait_ge(z_done, j + 1)
                    nc.scalar.copy(zh[:, j, :], ps[j % 4][0:B, 0:D]).then_inc(zh_out, 1)
                if layer < 2:
                    with act.Fori(0, NT) as t:
                        if mix:
                            act.wait_ge(mown, MDVE * t + 4)
                            nc.scalar.activation(sq[:], yo[:], ACT.Square).then_inc(mact, 1)
                            act.wait_ge(mpe, MPE * t + 3)
                            nc.scalar.activation(rr[:], ps[3][:, 0:T], ACT.Sqrt).then_inc(mact, 1)
                        act.wait_ge(own, DVE_N * t + 6)
                        nc.scalar.copy(c.yh[:, :, cols(t)], u[:]).then_inc(high, 1)

            @block.vector
            def _(dve):
                v = nc.vector
                step, mstep = Steps(dve, own), Steps(dve, mown)
                step(v.tensor_scalar(b64[:], w.gb[:, layer], WS, None, ALU.mult))
                if mix:
                    mstep(v.tensor_scalar(g16[:], w.gout[:], float(D) ** 0.5, None, ALU.mult))
                for j in range(NB):
                    dve.wait_ge(zh_out, j + 1)
                    v.tensor_tensor(zl[:, j, :], ps[j % 4][0:B, 0:D], zh[:, j, :], ALU.subtract).then_inc(zl_out, 1)
                def tile(t, b):
                    at = cols(t)
                    if mix:
                        mstep.turn(t, MDVE)
                        mstep.n = 1
                        dve.wait_ge(mpe, MPE * t + 1)
                        mstep(v.tensor_copy(oT[:], ps[2][:, 0:T]))
                        dve.wait_ge(mpe, MPE * t + 2)
                        for h in range(KH):
                            mstep(v.tensor_scalar(yo[:, h, :], ps[3 - h][:, 0:T], w.bout[:, h:h + 1], None, ALU.add))
                        dve.wait_ge(mact, MACT * t + 2)
                        mstep(v.tensor_scalar(rr[:], rr[:], 1e-12, None, ALU.max))
                        mstep(v.reciprocal(rr[:], rr[:]))
                        for h in range(KH):
                            mstep(v.scalar_tensor_tensor(yo[:, h, :], yo[:, h, :], g16[:, h:h + 1], rr[:], ALU.mult, ALU.mult))
                        mstep(v.tensor_tensor(yo[:], yo[:], c.yn[:, :, at], ALU.add))
                        mstep(v.tensor_tensor(c.xT[:, :, at], c.xT[:, :, at], yo[:], ALU.add))
                        dve.sem_inc(mown, 1)
                    step.turn(t, DVE_N)
                    step.n = 1
                    dve.wait_ge(adj_used, SG * t + SG)
                    for h in range(KH):
                        step(v.tensor_tensor(u[:, h, :], ps[4 * b + h][:, 0:T], w.rd[:, at], ALU.mult))
                    dve.wait_ge(own_done, t + 1)
                    for h in range(KH):
                        step(v.scalar_tensor_tensor(u[:, h, :], ps[6 + h][:, 0:T], b64[:, h:h + 1], u[:, h, :], ALU.add, ALU.add))
                    if layer < 2:
                        step(v.tensor_scalar(u[:], u[:], 1.0 / WS, 0.0, ALU.mult, ALU.max))
                        dve.wait_ge(high, t + 1)
                        step(v.tensor_tensor(c.yl[:, :, at], u[:], c.yh[:, :, at], ALU.subtract))
                    else:
                        for h in range(KH):
                            step(v.scalar_tensor_tensor(c.xT[:, h, at], u[:, h, :], 1.0 / WS, c.xT[:, h, at], ALU.mult, ALU.add))

                with dve.Fori(0, NT // 2) as i:
                    for b in range(2):
                        tile(2 * i + b, b)
                tile(NT - 1, 0)


def ffn1(nc, c, w, dram, out):
    M1 = HID1 // P
    with Scope(nc, "ffn1") as s:
        wrow = s.sb("wrow", [P, NP])
        sel = s.sb("sel", [P, NP])
        wc = s.sb("wc", [B, NB])
        rank = s.sb("rank", [B, 3, NB])
        junk = s.sb("junk", [B, 2, N], BF16)
        tie = s.sb("tie", [B, 2, B], BF16)
        ranked = s.sem("ranked")
        sT = s.sb("sT", [NB, B])
        hid = s.sb("hid", [P, M1, T])
        hh, hl = s.sb("hh", [P, M1, T], F16), s.sb("hl", [P, M1, T], F16)
        wrep = s.sb("wrep", [P, KH, P])
        y = s.sb("y", [P, KH, NP])
        ob = s.sb("ob", [B, 8, D])
        ps = c.ps
        own, sc_done, sc_out, wc_done, sel_done, sT_out, sel_st, sel_in = (s.sem(n) for n in (
            "f_steps", "sc_done", "sc_out", "wc_done", "sel_done", "sT_out", "sel_stored", "sel_in"))
        rep, f1, g1, low, f2, y_out, fin = (s.sem(n) for n in ("wrep_ready", "f_fc1", "f_gelu", "gelu_low", "f_fc2", "y_out", "x_final"))
        turned, copied = s.sem("o_turned"), [s.sem(f"o_copied{k}") for k in range(2)]
        stored = [s.sem(f"o_stored{k}") for k in range(8)]
        at = lambda t: slice(t * T, (t + 1) * T)
        with nc.Block() as block:
            @block.tensor
            def _(pe):
                mm = nc.tensor.matmul
                pe.wait_ge(rep, 1)
                for t in range(NT):
                    if t >= 4:
                        pe.wait_ge(sc_out, t - 3)
                    product(nc, ps[t % 4][:, 0:T], [wrep[:, k, :] for k in range(KH)], [c.yn[:, k, at(t)] for k in range(KH)]).then_inc(sc_done, 1)
                pe.wait_ge(sc_out, NT)
                for j in range(NB):
                    ins = nc.tensor.transpose(ps[4][0:B, j:j + 1], wrow[0:1, B * j:B * (j + 1)], c.ident[0:1, 0:1])
                ins.then_inc(wc_done, 1)
                pe.wait_ge(own, 1)

                def up(t, m):
                    pe.wait_ge(g1, M1 * t + (m + 5 if m < 2 else m + 1))
                    product3(nc, ps[m % 6][:, 0:T], [(w.w1[0][:, k, m * P:(m + 1) * P], w.w1[1][:, k, m * P:(m + 1) * P]) for k in range(KH)],
                             [(c.yh[:, k, cols(t)], c.yl[:, k, cols(t)]) for k in range(KH)]).then_inc(f1, 1)

                def down(t, m, n):
                    if m == 0:
                        pe.wait_ge(y_out, KH * t + 1)
                    pe.wait_ge(low, n + 1)
                    for h in range(KH):
                        ins = product3(nc, ps[6 + h][:, 0:T], [(w.w2[0][:, m, half(h)], w.w2[1][:, m, half(h)])], [(hh[:, m, :], hl[:, m, :])],
                                       start=(m == 0), stop=(m == M1 - 1))
                    ins.then_inc(f2, 1)

                def selection():
                    pe.wait_ge(sel_done, 1)
                    pe.wait_ge(g1, M1 * (NT - 2) + 6)
                    nc.tensor.transpose(ps[5][0:NB, 0:B], rank[:, 0, :], c.ident[0:B, 0:B]).then_inc(wc_done, 1)
                    pe.wait_ge(sT_out, 1)

                def tile(t, first=False, select=False):
                    for m in range(M1):
                        if select and m == 5:
                            selection()
                        up(t, m)
                        if m >= 2 or not first:
                            down(t, (m - 2) % M1, M1 * t + m - 2)

                tile(0, first=True)
                with pe.Fori(1, NT - 2) as t:
                    tile(t)
                tile(NT - 2, select=True)
                tile(NT - 1)
                for m in range(M1 - 2, M1):
                    down(NT - 1, m, M1 * (NT - 1) + m)
                for j in range(NB):
                    pe.wait_ge(fin, min(NT, (B * (j + 1) - 1) // T + 1))
                    if j == 6:
                        pe.wait_ge(y_out, KH * NT + 1)
                    if j >= 8:
                        pe.wait_ge(copied[j % 2], (j - 8) // 2 + 1)
                    for h in range(KH):
                        ins = nc.tensor.transpose(ps[j % 8][0:B, half(h)], c.xT[:, h, B * j:B * (j + 1)], c.ident[:])
                    ins.then_inc(turned, 1)

            @block.gpsimd
            def _(pool):
                with pool.Fori(0, NT) as t:
                    for m in range(M1):
                        pool.wait_ge(g1, M1 * t + m + 7)
                        nc.gpsimd.tensor_tensor(hl[:, m, :], hid[:, m, :], hh[:, m, :], ALU.subtract).then_inc(low, 1)

            @block.scalar
            def _(act):
                act.sem_inc(g1, 6)

                def finish(t):
                    act.wait_ge(f2, M1 * t + 2 * M1)
                    for h in range(KH):
                        nc.scalar.activation(y[:, h, cols(t)], ps[6 + h][:, 0:T], ACT.Identity, bias=w.b2f[:, h:h + 1], scale=1.0 / WS).then_inc(y_out, 1)

                def tile(t, first=False):
                    for m in range(M1):
                        act.wait_ge(f1, M1 * t + m + 1)
                        act.wait_ge(f2, M1 * t + m + 1)
                        for out in (hh, hid):
                            ins = nc.scalar.activation(out[:, m, :], ps[m % 6][:, 0:T], ACT.Gelu_apprx_tanh, bias=w.b1f[:, m:m + 1], scale=1.0 / WS)
                        ins.then_inc(g1, 1)
                        if m == 1 and not first:
                            finish(t - 1)

                tile(0, first=True)
                with act.Fori(1, NT) as t:
                    tile(t)
                finish(NT - 1)
                for j in range(0, NB, 2):
                    act.wait_ge(turned, j + 1)
                    if j >= 8:
                        act.wait_ge(stored[j % 8], 16 * (j // 8))
                    nc.scalar.copy(ob[:, j % 8, :], ps[j % 8][0:B, 0:D]).then_inc(copied[0], 1)

            @block.sync
            def _(sp):
                sp.wait_ge(sT_out, 1)
                sp.dma_start(dram.sel.rearrange("(a p) -> a p", p=B), sT[:]).then_inc(sel_st, 16)
                sp.wait_ge(sel_st, 16)
                sp.dma_start(sel[:, 0:N], dram.sel.partition_broadcast(P)).then_inc(sel_in, 16)
                for j in range(NB):
                    sp.wait_ge(copied[j % 2], j // 2 + 1)
                    sp.dma_start(out[B * j:B * (j + 1), :], ob[:, j % 8, :]).then_inc(stored[j % 8], 16)
                for k in range(8):
                    sp.wait_ge(stored[k], 16 * len(range(k, NB, 8)))

            @block.vector
            def _(dve):
                v = nc.vector
                step = Steps(dve, own)
                dve.sem_inc(f2, M1)
                dve.sem_inc(y_out, 1)
                v.memset(sel[:, N:NP], 0.0)
                dve.wait_ge(w.loaded, w.total)
                v.tensor_copy(wrep[:], w.wr1[:].to_broadcast([P, KH, P])).then_inc(rep, 1)
                for t in range(NT):
                    dve.wait_ge(sc_done, t + 1)
                    v.tensor_scalar(wrow[:, at(t)], ps[t % 4][:, 0:T], w.br1[:, 0:1], None, ALU.add).then_inc(sc_out, 1)
                dve.wait_ge(wc_done, 1)
                step(v.tensor_copy(wc[:], ps[4][0:B, 0:NB]))
                dve.wait_ge(sc_out, NT)
                step(v.memset(rank[:], 0.0))
                for j in range(NB):
                    me = wc[:, j:j + 1]
                    lo = B * j
                    if j >= 2:
                        dve.wait_ge(ranked, j - 1)
                    if j:
                        v.tensor_scalar(junk[:, j % 2, 0:lo], wrow[0:B, 0:lo], me, None, ALU.is_ge, ALU.add, accum_out=rank[:, 0, j:j + 1])
                    v.scalar_tensor_tensor(tie[:, j % 2, :], wrow[0:B, lo:lo + B], me, c.tri[:], ALU.is_equal, ALU.mult, accum_out=rank[:, 1, j:j + 1])
                    v.tensor_scalar(junk[:, j % 2, lo:N], wrow[0:B, lo:N], me, None, ALU.is_gt, ALU.add, accum_out=rank[:, 2, j:j + 1]).then_inc(ranked, 1)
                dve.wait_ge(ranked, NB)
                step(v.tensor_tensor(rank[:, 0], rank[:, 0], rank[:, 1], ALU.add))
                step(v.tensor_tensor(rank[:, 0], rank[:, 0], rank[:, 2], ALU.add))
                v.tensor_scalar(rank[:, 0], rank[:, 0], float(TOPK), None, ALU.is_lt).then_inc(sel_done, 1)
                dve.wait_ge(wc_done, 2)
                v.tensor_copy(sT[:], ps[5][0:NB, 0:B]).then_inc(sT_out, 1)
                step(v.tensor_tensor(c.xT[:], c.xT[:], c.yn[:], ALU.add))
                dve.wait_ge(sel_in, 16)
                step(v.tensor_tensor(sel[:], sel[:], wrow[:], ALU.mult))
                for t in range(NT):
                    dve.wait_ge(y_out, KH * t + KH + 1)
                    step(v.tensor_tensor(y[:, :, at(t)], y[:, :, at(t)], sel[:, at(t)].unsqueeze(1).to_broadcast([P, KH, T]), ALU.mult))
                    v.tensor_tensor(c.xT[:, :, at(t)], c.xT[:, :, at(t)], y[:, :, at(t)], ALU.add).then_inc(fin, 1)
                for j in range(1, NB, 2):
                    dve.wait_ge(turned, j + 1)
                    if j >= 8:
                        dve.wait_ge(stored[j % 8], 16 * (j // 8))
                    v.tensor_copy(ob[:, j % 8, :], ps[j % 8][0:B, 0:D]).then_inc(copied[1], 1)


class Names:
    pass


def load_weights(nc, w, plan):
    with nc.Block() as block:
        @block.sync
        def _(sp):
            with nc.allow_non_contiguous_dma(reason="weights in blocks of 128 rows"):
                for dst, src, sem in plan:
                    sp.dma_start(dst, src).then_inc(sem, 16)
    w.total = 16 * sum(sem is w.loaded for _, _, sem in plan)


def rows128(a):
    return a.rearrange("(k p) m -> p k m", p=P)


def build(nc, i, out):
    dram = Names()
    internal = lambda name, shape, dt=F32: nc.dram_tensor(name, shape, dt, kind="Internal").ap()
    dram.adj = internal("adjacency", (N + 1, NP), F16)
    dram.adj_flat = dram.adj.rearrange("a (b o) -> (a b) o", o=1)
    dram.rows = internal("b_rows", (N, D))
    dram.runs = internal("run_max", (E, D))
    dram.keys = internal("edge_keys", (E,))
    dram.reset = internal("edge_resets", (E,), BF16)
    dram.rdeg = internal("degree_inverse", (NP,))
    dram.gate = internal("gate_rows", (NEXP, NP))
    dram.sel = internal("selected", (N,))
    with Scope(nc, "all") as s:
        c = Names()
        c.ps = [s.enter_context(nc.psum_tensor(f"bank{b}", [P, 512], F32)) for b in range(8)]
        c.spare = s.sb("spare", [P, WC], I32)
        c.spare_f = s.sb("spare_f", [P, WC])
        c.row = s.sb("row", [P, P])
        c.row_b = s.sb("row_b", [B, B], BF16)
        c.ident = s.sb("ident", [P, P])
        c.upto = s.sb("upto", [P, P])
        c.before = s.sb("before", [B, 2 * WE - B], F16)
        c.tri = s.sb("tri", [B, B], BF16)
        c.cnt = s.sb("cnt", [B, EC])
        c.cell_idx = s.sb("cell_idx", [B, EC], I32)
        c.cell_val = s.sb("cell_val", [B, EC], F16)
        c.added = s.sem("cells_added")
        c.ones = s.sb("ones", [P, P])
        c.mean_w = s.sb("mean_w", [P, P])
        c.eps5 = s.sb("eps5", [P, 1])
        c.eps3 = s.sb("eps3", [P, 1])
        c.src_idx = s.sb("src_idx", [B, EC], I32)
        c.key_c = s.sb("key_c", [B, EC])
        c.has = s.sb("has", [B, NB])
        c.lack = s.sb("lack", [B, NB])
        c.last_idx = s.sb("last_idx", [B, NB], I32)
        c.xT = s.sb("xT", [P, KH, NP])
        c.yn = s.sb("yn", [P, KH, NP])
        c.a = s.sb("a", [P, KH, NP])
        c.attT = s.sb("attT", [P, KH, P])
        constants(nc, c)

        with Scope(nc, "w0") as g:
            w = Names()
            w.loaded = g.sem("w0_loaded")
            w.theta, w.phi = g.sb("theta", [P, KH, D]), g.sb("phi", [P, KH, D])
            w.qkv, w.fc1, w.fc2 = g.sb("qkv", [P, KH, 3 * D]), g.sb("fc1", [P, KH, HID0]), g.sb("fc2", [P, HID0 // P, D])
            w.bqkv_row = g.sb("bqkv_row", [1, 3 * D])
            w.tb, w.pb, w.bq, w.ng, w.nb, w.b2 = (g.sb(n, [P, KH]) for n in ("tb", "pb", "bq", "ng", "nb", "b2"))
            w.b1 = g.sb("b1", [P, HID0 // P])
            loads = [
                (w.theta[:], rows128(i.theta)), (w.phi[:], rows128(i.phi)), (w.qkv[:], rows128(i.qkv)),
                (w.fc1[:], rows128(i.fc1)), (w.fc2[:], rows128(i.fc2)), (w.bqkv_row[:], i.bqkv_row),
                (w.tb[:], i.theta_b), (w.pb[:], i.phi_b), (w.bq[:], i.bqkv[:, 0:KH]), (w.ng[:], i.norm_g),
                (w.nb[:], i.norm_b), (w.b2[:], i.b_fc2), (w.b1[:], i.b_fc1)]
            w.total = 16 * len(loads)
            edges_and_nodes(nc, c, i.src, i.dst, i.x, dram, w, loads)
            edges_and_mix0(nc, c, dram, w)
        f16 = c.a[:].bitcast(F16)
        c.yh, c.yl = f16[:, :, 0:NP], f16[:, :, NP:2 * NP]
        with Scope(nc, "w1") as g:
            w = Names()
            w.loaded, mats = g.sem("w1_loaded"), [g.sem(f"expert{n}_loaded") for n in range(3)]
            w.Wr, w.br, w.bo = g.sb("Wr", [P, KH, NEXP]), g.sb("br", [NEXP, 1]), g.sb("bo", [NEXP, D])
            w.W1, w.W2, w.Wo = ([g.sb(n + p, [P, NEXP, KH, D], F16) for p in "hl"] for n in ("W1", "W2", "Wo"))
            w.bn = g.sb("bn", [P, 2, 5, KH, NEXP])
            w.scale, w.shift = g.sb("scale", [P, 2, KH, NEXP]), g.sb("shift", [P, 2, KH, NEXP])
            blocks = lambda a: a.rearrange("e (k p) m -> p e k m", p=P)
            each = range(NEXP)
            with Scope(nc, "staged") as st:
                f = [st.sb(f"float{n}", [P, NEXP, KH, D]) for n in range(2)]
                load_weights(nc, w, [
                    (w.Wr[:], rows128(i.Wr), w.loaded), (w.br[:], i.br, w.loaded), (w.bo[:], i.bo, w.loaded), (w.bn[:], i.bn, w.loaded),
                    *((f[n][:, e], blocks(a)[:, e], mats[n]) for n, a in enumerate((i.W1, i.W2)) for e in each)])
                pieces = lambda f, W, sem: [(f[:, e:e + 2], W[0][:, e:e + 2], W[1][:, e:e + 2], sem, 16 * NEXP) for e in range(0, NEXP, 2)]
                join_max(nc, c, dram, w, pieces(f[0], w.W1, mats[0]))
                norm(nc, c, 1, lambda pool: add_cells(nc, c, dram, pool, 4, 9), [(f[0][:, e], blocks(i.Wo)[:, e], mats[2]) for e in each])
                gate(nc, c, w, dram, pieces(f[1], w.W2, mats[1]) + pieces(f[0], w.Wo, mats[2]), lambda pool: add_cells(nc, c, dram, pool, 9, 14))
            made = g.sem("cells_made")
            experts(nc, c, w, dram, made, lambda pool: add_cells(nc, c, dram, pool, 14, 82, made))
        with Scope(nc, "w2") as g:
            w, H = Names(), HEADS1 * HD1
            w.loaded, mats = g.sem("w2_loaded"), g.sem("w3_loaded")
            w.gl, w.gr = ([g.sb(n + p, [P, 3, KH, D], F16) for p in "hl"] for n in ("gl", "gr"))
            w.rd = g.sb("rd", [P, NP])
            w.gb, w.wout = g.sb("gbias", [P, 3, KH]), g.sb("wout", [P, D])
            w.gpre, w.gout, w.bout = (g.sb(n, [P, KH]) for n in ("gpre", "gout", "bout"))
            w.mqkv = g.sb("mqkv", [P, KH, 3 * H])
            w.mk, w.mv = g.sb("mk", [P, MEM]), g.sb("mv", [P, MEM])
            qT, ctx = g.sb("qT", [P, NP]), g.sb("ctx", [P, P])
            with Scope(nc, "staged2") as st:
                f = [st.sb(n, [P, 3, KH, D]) for n in ("gl", "gr")]
                plan = [(w.mqkv[:], rows128(i.mqkv)), (w.wout[:], i.wout), (w.mk[:], i.mk), (w.mv[:], i.mv),
                        (w.gpre[:], i.gpre), (w.gout[:], i.gout), (w.bout[:], i.bout), (w.gb[:], i.gb),
                        (w.rd[:], dram.rdeg.partition_broadcast(P))]
                w.total = 16 * len(plan)
                norm(nc, c, 2, lambda pool: add_cells(nc, c, dram, pool, 82, 87), [
                    *((f[n][:, k], rows128(a[k]), mats) for n, a in enumerate((i.gl, i.gr)) for k in range(3)),
                    *((dst, src, w.loaded) for dst, src in plan)])
                split_weights(nc, "split2", [(f[n][:], W[0][:], W[1][:], mats, 16 * 6) for n, W in enumerate((w.gl, w.gr))])
            mix1(nc, c, w, qT, ctx, lambda pool: add_cells(nc, c, dram, pool, 87, NW))
            sage(nc, c, w, dram, 0, (qT, ctx))
            sage(nc, c, w, dram, 1)
            sage(nc, c, w, dram, 2)
        with Scope(nc, "w4") as g:
            w = Names()
            w.loaded, mats = g.sem("w4_loaded"), g.sem("w5_loaded")
            w.w1, w.w2 = [g.sb(f"w1{p}", [P, KH, HID1], F16) for p in "hl"], [g.sb(f"w2{p}", [P, HID1 // P, D], F16) for p in "hl"]
            w.b1f, w.b2f = g.sb("b1f", [P, HID1 // P]), g.sb("b2f", [P, KH])
            w.wr1, w.br1 = g.sb("wr1", [P, KH, 1]), g.sb("br1", [P, 1])
            with Scope(nc, "staged3") as st:
                f1, f2 = st.sb("w1", [P, KH, HID1]), st.sb("w2", [P, HID1 // P, D])
                plan = [(w.b1f[:], i.b1f), (w.b2f[:], i.b2f), (w.wr1[:], rows128(i.wr1)), (w.br1[:], i.br1.partition_broadcast(P))]
                w.total = 16 * len(plan)
                norm(nc, c, 3, None, [(f1[:], rows128(i.w1), mats), (f2[:], rows128(i.w2), mats), *((dst, src, w.loaded) for dst, src in plan)])
                split_weights(nc, "split3", [(f1[:], w.w1[0][:], w.w1[1][:], mats, 32), (f2[:], w.w2[0][:], w.w2[1][:], mats, 32)])
            ffn1(nc, c, w, dram, out)


def kernel(**a):
    import numpy as np
    import concourse.bacc as bacc
    from concourse.bass_utils import run_bass_kernel_spmd as run

    nc = bacc.Bacc("TRN2", target_bir_lowering=False, num_devices=1)
    col = lambda v: v.reshape(-1, P).T
    bn = lambda n: np.stack([a[f"L0_ffn_{k}{n}"].reshape(NEXP, KH, P).transpose(2, 1, 0) for k in ("b", "g", "be", "m", "v")], axis=1)
    laid = {
        "x": a["x"], "src": a["src"], "dst": a["dst"],
        "theta": a["L0_gnn_theta_w"].T, "phi": a["L0_gnn_phi_w"].T,
        "theta_b": col(a["L0_gnn_theta_b"]), "phi_b": col(a["L0_gnn_phi_b"]),
        "qkv": a["L0_mix_w_qkv"], "bqkv": col(a["L0_mix_b_qkv"]), "bqkv_row": a["L0_mix_b_qkv"][None],
        "norm_g": col(a["L0_mix_norm_g"]), "norm_b": col(a["L0_mix_norm_b"]),
        "fc1": a["L0_mix_w_fc1"], "b_fc1": col(a["L0_mix_b_fc1"]), "fc2": a["L0_mix_w_fc2"], "b_fc2": col(a["L0_mix_b_fc2"]),
        "Wr": a["L0_ffn_Wr"], "br": a["L0_ffn_br"][:, None], "bo": a["L0_ffn_bo"],
        "W1": a["L0_ffn_W1"], "W2": a["L0_ffn_W2"], "Wo": a["L0_ffn_Wo"], "bn": np.stack([bn(1), bn(2)], axis=1),
        "gl": np.stack([a[f"L1_gnn_W{n}l"].T for n in (1, 2, 3)]), "gr": np.stack([a[f"L1_gnn_W{n}r"].T for n in (1, 2, 3)]),
        "gb": np.stack([col(a[f"L1_gnn_b{n}l"]) for n in (1, 2, 3)], axis=1),
        "mqkv": a["L1_mix_w_qkv"], "wout": a["L1_mix_w_out"], "mk": a["L1_mix_mem_kv"][0].reshape(P, MEM),
        "mv": a["L1_mix_mem_kv"][1].reshape(P, MEM), "gpre": col(a["L1_mix_g_pre"]), "gout": col(a["L1_mix_g_out"]),
        "bout": col(a["L1_mix_b_out"]),
        "w1": a["L1_ffn_w1"], "b1f": col(a["L1_ffn_b1"]), "w2": a["L1_ffn_w2"], "b2f": col(a["L1_ffn_b2"]),
        "wr1": a["L1_ffn_wr"], "br1": a["L1_ffn_br"],
    }
    arrays = {f"in_{k}": np.ascontiguousarray(v) for k, v in laid.items()}
    i = Names()
    for k, v in arrays.items():
        i.__dict__[k[3:]] = nc.dram_tensor(k, v.shape, mybir.dt.from_np(v.dtype), kind="ExternalInput").ap()
    out = nc.dram_tensor("out_x", (N, D), F32, kind="ExternalOutput").ap()
    build(nc, i, out)
    r = run(nc, [arrays], core_ids=[0])
    return r.results[0]["out_x"]
```
